# Optimizing a Trainium2 kernel written in Bass

```python
import numpy as np
import jax
import jax.numpy as jnp

def _softmax(x, axis=-1):
    return jax.nn.softmax(x, axis=axis)

def _gelu(x):
    return jax.nn.gelu(x, approximate=True)

def _silu(x):
    return jax.nn.silu(x)

def _sigmoid(x):
    return jax.nn.sigmoid(x)

def _layernorm(x, axis=-1, eps=1e-05):
    m = jnp.mean(x, axis=axis, keepdims=True)
    v = jnp.var(x, axis=axis, keepdims=True)
    return (x - m) / jnp.sqrt(v + eps)

def _scatter_add(tgt, idx, src, axis=0):
    return tgt.at[idx].add(src)

def _segment_sum(src, seg, n):
    return jax.ops.segment_sum(src, seg, n)
kernel_name = 'mk_hybrid_d1_jaxref_r8_16f0fa'

def setup_inputs(seed: int=0):
    np.random.seed(seed)
    _w = jnp.asarray

    def _L0_attn_a_setup():
        import jax, jax.numpy as jnp
        import numpy as np
        EPS = 1e-06

        def rmsnorm(y, w):
            return y * jax.lax.rsqrt(jnp.mean(y * y, axis=-1, keepdims=True) + EPS) * w

        def apply_rope_cumangle(z, cum_angle):
            B, T, H, N = z.shape
            zp = z.reshape(B, T, H, N // 2, 2)
            cos = jnp.cos(cum_angle)[..., None]
            sin = jnp.sin(cum_angle)[..., None]
            z0, z1 = (zp[..., 0], zp[..., 1])
            out = jnp.stack([z0 * cos - z1 * sin, z0 * sin + z1 * cos], axis=-1)
            return out.reshape(B, T, H, N)
        key = jax.random.key(seed)
        ks = jax.random.split(key, 6)
        B, T, D = (2, 128, 128)
        H, P, N = (8, 64, 128)
        d_inner = H * P
        x = jax.random.normal(ks[0], (B, T, D), dtype=jnp.float32)
        in_proj_w = jax.random.normal(ks[1], (d_inner, D), dtype=jnp.float32) * (1.0 / np.sqrt(D))
        sel_proj_w = jax.random.normal(ks[2], (2 * H * N + 3 * H, D), dtype=jnp.float32) * (1.0 / np.sqrt(D))
        out_proj_w = jax.random.normal(ks[3], (D, d_inner), dtype=jnp.float32) * (1.0 / np.sqrt(d_inner))
        A_log = jnp.log(jnp.arange(1, H + 1, dtype=jnp.float32))
        dt_bias = jax.random.normal(ks[4], (H,), dtype=jnp.float32) * 0.5
        rms_weight = jnp.ones((d_inner,), dtype=jnp.float32)
        return {'x': x, 'in_proj_w': in_proj_w, 'sel_proj_w': sel_proj_w, 'out_proj_w': out_proj_w, 'A_log': A_log, 'dt_bias': dt_bias, 'rms_weight': rms_weight}
    _L0_attn_a_in = _L0_attn_a_setup()

    def _L0_attn_b_setup():
        import jax, jax.numpy as jnp
        import numpy as np
        NUM_HEADS = 16
        CHUNK_SIZE = 64
        NEG_INF = -1000000000.0

        def chunk_mask(seq_len, chunk_size):
            idx = jnp.arange(seq_len)
            cid = idx // chunk_size
            future = idx[None, :] > idx[:, None]
            diff_chunk = cid[None, :] != cid[:, None]
            return future & diff_chunk
        key = jax.random.key(seed)
        k1, k2, k3 = jax.random.split(key, 3)
        S, B, E = (256, 2, 128)
        x = jax.random.normal(k1, (S, B, E), dtype=jnp.float32)
        in_proj_w = jax.random.normal(k2, (3 * E, E), dtype=jnp.float32) * E ** (-0.5)
        in_proj_b = jnp.zeros((3 * E,), dtype=jnp.float32)
        out_proj_w = jax.random.normal(k3, (E, E), dtype=jnp.float32) * E ** (-0.5)
        out_proj_b = jnp.zeros((E,), dtype=jnp.float32)
        return {'x': x, 'in_proj_w': in_proj_w, 'in_proj_b': in_proj_b, 'out_proj_w': out_proj_w, 'out_proj_b': out_proj_b}
    _L0_attn_b_in = _L0_attn_b_setup()

    def _L0_ffn_setup():
        import jax, jax.numpy as jnp
        import numpy as np
        THRESH_FACTOR = 0.7

        def ternary_quantize(w):
            delta = THRESH_FACTOR * jnp.mean(jnp.abs(w))
            return jnp.where(w > delta, 1.0, jnp.where(w < -delta, -1.0, 0.0)).astype(w.dtype)
        key = jax.random.key(seed)
        k1, k2, k3 = jax.random.split(key, 3)
        B, S, D_IN, D_OUT = (8, 512, 128, 128)
        inp = {'input': jax.random.normal(k1, (B, S, D_IN), dtype=jnp.float32), 'weight': jax.random.normal(k2, (D_OUT, D_IN), dtype=jnp.float32) * (1.0 / np.sqrt(D_IN)), 'alpha': jnp.ones((1,), dtype=jnp.float32), 'bias': jax.random.normal(k3, (D_OUT,), dtype=jnp.float32) * (1.0 / np.sqrt(D_IN))}
        return inp
    _L0_ffn_in = _L0_ffn_setup()
    _d = {'L0_attn_a_x': _L0_attn_a_in['x'], 'L0_attn_a_in_proj_w': _L0_attn_a_in['in_proj_w'], 'L0_attn_a_sel_proj_w': _L0_attn_a_in['sel_proj_w'], 'L0_attn_a_out_proj_w': _L0_attn_a_in['out_proj_w'], 'L0_attn_a_A_log': _L0_attn_a_in['A_log'], 'L0_attn_a_dt_bias': _L0_attn_a_in['dt_bias'], 'L0_attn_a_rms_weight': _L0_attn_a_in['rms_weight'], 'L0_attn_b_in_proj_w': _L0_attn_b_in['in_proj_w'], 'L0_attn_b_in_proj_b': _L0_attn_b_in['in_proj_b'], 'L0_attn_b_out_proj_w': _L0_attn_b_in['out_proj_w'], 'L0_attn_b_out_proj_b': _L0_attn_b_in['out_proj_b'], 'L0_ffn_weight': _L0_ffn_in['weight'], 'L0_ffn_alpha': _L0_ffn_in['alpha'], 'L0_ffn_bias': _L0_ffn_in['bias']}
    _x0 = _d['L0_attn_a_x']
    _d['L0_attn_a_x'] = jax.random.normal(jax.random.fold_in(jax.random.key(seed), 1), (8, 512, 128), dtype=_x0.dtype)
    del _x0
    return _d

def reference(L0_attn_a_x, L0_attn_a_in_proj_w, L0_attn_a_sel_proj_w, L0_attn_a_out_proj_w, L0_attn_a_A_log, L0_attn_a_dt_bias, L0_attn_a_rms_weight, L0_attn_b_in_proj_w, L0_attn_b_in_proj_b, L0_attn_b_out_proj_w, L0_attn_b_out_proj_b, L0_ffn_weight, L0_ffn_alpha, L0_ffn_bias):

    def _L0_attn_a_ref(x, in_proj_w, sel_proj_w, out_proj_w, A_log, dt_bias, rms_weight):
        import jax, jax.numpy as jnp
        import numpy as np
        EPS = 1e-06

        def rmsnorm(y, w):
            return y * jax.lax.rsqrt(jnp.mean(y * y, axis=-1, keepdims=True) + EPS) * w

        def apply_rope_cumangle(z, cum_angle):
            B, T, H, N = z.shape
            zp = z.reshape(B, T, H, N // 2, 2)
            cos = jnp.cos(cum_angle)[..., None]
            sin = jnp.sin(cum_angle)[..., None]
            z0, z1 = (zp[..., 0], zp[..., 1])
            out = jnp.stack([z0 * cos - z1 * sin, z0 * sin + z1 * cos], axis=-1)
            return out.reshape(B, T, H, N)
        B, T, D = x.shape
        H = A_log.shape[0]
        d_inner = in_proj_w.shape[0]
        P = d_inner // H
        N = (sel_proj_w.shape[0] - 3 * H) // (2 * H)
        u = (x @ in_proj_w.T).reshape(B, T, H, P)
        sel = x @ sel_proj_w.T
        B_proj = sel[..., :H * N].reshape(B, T, H, N)
        C_proj = sel[..., H * N:2 * H * N].reshape(B, T, H, N)
        scal = sel[..., 2 * H * N:].reshape(B, T, 3, H)
        dt = jax.nn.softplus(scal[:, :, 0] + dt_bias)
        lam = jax.nn.sigmoid(scal[:, :, 1])
        theta = scal[:, :, 2]
        cum_angle = jnp.cumsum(dt * theta, axis=1)
        B_proj = apply_rope_cumangle(B_proj, cum_angle)
        C_proj = apply_rope_cumangle(C_proj, cum_angle)
        A_neg = -jnp.exp(A_log)

        def step(carry, inp):
            h, Bx_prev = carry
            u_t, dt_t, lam_t, Bp_t, Cp_t = inp
            alpha = jnp.exp(dt_t * A_neg)
            beta = (1.0 - lam_t) * dt_t * alpha
            gamma = lam_t * dt_t
            Bx_t = u_t[:, :, :, None] * Bp_t[:, :, None, :]
            h = alpha[:, :, None, None] * h + beta[:, :, None, None] * Bx_prev + gamma[:, :, None, None] * Bx_t
            y_t = jnp.einsum('bhpn,bhn->bhp', h, Cp_t)
            return ((h, Bx_t), y_t)
        h0 = jnp.zeros((B, H, P, N), x.dtype)
        xs = (jnp.moveaxis(u, 1, 0), jnp.moveaxis(dt, 1, 0), jnp.moveaxis(lam, 1, 0), jnp.moveaxis(B_proj, 1, 0), jnp.moveaxis(C_proj, 1, 0))
        _, ys = jax.lax.scan(step, (h0, jnp.zeros_like(h0)), xs)
        y = jnp.moveaxis(ys, 0, 1).reshape(B, T, H * P)
        y = rmsnorm(y, rms_weight)
        return y @ out_proj_w.T

    def _L0_attn_b_ref(x, in_proj_w, in_proj_b, out_proj_w, out_proj_b):
        import jax, jax.numpy as jnp
        import numpy as np
        NUM_HEADS = 16
        CHUNK_SIZE = 64
        NEG_INF = -1000000000.0

        def chunk_mask(seq_len, chunk_size):
            idx = jnp.arange(seq_len)
            cid = idx // chunk_size
            future = idx[None, :] > idx[:, None]
            diff_chunk = cid[None, :] != cid[:, None]
            return future & diff_chunk
        S, B, E = x.shape
        H = NUM_HEADS
        D = E // H
        qkv = x @ in_proj_w.T + in_proj_b
        q, k, v = jnp.split(qkv, 3, axis=-1)
        q = q.reshape(S, B, H, D)
        k = k.reshape(S, B, H, D)
        v = v.reshape(S, B, H, D)
        scale = 1.0 / jnp.sqrt(jnp.asarray(D, dtype=x.dtype))
        scores = jnp.einsum('sbhd,tbhd->bhst', q * scale, k)
        mask = chunk_mask(S, CHUNK_SIZE)
        scores = jnp.where(mask[None, None, :, :], NEG_INF, scores)
        attn = jax.nn.softmax(scores, axis=-1)
        out = jnp.einsum('bhst,tbhd->sbhd', attn, v).reshape(S, B, E)
        return out @ out_proj_w.T + out_proj_b

    def _L0_ffn_ref(input, weight, alpha, bias):
        import jax, jax.numpy as jnp
        import numpy as np
        THRESH_FACTOR = 0.7

        def ternary_quantize(w):
            delta = THRESH_FACTOR * jnp.mean(jnp.abs(w))
            return jnp.where(w > delta, 1.0, jnp.where(w < -delta, -1.0, 0.0)).astype(w.dtype)
        w_ternary = ternary_quantize(weight)
        w_eff = w_ternary * alpha
        out = jnp.einsum('bsd,od->bso', input, w_eff) + bias
        return out
    x = L0_attn_a_x
    x = x + _L0_attn_a_ref(_layernorm(x, axis=-1), L0_attn_a_in_proj_w, L0_attn_a_sel_proj_w, L0_attn_a_out_proj_w, L0_attn_a_A_log, L0_attn_a_dt_bias, L0_attn_a_rms_weight)
    x = x + _L0_ffn_ref(_layernorm(x, axis=-1), L0_ffn_weight, L0_ffn_alpha, L0_ffn_bias)
    x = x + _L0_attn_b_ref(_layernorm(x, axis=-1), L0_attn_b_in_proj_w, L0_attn_b_in_proj_b, L0_attn_b_out_proj_w, L0_attn_b_out_proj_b)
    x = x + _L0_ffn_ref(_layernorm(x, axis=-1), L0_ffn_weight, L0_ffn_alpha, L0_ffn_bias)
    return x

_drawn_inputs = setup_inputs


def setup_inputs(seed=0):
    import zlib

    import numpy as np

    out = dict(_drawn_inputs(seed))
    spreads = {'L0_attn_a_rms_weight': (1.0, 0.2),
     'L0_attn_b_in_proj_b': (0.0, 0.615),
     'L0_attn_b_out_proj_b': (0.0, 0.8)}
    factors = {'L0_ffn_bias': 3.977}
    for name, (base, spread) in spreads.items():
        noise = np.random.default_rng([zlib.crc32(name.encode()), seed]).standard_normal(out[name].shape)
        drawn = base * np.exp(spread * noise) if base else spread * noise
        out[name] = jnp.asarray(drawn.astype(out[name].dtype))
    for name, factor in factors.items():
        out[name] = (out[name] * factor).astype(out[name].dtype)
    return out
```

```python
from contextlib import ExitStack

import numpy as np

import concourse.bass as bass
from concourse import mybir

F32 = mybir.dt.float32
ALU = mybir.AluOpType
ACT = mybir.ActivationFunctionType
AX = mybir.AxisListType
BF16 = mybir.dt.bfloat16

P = 128
NB = 8
NC = 4
NT = NB * NC
H = 8
HH = 4
N = 128
PD = 64
D = 128
UNITS = 2 * NB
AH = 16
AD = D // AH
BIAS_F, BIAS_O = 3 * D, 7 * D
BIAS = 11 * D
BIAS_IN = 5 * D
SC = 48
COS, SIN, BAND, SW, CD = 0, 8, 16, 32, 40
EPS_LN, EPS_RMS = 1e-5, 1e-6
TERNARY = 0.7
TWO_PI = 2.0 * np.pi
ROUND = 1.5 * 2.0 ** 23
POS = 3

USES = [("T", 0), ("T", 1), ("F", 0), ("F", 1), ("T", 2), ("T", 3)] + [("Q", s) for s in range(NB)] + \
       [("T", 4), ("T", 5), ("O", 0), ("O", 1), ("T", 6), ("T", 7), ("F", 2), ("F", 3)]
NUSE = len(USES)
VSTEPS = ["scaled", "mean0", "xc0", "var0", "xn0", "mean1", "xc1", "var1", "xn1", "max", "sub", "sum", "rec", "onorm",
          "mean2", "xc2", "var2", "xn2"]
GSTEPS = ["ms", "rr", "ve0", "rs0", "ve1", "rs1", "ve2", "rs2"]
XSTEPS = ["x1", ("F", 0), ("F", 1), ("O", 0), ("O", 1), ("F", 2), ("F", 3)]
POOL_PRODUCTS = (1, 4, 7, 10, 13)


PLACE = {"load": 2, "rr": 5, "x1": 6, "mean0": 6.5, "sq0": 7, "var0": 7.5, "rs0": 8, "xn0": 9, "T0": 10, "T1": 11, "xb0": 10, "F0": 11.5, "F1": 12.5,
         "addF0": 12, "addF1": 13, "mean1": 13.5, "sq1": 14, "var1": 14.5, "rs1": 15, "xn1": 16, "T2": 17, "T3": 18, "xb1": 17,
         "softmax": 31, "exp": 31.5, "norms": 32, "onorm": 40, "T4": 41, "T5": 41.5, "O0": 42, "O1": 42.5,
         "addO0": 42.5, "addO1": 43, "mean2": 43.3, "sq2": 43.5, "var2": 43.8, "rs2": 44, "xn2": 44.5, "T6": 45, "T7": 45.5, "xb2": 45,
         "F2": 46, "F3": 46.5, "addF2": 46.5, "addF3": 47, "store": 47.9}
PLACE.update({f"qkv{s}": 18.5 + s / 2 for s in range(NB)})
PLACE.update({f"qadd{s}": 19 + s / 2 for s in range(NB)})
PLACE.update({f"prod{m}": 23 + 0.9 * m + (2.3 if m >= NB else 0) for m in range(2 * NB)})
PLACE.update({f"red{m}": 23.45 + 0.9 * m + (2.3 if m >= NB else 0) for m in range(2 * NB)})


def place(pieces, name, emit):
    pieces.append((PLACE[name], emit))
    pieces.sort(key=lambda piece: piece[0])


def at_pos(pieces, pos, c):
    if c is not None:
        for at, emit in pieces:
            if int(at) == pos:
                emit(c)


def run_chunks(eng, step, pieces, finish=None):
    for k in range(UNITS):
        step(0, k, None, first=True)
    with eng.Fori(1, NC - 1) as c:
        for k in range(UNITS):
            step(c, k, c - 1)
    for k in range(UNITS):
        step(NC - 1, k, NC - 2, last=True)
    if finish:
        finish(NC - 1)
    for pos in range(POS * UNITS):
        at_pos(pieces, pos, NC - 1)


def v_step(name, c):
    return len(VSTEPS) * c + VSTEPS.index(name) + 1


def g_step(name, c):
    return len(GSTEPS) * c + GSTEPS.index(name) + 1


def x_step(name, c):
    return len(XSTEPS) * c + XSTEPS.index(name) + 1


def use_done(use, c):
    return NUSE * c + USES.index(use) + 1


def has_state(c, k):
    return not (isinstance(c, int) and c == NC - 1 and k >= 0)


def numbered(steps):
    return {name: at + 1 for at, name in enumerate(steps) if name is not None}


PA = numbered(["scal_w"] + [("T", c, g) for c in range(NC) for g in range(2)] +
              ["abs", "a", "ez", "es", "lz", "alpha", "dec", "suf", "cd", "rows_a", "rows"] +
              [("W", g) for g in (0, 1, 2, 3, 4, 6, 7)] + ["sin", "packed"])
PA["xnT"] = PA["T", NC - 1, 1]
PV = numbered(["even"] + [n for c in range(NC + 1) for n in
                          ([("bn", c), ("aggr", c)] if c < NC else []) + ([("xn", c - 1)] if c else [])] +
              [("scal", c, g) for c in range(NC) for g in range(2)] +
              [None, "az", None, "dt", "nla", "v", None, None, None, "vp", None, None, None, None, None, "beta"] +
              [None] * 7 + ["red", None, None, None, None, None, "packed", None, None, None, None, "tern", "w_out"])
PV["scal"] = PV["scal", NC - 1, 1]
PP = numbered(["scal_w"] + [n for c in range(NC + 1) for n in
                            ([("T", c, 0), ("T", c, 1)] if c < NC else []) +
                            ([("scal", c - 1, 0), ("scal", c - 1, 1)] if c else [])] +
              ["phi", "cums", "rows", "shifts"] + [("W", g) for g in range(8)])


def pi_parts():
    c1 = 6.28125
    c2 = float(np.float32(np.round((TWO_PI - c1) * 2.0 ** 21) / 2.0 ** 21))
    return c1, c2, float(np.float32(TWO_PI - c1 - c2))


def hybrid_block(nc, x, in_w, sel_w, out_w, a_log, dt_bias, rms_w, qkv_w, qkv_b, ob_w, ob_b, f_w, f_alpha, f_b, out):
    ctx = ExitStack()
    with ctx:
        def sb(name, shape):
            return ctx.enter_context(nc.sbuf_tensor(name, shape, F32))

        def sem(name):
            return ctx.enter_context(nc.semaphore(name))

        def after(eng, s, count):
            if not isinstance(count, int) or count > 0:
                eng.wait_ge(s, count)

        x_rows = x.rearrange("b (c t) d -> c t b d", c=NC)
        out_rows = out.rearrange("b (c t) d -> c t b d", c=NC)
        alpha_rows = nc.dram_tensor("alpha_rows", [NT * H, P], F32, kind="Internal").ap()
        decay_rows = nc.dram_tensor("decay_rows", [NT * H, P], F32, kind="Internal").ap()

        alpha_of_tile = alpha_rows.rearrange("(j h) t -> j (h t)", h=H)
        decay_of_tile = decay_rows.rearrange("(j r k) t -> j k r t", k=2, r=4)

        ident = sb("ident", [P, P])
        ones = sb("ones", [P, P])
        upto = sb("upto", [P, P])
        later = sb("later", [P, P])
        shift = sb("shift", [P, P])
        carry = sb("carry", [P, P])
        bandm = sb("bandm", [P, P])
        even = sb("even", [P, 2])
        mhalf = sb("mhalf", [P, NB])
        zeros = sb("zeros", [P, P])
        w_sel = sb("w_sel", [P, 2 * H * N])
        w_scal = sb("w_scal", [P, P])
        w_in = sb("w_in", [P, H * PD])
        w_out = sb("w_out", [P, 4, D])
        w_qkv = sb("w_qkv", [P, 3 * D])
        w_of = sb("w_of", [P, 2, D])
        bias3 = ctx.enter_context(nc.sbuf_tensor("bias3", [3, BIAS], BF16))
        ones3 = ctx.enter_context(nc.sbuf_tensor("ones3", [3, P], BF16))
        rms_c = sb("rms_c", [P, 4])
        dtb = sb("dtb", [P, H])
        alog = sb("alog", [P, H])
        a_pos = sb("a_pos", [P, H])
        alpha_c = sb("alpha_c", [P, 1])
        xnT = sb("xnT", [P, NT, P])
        scal = sb("scal", [P, NT, 24])
        packed = sb("packed", [P, NT, SC])
        small = sb("small", [P, 24, NT * H])
        stats4 = sb("stats4", [P, NC, NB, 6])
        mv4 = sb("mv4", [P, NC, NB, 2])
        rstd4 = sb("rstd4", [P, NC, NB])
        rows_sb = sb("rows_sb", [P, 2, 2, P])
        fsm = sb("fsm", [P, 4])

        area = sb("area", [P, 9216])
        x_all = area[:, 0:4096].rearrange("p (j d) -> p j d", d=D)
        sel_raw = area[:, 4096:6144].rearrange("p (r d) -> p r d", d=D)
        scal_raw = area[:, 6144:6272]
        in_raw = area[:, 6272:6784].rearrange("p (r d) -> p r d", d=D)
        out_raw = area[:, 6784:7296]
        qkv_raw = area[:, 7296:7680].rearrange("p (r d) -> p r d", d=D)
        ob_raw = area[:, 7680:7808]
        f_raw = area[:, 7808:7936]
        f_abs = area[:, 7936:8064]
        f_lo = area[:, 8064:8192]
        f_tern = area[:, 8192:8320]
        qkv = area[:, 0:3072].rearrange("p (s e) -> p s e", s=NB)
        xres = area[:, 3072:4096].rearrange("p (s d) -> p s d", s=NB)
        xn = area[:, 4096:5120].rearrange("p (s d) -> p s d", s=NB)
        xnT_f = area[:, 5120:6144].rearrange("p (s d) -> p s d", s=NB)
        prod = area[:, 6144:8192].rearrange("p (k e) -> p k e", k=2)
        att = area[:, 8192:9216]
        att_s = att.rearrange("p (s r h) -> p s r h", s=NB, r=NB)
        amax = sb("amax", [P, NB, AH])
        asum = sb("asum", [P, NB, AH])
        rr_f = sb("rr_f", [P, NB])
        mean_f = sb("mean_f", [P, NB])
        var_f = sb("var_f", [P, NB])
        eps_ln = sb("eps_ln", [P, NB])
        eps_rms = sb("eps_rms", [P, NB])
        rs_f = sb("rs_f", [P, NB])

        def two(name, cols):
            t = sb(name, [P, 2, cols])
            return [t[:, 0], t[:, 1]]

        xt = two("xt", P)
        sct = two("sct", SC)
        arow = two("arow", H * P)
        drow = two("drow", 4 * P)
        bc, bs, cc_, cs = two("bc", HH * N), two("bs", HH * N), two("cc", HH * N), two("cs", HH * N)
        bn, cn = two("bn", HH * N), two("cn", HH * N)
        bT, cT = two("bT", HH * P), two("cT", HH * P)
        band, lmat, mmat = two("band", HH * P), two("lmat", HH * P), two("mmat", HH * P)
        u_nat = two("u_nat", H * PD)
        wu = two("wu", HH * PD)
        yinter = sb("yinter", [P, 2 * P])
        sdec = sb("sdec", [P, HH * PD])
        yT_both = sb("yT", [P, 8 * P])
        yT = [yT_both[:, 0:4 * P], yT_both[:, 4 * P:8 * P]]
        ysq = sb("ysq", [P, 4 * P])
        ysum = two("ysum", P)
        state = sb("state", [P, NB, H * PD])
        xn_pro = [state[:, 2 * k:2 * k + 2].rearrange("p a (b d) -> p (a b) d", d=D) for k in range(2)]
        bias_row, bias_mid = state[0:1, 4:6].rearrange("o a b -> o (a b)")[:, 0:BIAS_IN], state[0:1, 6:8].rearrange("o a b -> o (a b)")[:, 0:BIAS_IN]
        bias_parts = [yT_both[0:1, 320 * k:320 * k + BIAS_IN // 2].bitcast(BF16) for k in range(3)]
        oraw = sb("oraw", [P, NB, 132])

        ps = ctx.enter_context(nc.psum_tensor("ps", [P, 8, 512], F32))
        BK_B, BK_C, BK_T, BK_G, BK_Y, BK_F0, BK_M, BK_F1 = range(8)
        BK_F = (BK_F0, BK_F1)

        ld_x = [sem(f"ld_x{c}") for c in range(NC)]
        ld_scal, ld_sel, ld_w, ld_small = sem("ld_scal"), sem("ld_sel"), sem("ld_w"), sem("ld_small")
        ld_bias, bias_in, bias_split = sem("ld_bias"), sem("bias_in"), sem("bias_split")
        consts = sem("consts")
        pv, pg, pa, pp = sem("pro_vector"), sem("pro_gpsimd"), sem("pro_scalar"), sem("pro_tensor")
        rows_stored = sem("rows_stored")
        packed_done = sem("packed_done")
        xt_in, sct_in = [sem("xt_in0"), sem("xt_in1")], [sem("sct_in0"), sem("sct_in1")]
        arow_in, drow_in = [sem("arow_in0"), sem("arow_in1")], [sem("drow_in0"), sem("drow_in1")]
        b_pe, c_pe, u_pe, tb_pe, tc_pe, g_pe = (sem(n) for n in ("b_pe", "c_pe", "u_pe", "tb_pe", "tc_pe", "g_pe"))
        y_pe, s_pe, o_pe = sem("y_pe"), sem("s_pe"), sem("o_pe")
        bc_dve, l_dve, m_dve, yi_dve, y_dve = (sem(n) for n in ("bc_dve", "l_dve", "m_dve", "yi_dve", "y_dve"))
        sd_dve, s_dve, ys_dve, o_dve = (sem(n) for n in ("sd_dve", "s_dve", "ys_dve", "o_dve"))
        bs_act, c_act, bT_act, cT_act, u_act, ysq_act = (sem(n) for n in ("bs_act", "c_act", "bT_act", "cT_act", "u_act", "ysq_act"))
        band_pool, bn_pool, cn_pool, wu_pool = sem("band_pool"), sem("bn_pool"), sem("cn_pool"), sem("wu_pool")
        fx_in, rows_free = sem("fx_in"), sem("rows_free")
        f_sq = sem("f_sq")
        f_pe, f_T, f_x, f_q, f_red, f_prod_v, f_prod_g, f_exp, f_v, f_g = (sem(n) for n in (
            "f_pe", "f_T", "f_x", "f_q", "f_red", "f_prod_v", "f_prod_g", "f_exp", "f_v", "f_g"))

        block = ctx.enter_context(nc.Block())

        def attention_product(eng, c, m, signal):
            eng.wait_ge(f_q, NB * c + NB)
            if m >= 2:
                eng.wait_ge(f_red, 2 * NB * c + m - 1)
            if m < NB:
                eng.tensor_tensor(prod[:, m % 2].rearrange("p (r e) -> p r e", r=NB),
                                  qkv[:, m, 0:D].unsqueeze(1).broadcast_to([P, NB, D]), qkv[:, :, D:2 * D],
                                  ALU.mult).then_inc(signal, 1)
            else:
                eng.wait_ge(f_exp, c + 1)
                eng.tensor_tensor(prod[:, m % 2].rearrange("p (r h d) -> p r h d", r=NB, d=AD),
                                  att_s[:, m - NB].unsqueeze(3).broadcast_to([P, NB, AH, AD]),
                                  qkv[:, :, 2 * D:3 * D].rearrange("p r (h d) -> p r h d", d=AD),
                                  ALU.mult).then_inc(signal, 1)

        def bank(k):
            return ps[:, k, :]

        (Z, AZ, EZ, LZ, RZ, DT, ES, LAM, OM, GAM, DEL, V, NLA, ALPHA, BETA, VP, PHI, R1, R2, DEC, SUF, G1, DIF, TMP) = (
            small[:, k, :] for k in range(24))

        def tiles(a):
            return a.rearrange("p (j h) -> p j h", h=H)

        @block.sync
        def _(sp):
            sp.dma_start(scal_raw, sel_w[2 * H * N + 3 * H - P:2 * H * N + 3 * H, :]).then_inc(ld_scal, 16)
            for c in range(NC):
                sp.dma_start(x_all[:, NB * c:NB * (c + 1), :], x_rows[c]).then_inc(ld_x[c], 16)
            def spread(v, n):
                return v.unsqueeze(0).broadcast_to([P, n])
            smalls = [(dtb[:], spread(dt_bias, H)), (alog[:], spread(a_log, H)),
                      (alpha_c[:], spread(f_alpha, 1))]
            for dst, src in smalls:
                sp.dma_start(dst, src).then_inc(ld_small, 16)
            with nc.allow_non_contiguous_dma("four columns of weights"):
                sp.dma_start(rms_c[:], rms_w.rearrange("(j p) -> p j", p=P)).then_inc(ld_small, 16)
            sp.dma_start(bias_row[:, 0:3 * D], qkv_b.unsqueeze(0)).then_inc(ld_bias, 16)
            sp.dma_start(bias_row[:, 3 * D:4 * D], f_b.unsqueeze(0)).then_inc(ld_bias, 16)
            sp.dma_start(bias_row[:, 4 * D:5 * D], ob_b.unsqueeze(0)).then_inc(ld_bias, 16)
            sp.dma_start(sel_raw, sel_w[0:2 * H * N, :].rearrange("(r p) d -> p r d", p=P)).then_inc(ld_sel, 16)
            for dst, src in [(in_raw, in_w.rearrange("(r p) d -> p r d", p=P)), (out_raw, out_w),
                             (qkv_raw, qkv_w.rearrange("(r p) d -> p r d", p=P)), (ob_raw, ob_w), (f_raw, f_w)]:
                sp.dma_start(dst, src).then_inc(ld_w, 16)

            sp.wait_ge(bias_split, 5)
            for k, part in enumerate(bias_parts):
                sp.dma_start(bias3[k:k + 1, 0:3 * D], part[:, 0:3 * D]).then_inc(bias_in, 16)
                for at, src in ((BIAS_F, 3 * D), (BIAS_O, 4 * D)):
                    sp.dma_start(bias3[k:k + 1, at:at + 4 * D].rearrange("o (r d) -> o r d", d=D),
                                 part[:, src:src + D].unsqueeze(1).broadcast_to([1, 4, D])).then_inc(bias_in, 16)

            sp.wait_ge(pa, PA["rows"])
            for k in range(2):
                sp.dma_start(alpha_rows[P * k:P * (k + 1), :], rows_sb[:, 0, k, :]).then_inc(rows_stored, 16)
                sp.dma_start(decay_rows[P * k:P * (k + 1), :], rows_sb[:, 1, k, :]).then_inc(rows_stored, 16)

            def tile_loads(c, b):
                i2 = b % 2
                tile = NB * c + b
                after(sp, c_pe, 2 * (tile - 2) + 2)
                sp.dma_start(xt[i2], xnT[:, tile, :]).then_inc(xt_in[i2], 16)
                after(sp, l_dve, 2 * (tile - 2) + 2)
                sp.dma_start(arow[i2], alpha_of_tile[tile].unsqueeze(0)
                             .broadcast_to([P, H * P])).then_inc(arow_in[i2], 16)
                after(sp, y_dve, 2 * (tile - 2) + 2)
                if not (isinstance(c, int) and c == NC - 1 and b >= 2):
                    after(sp, s_dve, 2 * (tile - 2) + 2)
                sp.dma_start(sct[i2], packed[:, tile, :]).then_inc(sct_in[i2], 16)
                rows = decay_of_tile[tile]
                for k in range(2):
                    sp.dma_start(drow[i2][64 * k:64 * k + 64].rearrange("p (r t) -> p r t", t=P),
                                 rows[k].unsqueeze(0).broadcast_to([64, 4, P])).then_inc(drow_in[i2], 16)

            sp.wait_ge(pv, PV["packed"])
            sp.wait_ge(pa, PA["packed"])
            sp.wait_ge(pa, PA["xnT"])
            sp.wait_ge(rows_stored, 64)
            for b in range(NB):
                tile_loads(0, b)
            with sp.Fori(1, NC - 1) as c:
                for b in range(NB):
                    tile_loads(c, b)
            for b in range(NB):
                tile_loads(NC - 1, b)

        @block.gpsimd
        def _(pool):
            def select(t, src, base, mult, step, op, fill):
                return pool.affine_select(out=t, in_=src, compare_op=op, fill=fill, base=base,
                                          pattern=[[step, P]], channel_multiplier=mult)
            pool.memset(zeros[:], 0.0)
            pool.memset(ones[:], 1.0)
            pool.memset(eps_ln[:], D * EPS_LN)
            pool.memset(eps_rms[:], H * PD * EPS_RMS)
            pool.memset(mhalf[:], -0.5).then_inc(consts, 1)
            pool.wait_ge(consts, 1)
            select(ident[:], zeros[:], 0, 1, -1, ALU.not_equal, 1.0).then_inc(consts, 1)
            select(upto[:], ones[:], 0, -1, 1, ALU.is_ge, 0.0)
            select(later[:], ones[:], 0, 1, -1, ALU.is_gt, 0.0)
            select(shift[:], zeros[:], -1, 1, -1, ALU.not_equal, 1.0)
            select(carry[:], zeros[:], P - 1, P, -1, ALU.not_equal, 1.0)
            pool.wait_ge(consts, 2)
            select(bandm[:], ident[:], 1, 1, -1, ALU.not_equal, 1.0).then_inc(consts, 1)
            for c in range(NC):
                pool.wait_ge(pv, PV["aggr", c])
                pool.tensor_scalar(rstd4[:, c], mv4[:, c, :, 1], 1.0, EPS_LN, ALU.mult, ALU.add).then_inc(pg, 1)
                pool.wait_ge(pg, 2 * c + 1)
                pool.tensor_tensor(rstd4[:, c], rstd4[:, c], mhalf[:], ALU.pow).then_inc(pg, 1)

            pool.memset(ones3[:], 1.0)
            pool.wait_ge(ld_bias, 48)
            pool.tensor_copy(bias_parts[0], bias_row).then_inc(bias_split, 1)
            pool.wait_ge(bias_split, 1)
            pool.tensor_tensor(bias_mid, bias_row, bias_parts[0], ALU.subtract).then_inc(bias_split, 1)
            pool.wait_ge(bias_split, 2)
            pool.tensor_copy(bias_parts[1], bias_mid).then_inc(bias_split, 1)
            pool.wait_ge(bias_split, 3)
            pool.tensor_tensor(bias_row, bias_mid, bias_parts[1], ALU.subtract).then_inc(bias_split, 1)
            pool.wait_ge(bias_split, 4)
            pool.tensor_copy(bias_parts[2], bias_row).then_inc(bias_split, 1)

            def add_b(c, k):
                h, n = k % 2, UNITS * c + k
                pool.wait_ge(bs_act, n + 1)
                after(pool, tb_pe, n - 1)
                if has_state(c, k - 2):
                    after(pool, s_pe, n - 1)
                pool.tensor_tensor(bn[h][:, 0::2], bc[h][:, 0::2], bs[h][:, 1::2], ALU.subtract)
                pool.tensor_tensor(bn[h][:, 1::2], bc[h][:, 1::2], bs[h][:, 0::2], ALU.add).then_inc(bn_pool, 1)

            def band_of(c, k):
                h, i2, n = k % 2, (k // 2) % 2, UNITS * c + k
                pool.wait_ge(sct_in[i2], 16 * (NB // 2 * c + k // 4 + 1))
                after(pool, l_dve, n - 1)
                mask = bandm[:].rearrange("p (a k) -> p a k", k=2).unsqueeze(1).broadcast_to([P, HH, P // 2, 2])
                vals = sct[i2][:, BAND + 2 * HH * h:BAND + 2 * HH * (h + 1)].rearrange("p (h k) -> p h k", k=2)
                pool.tensor_tensor(band[h].rearrange("p (h a k) -> p h a k", h=HH, k=2), mask,
                                  vals.unsqueeze(2).broadcast_to([P, HH, P // 2, 2]), ALU.mult).then_inc(band_pool, 1)

            def add_c(c, k):
                h, n = k % 2, UNITS * c + k
                pool.wait_ge(c_act, n + 1)
                after(pool, tc_pe, n - 1)
                pool.tensor_tensor(cn[h][:, 0::2], cc_[h][:, 0::2], cs[h][:, 1::2], ALU.subtract)
                pool.tensor_tensor(cn[h][:, 1::2], cc_[h][:, 1::2], cs[h][:, 0::2], ALU.add).then_inc(cn_pool, 1)

            def weigh_u(c, k):
                h, i2, n = k % 2, (k // 2) % 2, UNITS * c + k
                pool.wait_ge(u_act, NB * c + k // 2 + 1)
                after(pool, s_pe, n - 1)
                w = sct[i2][:, SW + HH * h:SW + HH * h + HH].unsqueeze(2).broadcast_to([P, HH, PD])
                pool.tensor_tensor(wu[h].rearrange("p (h q) -> p h q", q=PD),
                                   u_nat[i2][:, HH * PD * h:HH * PD * (h + 1)].rearrange("p (h q) -> p h q", q=PD),
                                   w, ALU.mult).then_inc(wu_pool, 1)

            def rms_root(c):
                pool.wait_ge(o_dve, NB * c + NB)
                pool.tensor_tensor(rr_f[:], oraw[:, :, D], eps_rms[:], ALU.add).then_inc(f_g, 1)
                pool.wait_ge(f_g, g_step("ms", c))
                pool.tensor_tensor(rr_f[:], rr_f[:], mhalf[:], ALU.pow).then_inc(f_g, 1)

            def ln_root(c, k):
                pool.wait_ge(f_v, v_step(f"var{k}", c))
                pool.tensor_tensor(rs_f[:], var_f[:], eps_ln[:], ALU.add).then_inc(f_g, 1)
                pool.wait_ge(f_g, g_step(f"ve{k}", c))
                pool.tensor_tensor(rs_f[:], rs_f[:], mhalf[:], ALU.pow).then_inc(f_g, 1)

            def product(c, m):
                attention_product(pool, c, m, f_prod_g)

            pieces = []
            place(pieces, "rr", lambda c: rms_root(c))
            for k in range(3):
                place(pieces, f"rs{k}", lambda c, k=k: ln_root(c, k))
            for m in POOL_PRODUCTS:
                place(pieces, f"prod{m}", lambda c, m=m: product(c, m))

            def step(c, k, follow, first=False, last=False):
                nxt = not (last and k == UNITS - 1)
                if nxt:
                    band_of(c, k + 1)
                at_pos(pieces, POS * k, follow)
                if nxt:
                    add_b(c, k + 1)
                at_pos(pieces, POS * k + 1, follow)
                if nxt:
                    add_c(c, k + 1)
                if not last:
                    weigh_u(c, k)
                at_pos(pieces, POS * k + 2, follow)

            band_of(0, 0)
            add_b(0, 0)
            add_c(0, 0)
            run_chunks(pool, step, pieces)

        @block.scalar
        def _(act):
            def evac(dst, src):
                return act.activation(dst, src, ACT.Copy)

            count = 0

            def tick(ins, name=None):
                nonlocal count
                count += 1
                ins.then_inc(pa, 1)
                if name is not None:
                    assert PA[name] == count, (name, count)

            act.wait_ge(pp, PP["scal_w"])
            tick(evac(w_scal[:], bank(0)[:, 0:P]), "scal_w")
            for c in range(NC):
                for g in range(2):
                    act.wait_ge(pp, PP["T", c, g])
                    tick(evac(xnT[:, NB * c + 4 * g:NB * c + 4 * g + 4, :].rearrange("p j t -> p (j t)"), bank(1 + g)), ("T", c, g))
            assert PA["xnT"] == count
            act.wait_ge(ld_w, 80)
            tick(act.activation(f_abs, f_raw, ACT.Abs, accum_out=fsm[:, 0:1]), "abs")
            act.wait_ge(ld_small, 64)
            tick(act.activation(a_pos[:], alog[:], ACT.Exp), "a")
            act.wait_ge(pv, PV["az"])
            tick(act.activation(EZ, AZ, ACT.Exp, scale=-1.0), "ez")
            act.wait_ge(pv, PV["scal"])
            tick(act.activation(tiles(ES), scal[:, :, 8:16], ACT.Exp, scale=-1.0), "es")
            act.wait_ge(pa, PA["ez"])
            tick(act.activation(LZ, EZ, ACT.Ln, bias=1.0), "lz")
            act.wait_ge(pv, PV["nla"])
            tick(act.activation(ALPHA, NLA, ACT.Exp), "alpha")
            act.wait_ge(pp, PP["cums"])
            tick(act.activation(DEC, bank(1)[:, 0:NT * H], ACT.Exp), "dec")
            tick(act.activation(SUF, bank(2)[:, 0:NT * H], ACT.Exp), "suf")
            tick(act.activation(packed[:, :, CD:CD + H], tiles(bank(3)[:, 0:NT * H]), ACT.Exp), "cd")
            act.wait_ge(pp, PP["rows"])
            tick(evac(rows_sb[:, 0, :, 1:P], bank(6)[:, 0:2 * P].rearrange("p (k t) -> p k t", k=2)[:, :, 1:P]), "rows_a")
            tick(evac(rows_sb[:, 1, :, :], bank(6)[:, 2 * P:4 * P].rearrange("p (k t) -> p k t", k=2)), "rows")
            for g in range(4):
                act.wait_ge(pp, PP["W", g])
                tick(evac(w_sel[:, 512 * g:512 * g + 512], bank(6 if g % 2 else 7)), ("W", g))
            act.wait_ge(pp, PP["W", 4])
            tick(evac(w_in[:], bank(7)), ("W", 4))
            act.wait_ge(pp, PP["W", 6])
            tick(evac(w_qkv[:], bank(6)[:, 0:3 * D]), ("W", 6))
            act.wait_ge(pp, PP["W", 7])
            tick(evac(w_of[:].rearrange("p k d -> p (k d)"), bank(7)[:, 0:2 * D]), ("W", 7))
            act.wait_ge(pv, PV["red"])
            tick(act.activation(packed[:, :, SIN:SIN + H], tiles(R1), ACT.Sin), "sin")
            tick(act.activation(packed[:, :, COS:COS + H], tiles(R2), ACT.Sin), "packed")

            def u_out(c, k):
                i2, tile = (k // 2) % 2, NB * c + k // 2
                act.wait_ge(u_pe, tile + 1)
                after(act, y_pe, 2 * (tile - 2) + 2)
                if has_state(c, k - 4):
                    after(act, wu_pool, 2 * (tile - 2) + 2)
                evac(u_nat[i2], bank(BK_M)).then_inc(u_act, 1)

            def b_sin(c, k):
                h, i2, n = k % 2, (k // 2) % 2, UNITS * c + k
                act.wait_ge(bc_dve, n + 1)
                act.wait_ge(sct_in[i2], 16 * (NB // 2 * c + k // 4 + 1))
                after(act, bn_pool, n - 1)
                for q in range(HH):
                    last = act.activation(bs[h][:, N * q:N * q + N], bank(BK_B)[:, N * q:N * q + N], ACT.Copy,
                                          scale=sct[i2][:, SIN + HH * h + q:SIN + HH * h + q + 1])
                last.then_inc(bs_act, 1)

            def c_turn(c, k, part):
                h, i2, n = k % 2, (k // 2) % 2, UNITS * c + k
                if part == 0:
                    act.wait_ge(c_pe, n + 1)
                    act.wait_ge(sct_in[i2], 16 * (NB // 2 * c + k // 4 + 1))
                    after(act, cn_pool, n - 1)
                for q in (2 * part, 2 * part + 1):
                    for dst, at in ((cc_, COS), (cs, SIN)):
                        last = act.activation(dst[h][:, N * q:N * q + N], bank(BK_C)[:, N * q:N * q + N], ACT.Copy,
                                              scale=sct[i2][:, at + HH * h + q:at + HH * h + q + 1])
                if part == 1:
                    last.then_inc(c_act, 1)

            def bT_out(c, k):
                h, n = k % 2, UNITS * c + k
                act.wait_ge(tb_pe, n + 1)
                after(act, g_pe, n - 1)
                evac(bT[h], bank(BK_T)).then_inc(bT_act, 1)

            def cT_out(c, k):
                h, n = k % 2, UNITS * c + k
                act.wait_ge(tc_pe, n + 1)
                after(act, y_pe, n - 1)
                evac(cT[h], bank(BK_T)).then_inc(cT_act, 1)

            def y_square(c, b):
                tile = NB * c + b
                act.wait_ge(y_dve, 2 * tile + 2)
                after(act, ys_dve, tile)
                act.activation(ysq[:], yT[b % 2], ACT.Square).then_inc(ysq_act, 1)

            def f_T_out(c, t):
                act.wait_ge(f_pe, use_done(("T", t), c))
                evac(xnT_f[:, 4 * (t % 2):4 * (t % 2) + 4, :].rearrange("p j t -> p (j t)"), bank(BK_F[USES.index(("T", t)) % 2])).then_inc(f_T, 1)

            def f_qkv_out(c, s):
                act.wait_ge(f_pe, use_done(("Q", s), c))
                evac(qkv[:, s, :], bank(BK_F[USES.index(("Q", s)) % 2])[:, 0:3 * D]).then_inc(f_q, 1)

            def f_softmax_exp(c):
                act.wait_ge(f_v, v_step("sub", c))
                act.activation(att, att, ACT.Exp, scale=float(AD) ** -0.5).then_inc(f_exp, 1)

            pieces = []
            for t in range(8):
                place(pieces, f"T{t}", lambda c, t=t: f_T_out(c, t))
            place(pieces, "exp", f_softmax_exp)
            for q in range(NB):
                place(pieces, f"qadd{q}", lambda c, q=q: f_qkv_out(c, q))

            def f_square(c, k):
                act.wait_ge(f_v, v_step(f"xc{k}", c))
                act.activation(prod[:, 1], xn.rearrange("p s d -> p (s d)"), ACT.Square).then_inc(f_sq, 1)

            for k in range(3):
                place(pieces, f"sq{k}", lambda c, k=k: f_square(c, k))

            def f_load(c):
                act.wait_ge(rows_free, 16 * c + 16)
                act.dma_start(xres, x_rows[c]).then_inc(fx_in, 16)

            def f_store(c):
                act.wait_ge(f_x, x_step(XSTEPS[-1], c))
                act.dma_start(out_rows[c], xres).then_inc(rows_free, 16)

            place(pieces, "load", f_load)
            place(pieces, "store", f_store)

            def step(c, k, follow, first=False, last=False):
                nxt = not (last and k == UNITS - 1)
                if k % 2 == 1 and nxt:
                    u_out(c, k + 1)
                if nxt:
                    b_sin(c, k + 1)
                at_pos(pieces, POS * k, follow)
                bT_out(c, k)
                if nxt:
                    c_turn(c, k + 1, 0)
                cT_out(c, k)
                at_pos(pieces, POS * k + 1, follow)
                if nxt:
                    c_turn(c, k + 1, 1)
                if k % 2 == 0 and not (first and k == 0):
                    y_square(c, k // 2 - 1)
                at_pos(pieces, POS * k + 2, follow)

            def finish(c):
                y_square(c, NB - 1)

            u_out(0, 0)
            b_sin(0, 0)
            c_turn(0, 0, 0)
            c_turn(0, 0, 1)
            run_chunks(act, step, pieces, finish)
            act.wait_ge(rows_free, 16 * NC + 16)

        @block.vector
        def _(dve):
            count = 0

            def tick(ins, name=None, wait=False):
                nonlocal count
                count += 1
                ins.then_inc(pv, 1)
                if name is not None:
                    assert PV[name] == count, (name, count)
                if wait:
                    dve.wait_ge(pv, count)

            dve.memset(rows_sb[:, 0, :, 0:1], 0.0)
            dve.wait_ge(consts, 3)
            tick(dve.tensor_reduce(even[:], ident[:].rearrange("p (a k) -> p k a", k=2), AX.X, ALU.add), "even")

            def normalise(dst, src, mean_var, root):
                for b in range(NB):
                    last = dve.tensor_scalar(dst[:, b], src[:, b], mean_var[:, b, 0:1], root[:, b:b + 1],
                                             ALU.subtract, ALU.mult)
                return last

            for c in range(NC + 1):
                if c < NC:
                    dve.wait_ge(ld_x[c], 16)
                    for b in range(NB):
                        last = dve.bn_stats(stats4[:, c, b], x_all[:, NB * c + b, :])
                    tick(last, ("bn", c), wait=True)
                    for b in range(NB):
                        last = dve.bn_aggr(mv4[:, c, b], stats4[:, c, b])
                    tick(last, ("aggr", c))
                if c >= 1:
                    dve.wait_ge(pg, 2 * c)
                    after(dve, pp, PP["T", c - 3, 1] if c >= 3 else 0)
                    tick(normalise(xn_pro[(c - 1) % 2], x_all[:, NB * (c - 1):NB * c, :], mv4[:, c - 1], rstd4[:, c - 1]), ("xn", c - 1))
            for c in range(NC):
                for g in range(2):
                    dve.wait_ge(pp, PP["scal", c, g])
                    tick(dve.tensor_copy(scal[:, NB * c + 4 * g:NB * c + 4 * g + 4, :],
                                         bank(3 + g).rearrange("p (j e) -> p j e", e=P)[:, :, P - 24:P]), ("scal", c, g))
            dve.wait_ge(ld_small, 64)
            dve.wait_ge(pv, PV["scal"])
            per_head = dtb[:].unsqueeze(1).broadcast_to([P, NT, H])
            tick(dve.tensor_tensor(tiles(Z), scal[:, :, 0:8], per_head, ALU.add), None, True)
            tick(dve.scalar_tensor_tensor(AZ, Z, -1.0, Z, ALU.mult, ALU.max), "az")
            tick(dve.tensor_scalar(RZ, Z, 0.0, None, ALU.max))
            dve.wait_ge(pa, PA["lz"])
            dve.wait_ge(pv, count)
            tick(dve.tensor_tensor(DT, RZ, LZ, ALU.add), "dt", True)
            dve.wait_ge(pa, PA["a"])
            per_head = a_pos[:].unsqueeze(1).broadcast_to([P, NT, H])
            tick(dve.scalar_tensor_tensor(tiles(NLA), tiles(DT), -1.0, per_head, ALU.mult, ALU.mult), "nla")
            tick(dve.tensor_tensor(tiles(V), tiles(DT), scal[:, :, 16:24], ALU.mult), "v", True)
            W = NB * H
            tick(dve.memset(VP[:, 0:W], 0.0), None, True)
            for c in range(1, NC):
                tick(dve.tensor_tensor(VP[:, W * c:W * (c + 1)], VP[:, W * (c - 1):W * c], V[:, W * (c - 1):W * c], ALU.add),
                     "vp" if c == NC - 1 else None, True)
            tick(dve.tensor_scalar(TMP, ES, 1.0, None, ALU.add), None, True)
            tick(dve.reciprocal(LAM, TMP), None, True)
            tick(dve.tensor_scalar(OM, LAM, -1.0, 1.0, ALU.mult, ALU.add), None, True)
            tick(dve.tensor_tensor(GAM, LAM, DT, ALU.mult))
            tick(dve.tensor_tensor(DEL, OM, DT, ALU.mult), None, True)
            dve.wait_ge(pa, PA["alpha"])
            tick(dve.tensor_tensor(BETA, DEL, ALPHA, ALU.mult), "beta")
            dve.wait_ge(pp, PP["phi"])
            c1, c2, c3 = pi_parts()
            tick(dve.tensor_scalar(R1, bank(0)[:, 0:NT * H], 1.0 / TWO_PI, ROUND, ALU.mult, ALU.add), None, True)
            tick(dve.tensor_scalar(R1, R1, -ROUND, None, ALU.add), None, True)
            tick(dve.scalar_tensor_tensor(PHI, R1, -c1, bank(0)[:, 0:NT * H], ALU.mult, ALU.add), None, True)
            tick(dve.scalar_tensor_tensor(R2, R1, -c2, PHI, ALU.mult, ALU.add), None, True)
            tick(dve.scalar_tensor_tensor(PHI, R1, -c3, R2, ALU.mult, ALU.add), None, True)
            pi32 = float(np.nextafter(np.float32(np.pi), np.float32(0)))
            tick(dve.tensor_scalar(R1, PHI, pi32, -pi32, ALU.min, ALU.max), None, True)
            tick(dve.scalar_tensor_tensor(R2, R1, -1.0, R1, ALU.mult, ALU.max), None, True)
            tick(dve.tensor_scalar(R2, R2, -1.0, float(np.pi / 2), ALU.mult, ALU.add), "red")
            dve.wait_ge(pp, PP["shifts"])
            tick(dve.tensor_tensor(G1, GAM, bank(4)[:, 0:NT * H], ALU.add), None, True)
            dve.wait_ge(pa, PA["suf"])
            tick(dve.tensor_tensor(packed[:, :, SW:SW + H], tiles(G1), tiles(SUF), ALU.mult))
            tick(dve.tensor_copy(TMP, bank(5)[:, 0:NT * H]), None, True)
            tick(dve.tensor_tensor(DIF, GAM, TMP, ALU.subtract), None, True)
            pairs = packed[:, :, BAND:BAND + 2 * H].rearrange("p j (h k) -> p j h k", k=2)
            for k in range(2):
                tick(dve.scalar_tensor_tensor(pairs[:, :, :, k], tiles(DIF), even[:, k:k + 1], tiles(TMP), ALU.mult, ALU.add),
                     "packed" if k == 1 else None)
            dve.wait_ge(pa, PA["cd"])
            tick(dve.tensor_scalar(fsm[:, 1:2], bank(3)[:, NT * H:NT * H + 1], 1.0 / (D * D), TERNARY, ALU.mult, ALU.mult), None, True)
            tick(dve.tensor_scalar(fsm[:, 2:3], fsm[:, 1:2], -1.0, None, ALU.mult), None, True)
            tick(dve.tensor_scalar(f_abs, f_raw, fsm[:, 1:2], alpha_c[:, 0:1], ALU.is_gt, ALU.mult))
            tick(dve.tensor_scalar(f_lo, f_raw, fsm[:, 2:3], alpha_c[:, 0:1], ALU.is_lt, ALU.mult), None, True)
            tick(dve.tensor_tensor(f_tern, f_abs, f_lo, ALU.subtract), "tern")
            dve.wait_ge(pp, PP["W", 5])
            for j in range(4):
                dve.tensor_scalar(w_out[:, j], bank(5)[:, P * j:P * j + P], rms_c[:, j:j + 1], None, ALU.mult)
            dve.wait_ge(bias_split, 5)
            dve.memset(state[:, 0:NB // 2], 0.0).then_inc(rows_free, 16)
            tick(dve.memset(state[:, NB // 2:NB], 0.0), "w_out")

            def b_cos(c, k):
                h, i2, n = k % 2, (k // 2) % 2, UNITS * c + k
                dve.wait_ge(b_pe, n + 1)
                dve.wait_ge(sct_in[i2], 16 * (NB // 2 * c + k // 4 + 1))
                after(dve, bn_pool, n - 1)
                cosv = sct[i2][:, COS + HH * h:COS + HH * h + HH].unsqueeze(2).broadcast_to([P, HH, N])
                dve.tensor_tensor(bc[h].rearrange("p (h n) -> p h n", n=N), bank(BK_B).rearrange("p (h n) -> p h n", n=N),
                                  cosv, ALU.mult).then_inc(bc_dve, 1)

            def scan(c, k):
                h, i2, n = k % 2, (k // 2) % 2, UNITS * c + k
                dve.wait_ge(arow_in[i2], 16 * (NB // 2 * c + k // 4 + 1))
                dve.wait_ge(band_pool, n + 1)
                dve.tensor_tensor_scan(lmat[h], arow[i2][:, HH * P * h:HH * P * (h + 1)], band[h], 0.0,
                                       ALU.mult, ALU.add).then_inc(l_dve, 1)

            def weigh_scores(c, k):
                h, n = k % 2, UNITS * c + k
                dve.wait_ge(g_pe, n + 1)
                dve.wait_ge(l_dve, n + 1)
                after(dve, y_pe, n - 1)
                dve.tensor_tensor(mmat[h], bank(BK_G), lmat[h], ALU.mult).then_inc(m_dve, 1)

            def y_of(c, k, inter):
                h, i2, n = k % 2, (k // 2) % 2, UNITS * c + k
                tile = NB * c + k // 2
                dve.wait_ge(y_pe, n + 1)
                after(dve, o_pe, tile - 1)
                dst = yT[i2][:, 2 * P * h:2 * P * (h + 1)]
                if inter:
                    dve.wait_ge(drow_in[i2], 32 * (NB // 2 * c + k // 4 + 1))
                    dve.tensor_tensor(yinter[:], bank(BK_Y)[:, 2 * P:4 * P], drow[i2][:, 2 * P * h:2 * P * (h + 1)],
                                      ALU.mult).then_inc(yi_dve, 1)
                    dve.wait_ge(yi_dve, n - UNITS + 2)
                    dve.tensor_tensor(dst, bank(BK_Y)[:, 0:2 * P], yinter[:], ALU.add).then_inc(y_dve, 1)
                else:
                    dve.tensor_copy(dst, bank(BK_Y)[:, 0:2 * P]).then_inc(y_dve, 1)

            def state_of(c, k):
                h, i2, n = k % 2, (k // 2) % 2, UNITS * c + k
                b = k // 2
                st = state[:, b, HH * PD * h:HH * PD * (h + 1)].rearrange("p (h q) -> p h q", q=PD)
                dec = sct[i2][:, CD + HH * h:CD + HH * h + HH].unsqueeze(2).broadcast_to([P, HH, PD])
                dve.tensor_tensor(sdec[:].rearrange("p (h q) -> p h q", q=PD), st, dec, ALU.mult).then_inc(sd_dve, 1)
                dve.wait_ge(s_pe, n + 1)
                dve.wait_ge(sd_dve, n + 1)
                own = bank(BK_G).rearrange("p (h q) -> p h q", q=N)[:, :, 0:PD]
                dve.tensor_tensor(st, sdec[:].rearrange("p (h q) -> p h q", q=PD), own, ALU.add).then_inc(s_dve, 1)

            def y_sum(c, b):
                tile = NB * c + b
                dve.wait_ge(ysq_act, tile + 1)
                after(dve, o_pe, tile - 1)
                dve.tensor_reduce(ysum[b % 2], ysq[:].rearrange("p (j t) -> p t j", t=P), AX.X, ALU.add).then_inc(ys_dve, 1)

            def o_out(c, b):
                dve.wait_ge(o_pe, NB * c + b + 1)
                dve.tensor_copy(oraw[:, b, 0:D + 1], bank(BK_M)[:, 0:D + 1]).then_inc(o_dve, 1)

            def f_x1(c):
                dve.wait_ge(f_g, len(GSTEPS) * c + GSTEPS.index("rr") + 1)
                dve.wait_ge(fx_in, 16 * c + 16)
                t = prod[:, 0].rearrange("p (s d) -> p s d", s=NB)
                dve.scalar_tensor_tensor(t, oraw[:, :, 0:D], float(np.sqrt(H * PD)), rr_f[:].unsqueeze(2).broadcast_to([P, NB, D]),
                                         ALU.mult, ALU.mult).then_inc(f_v, 1)
                dve.wait_ge(f_v, v_step("scaled", c))
                dve.tensor_tensor(xres, xres, t, ALU.add).then_inc(f_x, 1)

            def f_mean(c, k):
                dve.wait_ge(f_x, x_step(["x1", ("F", 1), ("O", 1)][k], c))
                dve.tensor_reduce(mean_f[:], xres, AX.X, ALU.add).then_inc(f_v, 1)
                dve.wait_ge(f_v, v_step(f"mean{k}", c))
                dve.scalar_tensor_tensor(xn, mean_f[:].unsqueeze(2).broadcast_to([P, NB, D]), -1.0 / D, xres,
                                         ALU.mult, ALU.add).then_inc(f_v, 1)

            def f_var(c, k):
                dve.wait_ge(f_sq, 3 * c + k + 1)
                dve.tensor_reduce(var_f[:], prod[:, 1].rearrange("p (s d) -> p s d", s=NB), AX.X, ALU.add).then_inc(f_v, 1)

            def f_norm(c, k):
                dve.wait_ge(f_g, g_step(f"rs{k}", c))
                dve.scalar_tensor_tensor(xn, xn, float(np.sqrt(D)), rs_f[:].unsqueeze(2).broadcast_to([P, NB, D]),
                                         ALU.mult, ALU.mult).then_inc(f_v, 1)

            def f_add(c, what):
                g = what[1] % 2
                dve.wait_ge(f_pe, use_done(what, c))
                rows = xres[:, 4 * g:4 * g + 4, :].rearrange("p j d -> p (j d)")
                dve.tensor_tensor(rows, bank(BK_F[USES.index(what) % 2]), rows, ALU.add).then_inc(f_x, 1)

            def f_product(c, m):
                attention_product(dve, c, m, f_prod_v)

            def f_reduce(c, m):
                if m in POOL_PRODUCTS:
                    dve.wait_ge(f_prod_g, len(POOL_PRODUCTS) * c + POOL_PRODUCTS.index(m) + 1)
                else:
                    mine = [q for q in range(2 * NB) if q not in POOL_PRODUCTS]
                    dve.wait_ge(f_prod_v, len(mine) * c + mine.index(m) + 1)
                if m < NB:
                    dve.tensor_reduce(att[:, P * m:P * (m + 1)], prod[:, m % 2].rearrange("p (e d) -> p e d", d=AD),
                                      AX.X, ALU.add).then_inc(f_red, 1)
                else:
                    dve.tensor_reduce(xn[:, m - NB, :], prod[:, m % 2].rearrange("p (r e) -> p e r", r=NB),
                                      AX.X, ALU.add).then_inc(f_red, 1)

            def f_softmax(c):
                dve.wait_ge(f_red, 2 * NB * c + NB)
                dve.tensor_reduce(amax[:], att_s.rearrange("p s r h -> p s h r"), AX.X, ALU.max).then_inc(f_v, 1)
                dve.wait_ge(f_v, v_step("max", c))
                dve.tensor_tensor(att_s, att_s, amax[:].unsqueeze(2).broadcast_to([P, NB, NB, AH]), ALU.subtract).then_inc(f_v, 1)

            def f_norms(c):
                dve.wait_ge(f_exp, c + 1)
                dve.tensor_reduce(asum[:], att_s.rearrange("p s r h -> p s h r"), AX.X, ALU.add).then_inc(f_v, 1)
                dve.wait_ge(f_v, v_step("sum", c))
                dve.reciprocal(asum[:], asum[:]).then_inc(f_v, 1)

            def f_onorm(c):
                dve.wait_ge(f_red, 2 * NB * c + 2 * NB)
                dve.wait_ge(f_v, v_step("rec", c))
                rows = xn.rearrange("p s (h d) -> p (s h) d", d=AD)
                dve.tensor_tensor(rows, rows, asum[:].rearrange("p s h -> p (s h)").unsqueeze(2).broadcast_to([P, NB * AH, AD]),
                                  ALU.mult).then_inc(f_v, 1)

            pieces = []
            place(pieces, "x1", f_x1)
            for k in range(3):
                place(pieces, f"mean{k}", lambda c, k=k: f_mean(c, k))
                place(pieces, f"var{k}", lambda c, k=k: f_var(c, k))
                place(pieces, f"xn{k}", lambda c, k=k: f_norm(c, k))
            for what in (("F", 0), ("F", 1), ("O", 0), ("O", 1), ("F", 2), ("F", 3)):
                place(pieces, f"add{what[0]}{what[1]}", lambda c, what=what: f_add(c, what))
            for m in range(2 * NB):
                if m not in POOL_PRODUCTS:
                    place(pieces, f"prod{m}", lambda c, m=m: f_product(c, m))
                place(pieces, f"red{m}", lambda c, m=m: f_reduce(c, m))
            place(pieces, "softmax", f_softmax)
            place(pieces, "norms", f_norms)
            place(pieces, "onorm", f_onorm)

            def step(c, k, follow, first=False, last=False):
                nxt = not (last and k == UNITS - 1)
                before = not (first and k == 0)
                pc, pk = (c, k - 1) if k else (c - 1, UNITS - 1)
                if nxt:
                    b_cos(c, k + 1)
                at_pos(pieces, POS * k, follow)
                if before:
                    y_of(pc, pk, not first)
                    if (not last or k == 0):
                        state_of(pc, pk)
                if nxt:
                    scan(c, k + 1)
                at_pos(pieces, POS * k + 1, follow)
                weigh_scores(c, k)
                if k % 2 == 0 and before:
                    y_sum(c, k // 2 - 1)
                if k % 2 == 1 and not (first and k == 1):
                    o_out(c if k > 1 else c - 1, (k // 2 - 1) % NB)
                at_pos(pieces, POS * k + 2, follow)

            def finish(c):
                y_of(c, UNITS - 1, True)
                y_sum(c, NB - 1)
                o_out(c, NB - 1)

            b_cos(0, 0)
            scan(0, 0)
            run_chunks(dve, step, pieces, finish)

        @block.tensor
        def _(pe):
            count = 0

            def tick(ins, name):
                nonlocal count
                count += 1
                ins.then_inc(pp, 1)
                assert PP[name] == count, (name, count)

            def turn(k, src, into=0):
                for q, s in enumerate(src):
                    last = pe.transpose(bank(k)[:, into + P * q:into + P * q + P], s, ident[:])
                return last

            pe.wait_ge(consts, 2)
            pe.wait_ge(ld_scal, 16)
            tick(turn(0, [scal_raw]), "scal_w")
            for c in range(NC + 1):
                if c < NC:
                    for g in range(2):
                        pe.wait_ge(pv, PV["xn", c])
                        after(pe, pa, PA["T", c - 1, g] if c else 0)
                        tick(turn(1 + g, [xn_pro[c % 2][:, 4 * g + q, :] for q in range(4)]), ("T", c, g))
                if c >= 1:
                    for g in range(2):
                        pe.wait_ge(pa, PA["T", c - 1, g])
                        after(pe, pv, PV["scal", c - 2, g] if c >= 2 else 0)
                        for q in range(4):
                            last = pe.matmul(bank(3 + g)[:, P * q:P * q + P], xnT[:, NB * (c - 1) + 4 * g + q, :], w_scal[:],
                                             start=True, stop=True)
                        tick(last, ("scal", c - 1, g))
            groups = [[sel_raw[:, 4 * g + q, :] for q in range(4)] for g in range(4)]
            groups += [[in_raw[:, q, :] for q in range(4)], [out_raw[:, P * q:P * q + P] for q in range(4)],
                       [qkv_raw[:, q, :] for q in range(3)], [ob_raw, f_tern]]
            col = slice(0, NT * H)
            total = NT * H
            pe.wait_ge(consts, 3)
            pe.wait_ge(pv, PV["vp"])
            pe.matmul(bank(0)[:, col], upto[:], V, start=True, stop=False)
            tick(pe.matmul(bank(0)[:, col], ones[:], VP, start=False, stop=True), "phi")
            pe.matmul(bank(1)[:, col], upto[:], NLA, start=True, stop=True)
            pe.matmul(bank(2)[:, col], later[:], NLA, start=True, stop=True)
            pe.matmul(bank(3)[:, col], ones[:], NLA, start=True, stop=True)
            pe.wait_ge(pa, PA["abs"])
            tick(pe.matmul(bank(3)[:, total:total + 1], ones[:], fsm[:, 0:1], start=True, stop=True), "cums")
            pe.wait_ge(pa, PA["dec"])
            turn(6, [ALPHA[:, 0:P], ALPHA[:, P:2 * P]])
            tick(turn(6, [DEC[:, 0:P], DEC[:, P:2 * P]], 2 * P), "rows")
            pe.wait_ge(pv, PV["beta"])
            pe.matmul(bank(4)[:, col], shift[:], DEL, start=True, stop=False)
            pe.matmul(bank(4)[:, 0:total - NB * H], carry[:], DEL[:, NB * H:total], start=False, stop=True)
            tick(pe.matmul(bank(5)[:, col], shift[:], BETA, start=True, stop=True), "shifts")
            bank_of = [7, 6, 7, 6, 7, 5, 6, 7]
            freed = {0: None, 1: ("rows", pa), 2: (("W", 0), pa), 3: (("W", 1), pa), 4: (("W", 2), pa), 6: (("W", 3), pa), 7: (("W", 4), pa)}
            for g in range(8):
                pe.wait_ge(ld_sel if g < 4 else ld_w, 16 if g < 4 else 80)
                if g == 5:
                    pe.wait_ge(pv, PV["packed"])
                elif freed[g]:
                    pe.wait_ge(pa, PA[freed[g][0]])
                if g == 7:
                    pe.wait_ge(pv, PV["tern"])
                tick(turn(bank_of[g], groups[g]), ("W", g))

            pe.wait_ge(bias_in, 144)
            pe.wait_ge(pa, PA["W", 7])
            pe.wait_ge(pv, PV["w_out"])

            def project(c, k):
                h, i2, n = k % 2, (k // 2) % 2, UNITS * c + k
                tile = NB * c + k // 2
                pe.wait_ge(xt_in[i2], 16 * (NB // 2 * c + k // 4 + 1))
                if h == 0:
                    after(pe, u_act, tile)
                    after(pe, o_dve, tile - 2)
                    pe.matmul(bank(BK_M), xt[i2], w_in[:], start=True, stop=True).then_inc(u_pe, 1)
                after(pe, bs_act, n)
                pe.matmul(bank(BK_B), xt[i2], w_sel[:, HH * N * h:HH * N * (h + 1)], start=True, stop=True).then_inc(b_pe, 1)
                after(pe, c_act, n)
                pe.matmul(bank(BK_C), xt[i2], w_sel[:, H * N + HH * N * h:H * N + HH * N * (h + 1)],
                          start=True, stop=True).then_inc(c_pe, 1)

            def turn_b(c, k):
                h, n = k % 2, UNITS * c + k
                pe.wait_ge(bn_pool, n + 1)
                after(pe, cT_act, n)
                turn(BK_T, [bn[h][:, N * q:N * q + N] for q in range(HH)]).then_inc(tb_pe, 1)

            def turn_c(c, k):
                h, n = k % 2, UNITS * c + k
                pe.wait_ge(cn_pool, n + 1)
                pe.wait_ge(bT_act, n + 1)
                turn(BK_T, [cn[h][:, N * q:N * q + N] for q in range(HH)]).then_inc(tc_pe, 1)

            def scores(c, k):
                h, n = k % 2, UNITS * c + k
                pe.wait_ge(bT_act, n + 1)
                pe.wait_ge(cT_act, n + 1)
                after(pe, m_dve, n)
                if has_state(c, k - 1):
                    after(pe, s_dve, n)
                for q in range(HH):
                    last = pe.matmul(bank(BK_G)[:, P * q:P * q + P], bT[h][:, P * q:P * q + P], cT[h][:, P * q:P * q + P],
                                     start=True, stop=True)
                last.then_inc(g_pe, 1)

            def outputs(c, k, inter):
                h, i2, n = k % 2, (k // 2) % 2, UNITS * c + k
                b, tile = k // 2, NB * c + k // 2
                pe.wait_ge(m_dve, n + 1)
                pe.wait_ge(u_act, tile + 1)
                after(pe, y_dve, n)
                for q in range(HH):
                    rows, at = slice(64 * (q % 2), 64 * (q % 2) + 64), P * (q // 2)
                    last = pe.matmul(bank(BK_Y)[rows, at:at + P], u_nat[i2][:, PD * (HH * h + q):PD * (HH * h + q + 1)],
                                     mmat[h][:, P * q:P * q + P], start=True, stop=True)
                if inter:
                    if isinstance(c, int) or k < UNITS - 1:
                        pe.wait_ge(s_dve, n - UNITS + 1)
                    for q in range(HH):
                        rows, at = slice(64 * (q % 2), 64 * (q % 2) + 64), 2 * P + P * (q // 2)
                        last = pe.matmul(bank(BK_Y)[rows, at:at + P], state[:, b, PD * (HH * h + q):PD * (HH * h + q + 1)],
                                         cT[h][:, P * q:P * q + P], start=True, stop=True)
                last.then_inc(y_pe, 1)

            def states(c, k):
                h, n = k % 2, UNITS * c + k
                pe.wait_ge(wu_pool, n + 1)
                after(pe, m_dve, n + 1)
                for q in range(HH):
                    at = 2 * P * (q // 2) + 64 * (q % 2)
                    last = pe.matmul(bank(BK_G)[:, at:at + P], bn[h][:, N * q:N * q + N],
                                     wu[h][:, 2 * PD * (q // 2):2 * PD * (q // 2) + 2 * PD], start=True, stop=True)
                last.then_inc(s_pe, 1)

            def project_out(c, b, more):
                tile = NB * c + b
                pe.wait_ge(ys_dve, tile + 1)
                pe.wait_ge(u_act, tile + 3 if more else NT)
                for j in range(4):
                    pe.matmul(bank(BK_M)[:, 0:D], yT[b % 2][:, P * j:P * j + P], w_out[:, j], start=(j == 0), stop=(j == 3))
                pe.matmul(bank(BK_M)[:, D:2 * D], ysum[b % 2], ones[:], start=True, stop=True).then_inc(o_pe, 1)

            def f_free(c, use):
                m = USES.index(use)
                what, q = USES[m - 2]
                if m < 2:
                    return
                if what == "T":
                    pe.wait_ge(f_T, 8 * c + q + 1)
                elif what == "Q":
                    pe.wait_ge(f_q, NB * c + q + 1)
                else:
                    pe.wait_ge(f_x, x_step((what, q), c))

            def f_bank(use):
                return bank(BK_F[USES.index(use) % 2])

            def f_turn(c, t):
                f_free(c, ("T", t))
                pe.wait_ge(f_v, v_step(["xn0", "xn1", "onorm", "xn2"][t // 2], c))
                turn(BK_F[USES.index(("T", t)) % 2], [xn[:, 4 * (t % 2) + q, :] for q in range(4)]).then_inc(f_pe, 1)

            def f_project(c, use):
                what, q4 = use
                f_free(c, use)
                w = w_of[:, 0 if what == "O" else 1]
                first_t = 4 if what == "O" else 0 if q4 < 2 else 6
                pe.wait_ge(f_T, 8 * c + first_t + q4 % 2 + 1)
                at = BIAS_O if what == "O" else BIAS_F
                pe.matmul(f_bank(use), ones3[:], bias3[:, at:at + 4 * D], start=True, stop=False)
                for q in range(4):
                    last = pe.matmul(f_bank(use)[:, P * q:P * q + P], xnT_f[:, 4 * (q4 % 2) + q, :], w, start=False, stop=(q == 3))
                last.then_inc(f_pe, 1)

            def f_qkv(c, s):
                f_free(c, ("Q", s))
                dst = f_bank(("Q", s))[:, 0:3 * D]
                pe.matmul(dst, ones3[:], bias3[:, 0:3 * D], start=True, stop=False)
                pe.matmul(dst, xnT_f[:, s, :], w_qkv[:], start=False, stop=True).then_inc(f_pe, 1)

            pieces = []
            for what, q in USES:
                if what == "T":
                    place(pieces, f"T{q}", lambda c, q=q: f_turn(c, q))
                elif what == "Q":
                    place(pieces, f"qkv{q}", lambda c, q=q: f_qkv(c, q))
                else:
                    place(pieces, f"{what}{q}", lambda c, what=what, q=q: f_project(c, (what, q)))

            def step(c, k, follow, first=False, last=False):
                nxt = not (last and k == UNITS - 1)
                before = not (first and k == 0)
                pc, pk = (c, k - 1) if k else (c - 1, UNITS - 1)
                if nxt:
                    project(c, k + 1)
                turn_b(c, k)
                at_pos(pieces, POS * k, follow)
                if before:
                    outputs(pc, pk, not first)
                turn_c(c, k)
                if before and (not last or k == 0):
                    states(pc, pk)
                at_pos(pieces, POS * k + 1, follow)
                if k % 2 == 1 and not (first and k == 1):
                    project_out(c if k > 1 else c - 1, (k // 2 - 1) % NB, not (last and k >= UNITS - 1))
                scores(c, k)
                at_pos(pieces, POS * k + 2, follow)

            def finish(c):
                outputs(c, UNITS - 1, True)
                project_out(c, NB - 1, False)

            project(0, 0)
            run_chunks(pe, step, pieces, finish)


_INS = ["L0_attn_a_x", "L0_attn_a_in_proj_w", "L0_attn_a_sel_proj_w", "L0_attn_a_out_proj_w", "L0_attn_a_A_log",
        "L0_attn_a_dt_bias", "L0_attn_a_rms_weight", "L0_attn_b_in_proj_w", "L0_attn_b_in_proj_b",
        "L0_attn_b_out_proj_w", "L0_attn_b_out_proj_b", "L0_ffn_weight", "L0_ffn_alpha", "L0_ffn_bias"]


def kernel(**inputs):
    import concourse.bacc as bacc
    from concourse.bass_utils import run_bass_kernel_spmd

    nc = bacc.Bacc("TRN2", target_bir_lowering=False, num_devices=1)
    arrays, args = {}, []
    for name in _INS:
        a = np.ascontiguousarray(inputs[name])
        arrays[f"in_{name}_dram"] = a
        args.append(nc.dram_tensor(f"in_{name}_dram", a.shape, mybir.dt.from_np(a.dtype), kind="ExternalInput").ap())
    args.append(nc.dram_tensor("out_dram", arrays["in_L0_attn_a_x_dram"].shape, F32, kind="ExternalOutput").ap())
    hybrid_block(nc, *args)
    r = run_bass_kernel_spmd(nc, [arrays], core_ids=[0])
    return r.results[0]["out_dram"]
```

```python
from contextlib import ExitStack

import numpy as np

import concourse.bass as bass
from concourse import mybir

F32 = mybir.dt.float32
ALU = mybir.AluOpType
ACT = mybir.ActivationFunctionType
AX = mybir.AxisListType
BF16 = mybir.dt.bfloat16
F32R = mybir.dt.float32r

P = 128
NB = 8
NC = 4
NT = NB * NC
H = 8
HH = 4
N = 128
PD = 64
D = 128
UNITS = 2 * NB
AH = 16
AD = D // AH
BIAS_F, BIAS_O = 3 * D, 7 * D
BIAS = 11 * D
BIAS_IN = 5 * D
SC = 48
COS, SIN, BAND, SW, CD = 0, 8, 16, 32, 40
EPS_LN, EPS_RMS = 1e-5, 1e-6
TERNARY = 0.7
TWO_PI = 2.0 * np.pi
ROUND = 1.5 * 2.0 ** 23
START = 10
POS = 3

USES = [("T", 0), ("F", 0), ("T", 1), ("F", 1), ("T", 2)] + [("Q", s) for s in range(4)] + \
       [("T", 3)] + [("Q", s) for s in range(4, NB)] + \
       [("T", 4), ("O", 0), ("T", 5), ("O", 1), ("T", 6), ("F", 2), ("T", 7), ("F", 3)]
NUSE = len(USES)
VSTEPS = ["scaled", "mean0", "xc0", "var0", "xn0", "mean1", "xc1", "var1", "xn1", "max", "sub", "sum", "rec", "onorm",
          "mean2", "xc2", "var2", "xn2"]
GSTEPS = ["ms", "rr", "ve0", "rs0", "ve1", "rs1", "ve2", "rs2"]
XSTEPS = ["x1", "ffn0", "attn", "ffn1"]
POOL_PRODUCTS = (2, 4, 5, 7, 8, 9, 10, 12, 13, 14, 15)


PLACE = {"load:0": 30, "rr:0": 30.01, "x1:0": 31, "mean0:0": 32, "sq0:0": 32.01, "var0:0": 33, "rs0:0": 34,
         "xn0:0": 35, "T0": 36, "F0": 37, "addF0": 39, "mean1:0": 40, "sq1:0": 41, "var1:0": 42, "rs1:0": 43,
         "xn1:0": 44, "load:1": 52, "rr:1": 52.01, "x1:1": 53, "mean0:1": 54, "sq0:1": 54.01, "var0:1": 54.02,
         "rs0:1": 54.03, "xn0:1": 54.04, "T1": 55, "F1": 55.01, "T2": 55.02, "addF1": 55.03, "mean1:1": 55.04,
         "sq1:1": 55.05, "var1:1": 56, "qkv0": 56.01, "qadd0": 56.02, "rs1:1": 56.03, "qkv1": 56.04, "qadd1": 56.05,
         "qkv2": 56.06, "qadd2": 56.07, "qkv3": 56.08, "qadd3": 56.09, "xn1:1": 56.10, "T3": 57, "qkv4": 57.01,
         "qadd4": 57.02, "qkv5": 57.03, "qadd5": 57.04, "qkv6": 57.05, "qadd6": 57.06, "qkv7": 57.07, "qadd7": 57.08,
         "prod0": 58, "red0": 58.01, "prod1": 59, "prod2": 59.01, "red1": 60, "red2": 60.01, "prod3": 60.02,
         "red3": 60.03, "prod4": 61, "red4": 61.01, "prod5": 61.02, "red5": 62, "prod6": 62.01, "red6": 62.02,
         "prod7": 62.03, "softmax:0": 63, "exp:0": 63.01, "red7": 63.02, "norms:0": 63.03, "softmax:1": 64,
         "exp:1": 66, "prod8": 66.01, "red8": 66.02, "prod9": 66.03, "norms:1": 67, "red9": 67.01, "prod10": 67.02,
         "red10": 67.03, "prod11": 68, "red11": 68.01, "prod12": 68.02, "prod13": 69, "onorm:0": 69.01,
         "red12": 69.02, "red13": 69.03, "prod14": 69.04, "T4": 70, "O0": 70.01, "addO0": 70.02, "mean2:0": 70.03,
         "sq2:0": 70.04, "red14": 70.05, "var2:0": 70.06, "prod15": 70.07, "rs2:0": 70.08, "red15": 71,
         "onorm:1": 72, "T5": 72.01, "xn2:0": 73, "O1": 73.01, "addO1": 73.02, "mean2:1": 73.03, "sq2:1": 74,
         "T6": 74.01, "var2:1": 74.02, "rs2:1": 74.03, "F2": 74.04, "addF2": 75, "store:0": 75.01, "xn2:1": 75.02,
         "T7": 75.03, "F3": 76, "addF3": 76.01, "store:1": 77}


def place(pieces, name, emit):
    pieces.append((PLACE[name], emit))
    pieces.sort(key=lambda piece: piece[0])


def at_pos(pieces, pos, c):
    for at, emit in pieces:
        if int(at) == pos:
            emit(c)


def run_chunks(eng, step, pieces, finish=None):
    for k in range(UNITS):
        step(0, k, pieces, first=True)
    with eng.Fori(1, NC - 1) as c:
        for k in range(UNITS):
            step(c, k, pieces)
    for k in range(UNITS):
        step(NC - 1, k, pieces, last=True)
    if finish:
        finish(NC - 1)
    for pos in range(POS * UNITS, POS * (UNITS + START)):
        at_pos(pieces, pos, NC - 1)


def at_step(pieces, c, k, sub):
    if k >= START:
        at_pos(pieces, POS * k + sub, c)
    elif not (isinstance(c, int) and c == 0):
        at_pos(pieces, POS * (UNITS + k) + sub, c - 1)


def v_step(name, c):
    return len(VSTEPS) * c + VSTEPS.index(name) + 1


def g_step(name, c):
    return len(GSTEPS) * c + GSTEPS.index(name) + 1


def x_step(name, c):
    return len(XSTEPS) * c + XSTEPS.index(name) + 1


def use_done(use, c):
    return NUSE * c + USES.index(use) + 1


def has_state(c, k):
    return not (isinstance(c, int) and c == NC - 1 and k >= 0)


def numbered(steps):
    return {name: at + 1 for at, name in enumerate(steps) if name is not None}


PA = numbered(["scal_w"] + [n for c in range(NC + 1) for n in
                            ([("xn", c)] if c < NC else []) + ([("T", c - 1, 0), ("T", c - 1, 1)] if c else [])] +
              ["abs", "a", ("W", 0), ("W", 1), "ez", "es", "lz", "alpha", "dec", "suf", "cd", ("W", 2), "rows_a", "rows",
               "sin", "packed"] + [("W", g) for g in (3, 4, 6, 7)])
PA["xnT"] = PA["T", NC - 1, 1]
PV = numbered(["even"] + [n for c in range(NC) for n in (("bn", c), ("aggr", c))] +
              [("scal", c, g) for c in range(NC) for g in range(2)] +
              [None, "az"] + [None] * 5 + ["dt", "nla", "v", None, None, "vp", ("lo", 0), None, None, "beta"] +
              [None] * 7 + ["red", ("lo", 1), ("lo", 2), None, None, None, None, None, "packed", None, None,
                            ("lo", 3), ("lo", 4), None, None, "tern", "w_out"])
PV["scal"] = PV["scal", NC - 1, 1]
PP = numbered(["scal_w"] + [n for c in range(NC + 1) for n in
                            ([("T", c, 0), ("T", c, 1)] if c < NC else []) +
                            ([("scal", c - 1, 0), ("scal", c - 1, 1)] if c else [])] +
              [("W", 0), ("W", 1), "phi", "cums", ("W", 2), "rows", "shifts"] + [("W", g) for g in range(3, 8)])


def pi_parts():
    c1 = 6.28125
    c2 = float(np.float32(np.round((TWO_PI - c1) * 2.0 ** 21) / 2.0 ** 21))
    return c1, c2, float(np.float32(TWO_PI - c1 - c2))


def hybrid_block(nc, x, in_w, sel_w, out_w, a_log, dt_bias, rms_w, qkv_w, qkv_b, ob_w, ob_b, f_w, f_alpha, f_b, out):
    ctx = ExitStack()
    with ctx:
        def sb(name, shape):
            return ctx.enter_context(nc.sbuf_tensor(name, shape, F32))

        def sem(name):
            return ctx.enter_context(nc.semaphore(name))

        def after(eng, s, count):
            if not isinstance(count, int) or count > 0:
                eng.wait_ge(s, count)

        x_rows = x.rearrange("b (c t) d -> c t b d", c=NC)
        out_rows = out.rearrange("b (c t) d -> c t b d", c=NC)
        alpha_rows = nc.dram_tensor("alpha_rows", [NT * H, P], F32, kind="Internal").ap()
        xT_rows = nc.dram_tensor("xT_rows", [NT, D, P], F32, kind="Internal").ap()
        decay_rows = nc.dram_tensor("decay_rows", [NT * H, P], F32, kind="Internal").ap()

        alpha_of_tile = alpha_rows.rearrange("(j h) t -> j (h t)", h=H)
        decay_of_tile = decay_rows.rearrange("(j r k) t -> j k r t", k=2, r=4)

        ident = sb("ident", [P, P])
        ones = sb("ones", [P, P])
        upto = sb("upto", [P, P])
        later = sb("later", [P, P])
        shift = sb("shift", [P, P])
        carry = sb("carry", [P, P])
        bandm = sb("bandm", [P, P])
        even = sb("even", [P, 2])
        mhalf = sb("mhalf", [P, NB])
        zeros = sb("zeros", [P, P])
        w_sel_hi = ctx.enter_context(nc.sbuf_tensor("w_sel_hi", [P, 2 * H * N], F32R))
        w_sel_lo = ctx.enter_context(nc.sbuf_tensor("w_sel_lo", [P, 2 * H * N], F32R))
        w_in_hi = ctx.enter_context(nc.sbuf_tensor("w_in_hi", [P, H * PD], F32R))
        w_in_lo = ctx.enter_context(nc.sbuf_tensor("w_in_lo", [P, H * PD], F32R))
        w_scal = sb("w_scal", [P, P])
        w_out = sb("w_out", [P, 4, D])
        w_qkv = sb("w_qkv", [P, 3 * D])
        w_of = sb("w_of", [P, 2, D])
        bias3 = ctx.enter_context(nc.sbuf_tensor("bias3", [3, BIAS], BF16))
        ones3 = ctx.enter_context(nc.sbuf_tensor("ones3", [3, P], BF16))
        rms_c = sb("rms_c", [P, 4])
        dtb = sb("dtb", [P, H])
        alog = sb("alog", [P, H])
        a_pos = sb("a_pos", [P, H])
        alpha_c = sb("alpha_c", [P, 1])
        turned = sb("turned", [P, NT * P])
        xnT = turned[:].rearrange("p (j t) -> p j t", t=P)
        scal = sb("scal", [P, NT, 24])
        packed = sb("packed", [P, NT, SC])
        small = sb("small", [P, 24, NT * H])
        stats4 = sb("stats4", [P, NC, NB, 6])
        mv4 = sb("mv4", [P, NC, NB, 2])
        rstd4 = sb("rstd4", [P, NC, NB])
        shift4 = sb("shift4", [P, NC, NB])
        rows_sb = sb("rows_sb", [P, 2, 2, P])
        fsm = sb("fsm", [P, 4])

        area = sb("area", [P, 9216])
        x_all = area[:, 0:4096].rearrange("p (j d) -> p j d", d=D)
        sel_raw = area[:, 4096:6144].rearrange("p (r d) -> p r d", d=D)
        scal_raw = area[:, 6144:6272]
        in_raw = area[:, 6272:6784].rearrange("p (r d) -> p r d", d=D)
        out_raw = area[:, 6784:7296]
        qkv_raw = area[:, 7296:7680].rearrange("p (r d) -> p r d", d=D)
        ob_raw = area[:, 7680:7808]
        f_raw = area[:, 7808:7936]
        f_abs = area[:, 7936:8064]
        f_lo = area[:, 8064:8192]
        f_tern = area[:, 8192:8320]
        qkv = area[:, 0:3072].rearrange("p (s e) -> p s e", s=NB)
        xres = area[:, 3072:4096].rearrange("p (s d) -> p s d", s=NB)
        xn = area[:, 4096:5120].rearrange("p (s d) -> p s d", s=NB)
        xnT_f = area[:, 5120:6144].rearrange("p (s d) -> p s d", s=NB)
        prod = area[:, 6144:8192].rearrange("p (k e) -> p k e", k=2)
        att = area[:, 8192:9216]
        att_s = att.rearrange("p (s r h) -> p s r h", s=NB, r=NB)
        amax = sb("amax", [P, NB, AH])
        asum = sb("asum", [P, NB, AH])
        rr_f = sb("rr_f", [P, NB])
        temp = small[:, 0:4].rearrange("p a (s d) -> p (a s) d", d=D)
        mean_f = sb("mean_f", [P, NB])
        var_f = sb("var_f", [P, NB])
        eps_ln = sb("eps_ln", [P, NB])
        eps_rms = sb("eps_rms", [P, NB])
        rs_f = sb("rs_f", [P, NB])

        def two(name, cols):
            t = sb(name, [P, 2, cols])
            return [t[:, 0], t[:, 1]]

        xt = two("xt", P)
        xt_hi_both = ctx.enter_context(nc.sbuf_tensor("xt_hi", [P, 2, P], F32R))
        xt_lo_both = ctx.enter_context(nc.sbuf_tensor("xt_lo", [P, 2, P], F32R))
        xt_hi, xt_lo = [xt_hi_both[:, k] for k in range(2)], [xt_lo_both[:, k] for k in range(2)]
        sct = two("sct", SC)
        arow = two("arow", H * P)
        drow = two("drow", 4 * P)
        bc, bs, cc_, cs = ([turned[:, 1024 * m + 512 * k:1024 * m + 512 * k + 512] for k in range(2)] for m in range(4))
        bn, cn = two("bn", HH * N), two("cn", HH * N)
        bT, cT = two("bT", HH * P), two("cT", HH * P)
        band, lmat, mmat = two("band", HH * P), two("lmat", HH * P), two("mmat", HH * P)
        u_nat = two("u_nat", H * PD)
        wu = two("wu", HH * PD)
        yinter = sb("yinter", [P, 2 * P])
        sdec = sb("sdec", [P, HH * PD])
        yT_both = sb("yT", [P, 8 * P])
        yT = [yT_both[:, 0:4 * P], yT_both[:, 4 * P:8 * P]]
        ysq = sb("ysq", [P, 4 * P])
        state = sb("state", [P, NB, H * PD])
        xn_pro = [state[:, 2 * k:2 * k + 2].rearrange("p a (b d) -> p (a b) d", d=D) for k in range(2)]
        bias_row, bias_mid = state[0:1, 4:6].rearrange("o a b -> o (a b)")[:, 0:BIAS_IN], state[0:1, 6:8].rearrange("o a b -> o (a b)")[:, 0:BIAS_IN]
        bias_parts = [yT_both[0:1, 320 * k:320 * k + BIAS_IN // 2].bitcast(BF16) for k in range(3)]
        oraw = sb("oraw", [P, NB, 132])

        ps = ctx.enter_context(nc.psum_tensor("ps", [P, 8, 512], F32))
        BK_B, BK_C, BK_T, BK_G, BK_Y, BK_F0, BK_M, BK_F1 = range(8)
        BK_F = (BK_F0, BK_F1)

        ld_x = [sem(f"ld_x{c}") for c in range(NC)]
        ld_scal, ld_sel, ld_w, ld_small = sem("ld_scal"), sem("ld_sel"), sem("ld_w"), sem("ld_small")
        ld_bias, bias_in, bias_split = sem("ld_bias"), sem("bias_in"), sem("bias_split")
        consts = sem("consts")
        pv, pg, pa, pp = sem("pro_vector"), sem("pro_gpsimd"), sem("pro_scalar"), sem("pro_tensor")
        rows_stored = sem("rows_stored")
        xT_stored, xh_act, xl_dve = sem("xT_stored"), sem("xh_act"), sem("xl_dve")
        packed_done = sem("packed_done")
        xt_in, sct_in = [sem("xt_in0"), sem("xt_in1")], [sem("sct_in0"), sem("sct_in1")]
        arow_in, drow_in = [sem("arow_in0"), sem("arow_in1")], [sem("drow_in0"), sem("drow_in1")]
        b_pe, c_pe, u_pe, tb_pe, tc_pe, g_pe = (sem(n) for n in ("b_pe", "c_pe", "u_pe", "tb_pe", "tc_pe", "g_pe"))
        y_pe, s_pe, o_pe = sem("y_pe"), sem("s_pe"), sem("o_pe")
        bc_dve, l_dve, m_dve, yi_dve, y_dve = (sem(n) for n in ("bc_dve", "l_dve", "m_dve", "yi_dve", "y_dve"))
        sd_dve, s_dve, o_dve = (sem(n) for n in ("sd_dve", "s_dve", "o_dve"))
        bs_act, c_act, bT_act, cT_act, u_act, ysq_act = (sem(n) for n in ("bs_act", "c_act", "bT_act", "cT_act", "u_act", "ysq_act"))
        band_pool, bn_pool, cn_pool, wu_pool = sem("band_pool"), sem("bn_pool"), sem("cn_pool"), sem("wu_pool")
        f_pe, f_q, f_red, f_prod_v, f_prod_g = (sem(n) for n in ("f_pe", "f_q", "f_red", "f_prod_v", "f_prod_g"))
        fx_in, rows_free, f_sq, f_T, f_x, f_exp, f_v, f_g = ([sem(f"{n}{g}") for g in range(2)] for n in (
            "fx_in", "rows_free", "f_sq", "f_T", "f_x", "f_exp", "f_v", "f_g"))

        block = ctx.enter_context(nc.Block())

        def attention_product(eng, c, m, signal):
            eng.wait_ge(f_q, NB * c + NB)
            if m >= 2:
                eng.wait_ge(f_red, 2 * NB * c + m - 1)
            if m < NB:
                eng.tensor_tensor(prod[:, m % 2].rearrange("p (r e) -> p r e", r=NB),
                                  qkv[:, m, 0:D].unsqueeze(1).broadcast_to([P, NB, D]), qkv[:, :, D:2 * D],
                                  ALU.mult).then_inc(signal, 1)
            else:
                eng.wait_ge(f_exp[(m - NB) // 4], c + 1)
                eng.tensor_tensor(prod[:, m % 2].rearrange("p (r h d) -> p r h d", r=NB, d=AD),
                                  att_s[:, m - NB].unsqueeze(3).broadcast_to([P, NB, AH, AD]),
                                  qkv[:, :, 2 * D:3 * D].rearrange("p r (h d) -> p r h d", d=AD),
                                  ALU.mult).then_inc(signal, 1)

        def bank(k):
            return ps[:, k, :]

        def half(g):
            return slice(4 * g, 4 * g + 4)

        bank_of = [7, 6, 7, 6, 7, 5, 6, 7]

        (Z, AZ, EZ, LZ, RZ, DT, ES, LAM, OM, GAM, DEL, V, NLA, ALPHA, BETA, VP, PHI, R1, R2, DEC, SUF, G1, DIF, TMP) = (
            small[:, k, :] for k in range(24))

        def tiles(a):
            return a.rearrange("p (j h) -> p j h", h=H)

        @block.sync
        def _(sp):
            sp.dma_start(scal_raw, sel_w[2 * H * N + 3 * H - P:2 * H * N + 3 * H, :]).then_inc(ld_scal, 16)
            for c in range(NC):
                sp.dma_start(x_all[:, NB * c:NB * (c + 1), :], x_rows[c]).then_inc(ld_x[c], 16)
            def spread(v, n):
                return v.unsqueeze(0).broadcast_to([P, n])
            smalls = [(dtb[:], spread(dt_bias, H)), (alog[:], spread(a_log, H)),
                      (alpha_c[:], spread(f_alpha, 1))]
            for dst, src in smalls:
                sp.dma_start(dst, src).then_inc(ld_small, 16)
            with nc.allow_non_contiguous_dma("four columns of weights"):
                sp.dma_start(rms_c[:], rms_w.rearrange("(j p) -> p j", p=P)).then_inc(ld_small, 16)
            sp.dma_start(bias_row[:, 0:3 * D], qkv_b.unsqueeze(0)).then_inc(ld_bias, 16)
            sp.dma_start(bias_row[:, 3 * D:4 * D], f_b.unsqueeze(0)).then_inc(ld_bias, 16)
            sp.dma_start(bias_row[:, 4 * D:5 * D], ob_b.unsqueeze(0)).then_inc(ld_bias, 16)
            for j in range(2):
                sp.dma_start(sel_raw[N // 2 * j:N // 2 * (j + 1)],
                             sel_w[0:2 * H * N, :].rearrange("(r p j) d -> j p r d", j=2, p=N // 2)[j]).then_inc(ld_sel, 16)
            for dst, src in [(in_raw, in_w.rearrange("(r p) d -> p r d", p=P)), (out_raw, out_w),
                             (qkv_raw, qkv_w.rearrange("(r p) d -> p r d", p=P)), (ob_raw, ob_w), (f_raw, f_w)]:
                sp.dma_start(dst, src).then_inc(ld_w, 16)

            for c in range(NC):
                sp.wait_ge(pa, PA["T", c, 1])
                sp.dma_start(xT_rows[NB * c:NB * (c + 1)].rearrange("j d t -> d j t"), xnT[:, NB * c:NB * (c + 1), :]).then_inc(xT_stored, 16)

            sp.wait_ge(bias_split, 5)
            for k, part in enumerate(bias_parts):
                sp.dma_start(bias3[k:k + 1, 0:3 * D], part[:, 0:3 * D]).then_inc(bias_in, 16)
                for at, src in ((BIAS_F, 3 * D), (BIAS_O, 4 * D)):
                    sp.dma_start(bias3[k:k + 1, at:at + 4 * D].rearrange("o (r d) -> o r d", d=D),
                                 part[:, src:src + D].unsqueeze(1).broadcast_to([1, 4, D])).then_inc(bias_in, 16)

            sp.wait_ge(pa, PA["rows"])
            for k in range(2):
                sp.dma_start(alpha_rows[P * k:P * (k + 1), :], rows_sb[:, 0, k, :]).then_inc(rows_stored, 16)
                sp.dma_start(decay_rows[P * k:P * (k + 1), :], rows_sb[:, 1, k, :]).then_inc(rows_stored, 16)

            def tile_loads(c, b):
                i2 = b % 2
                tile = NB * c + b
                after(sp, xl_dve, tile - 1)
                sp.dma_start(xt[i2], xT_rows[tile]).then_inc(xt_in[i2], 16)
                after(sp, l_dve, 2 * (tile - 2) + 2)
                sp.dma_start(arow[i2], alpha_of_tile[tile].unsqueeze(0)
                             .broadcast_to([P, H * P])).then_inc(arow_in[i2], 16)
                after(sp, y_dve, 2 * (tile - 2) + 2)
                if has_state(c, 2 * (b - 2)):
                    after(sp, s_dve, 2 * (tile - 2) + 2)
                sp.dma_start(sct[i2], packed[:, tile, :]).then_inc(sct_in[i2], 16)
                rows = decay_of_tile[tile]
                for k in range(2):
                    sp.dma_start(drow[i2][64 * k:64 * k + 64].rearrange("p (r t) -> p r t", t=P),
                                 rows[k].unsqueeze(0).broadcast_to([64, 4, P])).then_inc(drow_in[i2], 16)

            sp.wait_ge(pv, PV["packed"])
            sp.wait_ge(pa, PA["packed"])
            sp.wait_ge(xT_stored, 16 * NC)
            sp.wait_ge(rows_stored, 64)
            for b in range(NB):
                tile_loads(0, b)
            with sp.Fori(1, NC - 1) as c:
                for b in range(NB):
                    tile_loads(c, b)
            for b in range(NB):
                tile_loads(NC - 1, b)

        def f_bank(use):
            return bank(BK_F[USES.index(use) % 2])

        @block.gpsimd
        def _(pool):
            def select(t, src, base, mult, step, op, fill):
                return pool.affine_select(out=t, in_=src, compare_op=op, fill=fill, base=base,
                                          pattern=[[step, P]], channel_multiplier=mult)
            pool.memset(zeros[:], 0.0)
            pool.memset(ones[:], 1.0)
            pool.memset(eps_ln[:], D * EPS_LN)
            pool.memset(eps_rms[:], H * PD * EPS_RMS)
            pool.memset(mhalf[:], -0.5).then_inc(consts, 1)
            pool.wait_ge(consts, 1)
            select(ident[:], zeros[:], 0, 1, -1, ALU.not_equal, 1.0).then_inc(consts, 1)
            select(upto[:], ones[:], 0, -1, 1, ALU.is_ge, 0.0)
            select(later[:], ones[:], 0, 1, -1, ALU.is_gt, 0.0)
            select(shift[:], zeros[:], -1, 1, -1, ALU.not_equal, 1.0)
            select(carry[:], zeros[:], P - 1, P, -1, ALU.not_equal, 1.0)
            pool.wait_ge(consts, 2)
            select(bandm[:], ident[:], 1, 1, -1, ALU.not_equal, 1.0).then_inc(consts, 1)
            for c in range(NC):
                pool.wait_ge(pv, PV["aggr", c])
                pool.tensor_scalar(rstd4[:, c], mv4[:, c, :, 1], 1.0, EPS_LN, ALU.mult, ALU.add).then_inc(pg, 1)
                pool.tensor_scalar(shift4[:, c], mv4[:, c, :, 0], -1.0, None, ALU.mult).then_inc(pg, 1)
                pool.wait_ge(pg, 4 * c + 1)
                pool.tensor_tensor(rstd4[:, c], rstd4[:, c], mhalf[:], ALU.pow).then_inc(pg, 1)
                pool.wait_ge(pg, 4 * c + 3)
                pool.tensor_tensor(shift4[:, c], shift4[:, c], rstd4[:, c], ALU.mult).then_inc(pg, 1)

            pool.memset(ones3[:], 1.0)
            pool.wait_ge(ld_bias, 48)
            pool.tensor_copy(bias_parts[0], bias_row).then_inc(bias_split, 1)
            pool.wait_ge(bias_split, 1)
            pool.tensor_tensor(bias_mid, bias_row, bias_parts[0], ALU.subtract).then_inc(bias_split, 1)
            pool.wait_ge(bias_split, 2)
            pool.tensor_copy(bias_parts[1], bias_mid).then_inc(bias_split, 1)
            pool.wait_ge(bias_split, 3)
            pool.tensor_tensor(bias_row, bias_mid, bias_parts[1], ALU.subtract).then_inc(bias_split, 1)
            pool.wait_ge(bias_split, 4)
            pool.tensor_copy(bias_parts[2], bias_row).then_inc(bias_split, 1)

            pool.wait_ge(pp, PP["T", NC - 1, 1])
            pool.wait_ge(bias_split, 5)
            for g in range(2):
                pool.memset(state[:, 4 * g:4 * g + 4], 0.0).then_inc(rows_free[g], 16)

            def rotate(dst, by_cos, by_sin):
                out, zc, zs = (a.rearrange("p (h j n) -> p j h n", h=HH, j=2) for a in (dst, by_cos, by_sin))
                pool.tensor_tensor(out[:, 0], zc[:, 0], zs[:, 1], ALU.subtract)
                return pool.tensor_tensor(out[:, 1], zc[:, 1], zs[:, 0], ALU.add)

            def add_b(c, k):
                h, n = k % 2, UNITS * c + k
                pool.wait_ge(bs_act, n + 1)
                after(pool, tb_pe, n - 1)
                if has_state(c, k - 2):
                    after(pool, s_pe, n - 1)
                rotate(bn[h], bc[h], bs[h]).then_inc(bn_pool, 1)

            def band_of(c, k):
                h, i2, n = k % 2, (k // 2) % 2, UNITS * c + k
                pool.wait_ge(sct_in[i2], 16 * (NB // 2 * c + k // 4 + 1))
                after(pool, l_dve, n - 1)
                mask = bandm[:].rearrange("p (a k) -> p a k", k=2).unsqueeze(1).broadcast_to([P, HH, P // 2, 2])
                vals = sct[i2][:, BAND + 2 * HH * h:BAND + 2 * HH * (h + 1)].rearrange("p (h k) -> p h k", k=2)
                pool.tensor_tensor(band[h].rearrange("p (h a k) -> p h a k", h=HH, k=2), mask,
                                  vals.unsqueeze(2).broadcast_to([P, HH, P // 2, 2]), ALU.mult).then_inc(band_pool, 1)

            def add_c(c, k):
                h, n = k % 2, UNITS * c + k
                pool.wait_ge(c_act, n + 1)
                after(pool, tc_pe, n - 1)
                rotate(cn[h], cc_[h], cs[h]).then_inc(cn_pool, 1)

            def weigh_u(c, k):
                h, i2, n = k % 2, (k // 2) % 2, UNITS * c + k
                pool.wait_ge(u_act, NB * c + k // 2 + 1)
                after(pool, s_pe, n - 1)
                w = sct[i2][:, SW + HH * h:SW + HH * h + HH].unsqueeze(2).broadcast_to([P, HH, PD])
                pool.tensor_tensor(wu[h].rearrange("p (h q) -> p h q", q=PD),
                                   u_nat[i2][:, HH * PD * h:HH * PD * (h + 1)].rearrange("p (h q) -> p h q", q=PD),
                                   w, ALU.mult).then_inc(wu_pool, 1)

            def rms_root(c, g):
                rr = rr_f[:, half(g)]
                pool.wait_ge(o_dve, NB * c + 4 * g + 4)
                pool.tensor_tensor(rr, oraw[:, half(g), D], eps_rms[:, half(g)], ALU.add).then_inc(f_g[g], 1)
                pool.wait_ge(f_g[g], g_step("ms", c))
                pool.tensor_tensor(rr, rr, mhalf[:, half(g)], ALU.pow).then_inc(f_g[g], 1)

            def ln_root(c, k, g):
                rs = rs_f[:, half(g)]
                pool.wait_ge(f_v[g], v_step(f"var{k}", c))
                pool.tensor_tensor(rs, var_f[:, half(g)], eps_ln[:, half(g)], ALU.add).then_inc(f_g[g], 1)
                pool.wait_ge(f_g[g], g_step(f"ve{k}", c))
                pool.tensor_tensor(rs, rs, mhalf[:, half(g)], ALU.pow).then_inc(f_g[g], 1)

            def product(c, m):
                attention_product(pool, c, m, f_prod_g)

            pieces = []
            for g in range(2):
                place(pieces, f"rr:{g}", lambda c, g=g: rms_root(c, g))
                for k in range(3):
                    place(pieces, f"rs{k}:{g}", lambda c, k=k, g=g: ln_root(c, k, g))
            for m in POOL_PRODUCTS:
                place(pieces, f"prod{m}", lambda c, m=m: product(c, m))

            def step(c, k, pieces, first=False, last=False):
                nxt = not (last and k == UNITS - 1)
                if k % 2 == 0:
                    at_step(pieces, c, k, 0)
                    if not last:
                        weigh_u(c, k)
                    band_of(c, k + 1)
                    at_step(pieces, c, k, 1)
                    add_b(c, k + 1)
                    at_step(pieces, c, k, 2)
                    add_c(c, k + 1)
                else:
                    if nxt:
                        band_of(c, k + 1)
                    at_step(pieces, c, k, 0)
                    if not last:
                        weigh_u(c, k)
                    if nxt:
                        add_b(c, k + 1)
                    at_step(pieces, c, k, 1)
                    if nxt:
                        add_c(c, k + 1)
                    at_step(pieces, c, k, 2)

            band_of(0, 0)
            add_b(0, 0)
            add_c(0, 0)
            run_chunks(pool, step, pieces)

        @block.scalar
        def _(act):
            def evac(dst, src):
                return act.activation(dst, src, ACT.Copy)

            count = 0

            def tick(ins, name=None):
                nonlocal count
                count += 1
                ins.then_inc(pa, 1)
                if name is not None:
                    assert PA[name] == count, (name, count)

            act.wait_ge(pp, PP["scal_w"])
            tick(evac(w_scal[:], bank(0)[:, 0:P]), "scal_w")
            for c in range(NC + 1):
                if c < NC:
                    act.wait_ge(pg, 4 * c + 4)
                    after(act, pp, PP["T", c - 2, 1] if c >= 2 else 0)
                    for b in range(NB):
                        last = act.activation(xn_pro[c % 2][:, b], x_all[:, NB * c + b, :], ACT.Identity,
                                              bias=shift4[:, c, b:b + 1], scale=rstd4[:, c, b:b + 1])
                    tick(last, ("xn", c))
                if c >= 1:
                    for g in range(2):
                        act.wait_ge(pp, PP["T", c - 1, g])
                        at = NB * (c - 1) + 4 * g
                        tick(evac(xnT[:, at:at + 4, :].rearrange("p j t -> p (j t)"), bank(1 + g)), ("T", c - 1, g))
            assert PA["xnT"] == count
            act.wait_ge(ld_w, 80)
            tick(act.activation(f_abs, f_raw, ACT.Abs, accum_out=fsm[:, 0:1]), "abs")
            act.wait_ge(ld_small, 64)
            tick(act.activation(a_pos[:], alog[:], ACT.Exp), "a")
            for g in range(2):
                act.wait_ge(pp, PP["W", g])
                tick(evac(w_sel_hi[:, 512 * g:512 * g + 512], bank(bank_of[g])), ("W", g))
            act.wait_ge(pv, PV["az"])
            tick(act.activation(EZ, AZ, ACT.Exp, scale=-1.0), "ez")
            act.wait_ge(pv, PV["scal"])
            tick(act.activation(tiles(ES), scal[:, :, 8:16], ACT.Exp, scale=-1.0), "es")
            act.wait_ge(pa, PA["ez"])
            tick(act.activation(LZ, EZ, ACT.Ln, bias=1.0), "lz")
            act.wait_ge(pv, PV["nla"])
            tick(act.activation(ALPHA, NLA, ACT.Exp), "alpha")
            act.wait_ge(pp, PP["cums"])
            tick(act.activation(DEC, bank(1)[:, 0:NT * H], ACT.Exp), "dec")
            tick(act.activation(SUF, bank(2)[:, 0:NT * H], ACT.Exp), "suf")
            tick(act.activation(packed[:, :, CD:CD + H], tiles(bank(3)[:, 0:NT * H]), ACT.Exp), "cd")
            act.wait_ge(pp, PP["W", 2])
            tick(evac(w_sel_hi[:, 1024:1536], bank(bank_of[2])), ("W", 2))
            act.wait_ge(pp, PP["rows"])
            tick(evac(rows_sb[:, 0, :, 1:P], bank(4)[:, 0:2 * P].rearrange("p (k t) -> p k t", k=2)[:, :, 1:P]), "rows_a")
            tick(evac(rows_sb[:, 1, :, :], bank(4)[:, 2 * P:4 * P].rearrange("p (k t) -> p k t", k=2)), "rows")
            act.wait_ge(pv, PV["red"])
            tick(act.activation(packed[:, :, SIN:SIN + H], tiles(R1), ACT.Sin), "sin")
            tick(act.activation(packed[:, :, COS:COS + H], tiles(R2), ACT.Sin), "packed")
            act.wait_ge(pp, PP["W", 3])
            tick(evac(w_sel_hi[:, 1536:2048], bank(bank_of[3])), ("W", 3))
            act.wait_ge(pp, PP["W", 4])
            tick(evac(w_in_hi[:], bank(bank_of[4])), ("W", 4))
            act.wait_ge(pp, PP["W", 6])
            tick(evac(w_qkv[:], bank(bank_of[6])[:, 0:3 * D]), ("W", 6))
            act.wait_ge(pp, PP["W", 7])
            tick(evac(w_of[:].rearrange("p k d -> p (k d)"), bank(bank_of[7])[:, 0:2 * D]), ("W", 7))

            def x_high(c, b):
                act.wait_ge(xt_in[b % 2], 16 * (NB // 2 * c + b // 2 + 1))
                after(act, c_pe, 2 * (NB * c + b) - 2)
                evac(xt_hi[b % 2], xt[b % 2]).then_inc(xh_act, 1)

            def u_out(c, k):
                i2, tile = (k // 2) % 2, NB * c + k // 2
                act.wait_ge(u_pe, tile + 1)
                after(act, y_pe, 2 * (tile - 2) + 2)
                if has_state(c, k - 4):
                    after(act, wu_pool, 2 * (tile - 2) + 2)
                evac(u_nat[i2], bank(BK_M)).then_inc(u_act, 1)

            def b_sin(c, k):
                h, i2, n = k % 2, (k // 2) % 2, UNITS * c + k
                act.wait_ge(bc_dve, n + 1)
                act.wait_ge(sct_in[i2], 16 * (NB // 2 * c + k // 4 + 1))
                after(act, bn_pool, n - 1)
                for q in range(HH):
                    last = act.activation(bs[h][:, N * q:N * q + N], bank(BK_B)[:, N * q:N * q + N], ACT.Copy,
                                          scale=sct[i2][:, SIN + HH * h + q:SIN + HH * h + q + 1])
                last.then_inc(bs_act, 1)

            def c_turn(c, k, part):
                h, i2, n = k % 2, (k // 2) % 2, UNITS * c + k
                if part == 0:
                    act.wait_ge(c_pe, n + 1)
                    act.wait_ge(sct_in[i2], 16 * (NB // 2 * c + k // 4 + 1))
                    after(act, cn_pool, n - 1)
                for q in (2 * part, 2 * part + 1):
                    for dst, at in ((cc_, COS), (cs, SIN)):
                        last = act.activation(dst[h][:, N * q:N * q + N], bank(BK_C)[:, N * q:N * q + N], ACT.Copy,
                                              scale=sct[i2][:, at + HH * h + q:at + HH * h + q + 1])
                if part == 1:
                    last.then_inc(c_act, 1)

            def bT_out(c, k):
                h, n = k % 2, UNITS * c + k
                act.wait_ge(tb_pe, n + 1)
                after(act, g_pe, n - 1)
                evac(bT[h], bank(BK_T)).then_inc(bT_act, 1)

            def cT_out(c, k):
                h, n = k % 2, UNITS * c + k
                act.wait_ge(tc_pe, n + 1)
                after(act, y_pe, n - 1)
                evac(cT[h], bank(BK_T)).then_inc(cT_act, 1)

            def y_square(c, b):
                tile = NB * c + b
                act.wait_ge(y_dve, 2 * tile + 2)
                after(act, o_pe, tile)
                act.activation(ysq[:], yT[b % 2], ACT.Square).then_inc(ysq_act, 1)

            def f_T_out(c, t):
                act.wait_ge(f_pe, use_done(("T", t), c))
                evac(xnT_f[:, half(t % 2), :].rearrange("p j t -> p (j t)"), f_bank(("T", t))).then_inc(f_T[t % 2], 1)

            def f_qkv_out(c, s):
                act.wait_ge(f_pe, use_done(("Q", s), c))
                evac(qkv[:, s, :], f_bank(("Q", s))[:, 0:3 * D]).then_inc(f_q, 1)

            def f_softmax_exp(c, g):
                act.wait_ge(f_v[g], v_step("sub", c))
                rows = att[:, 4 * P * g:4 * P * (g + 1)]
                act.activation(rows, rows, ACT.Exp, scale=float(AD) ** -0.5).then_inc(f_exp[g], 1)

            pieces = []
            for t in range(8):
                place(pieces, f"T{t}", lambda c, t=t: f_T_out(c, t))
            for q in range(NB):
                place(pieces, f"qadd{q}", lambda c, q=q: f_qkv_out(c, q))

            def f_square(c, k, g):
                act.wait_ge(f_v[g], v_step(f"xc{k}", c))
                act.activation(temp[:, half(g)], xn[:, half(g)], ACT.Square).then_inc(f_sq[g], 1)

            def f_load(c, g):
                act.wait_ge(rows_free[g], 16 * c + 16)
                act.dma_start(xres[:, half(g)], x_rows[c][:, half(g)]).then_inc(fx_in[g], 16)

            def f_store(c, g):
                act.wait_ge(f_x[g], x_step("ffn1", c))
                act.dma_start(out_rows[c][:, half(g)], xres[:, half(g)]).then_inc(rows_free[g], 16)

            for g in range(2):
                for k in range(3):
                    place(pieces, f"sq{k}:{g}", lambda c, k=k, g=g: f_square(c, k, g))
                place(pieces, f"exp:{g}", lambda c, g=g: f_softmax_exp(c, g))
                place(pieces, f"load:{g}", lambda c, g=g: f_load(c, g))
                place(pieces, f"store:{g}", lambda c, g=g: f_store(c, g))

            def step(c, k, pieces, first=False, last=False):
                nxt = not (last and k == UNITS - 1)
                if k % 2 == 0:
                    bT_out(c, k)
                    if not (last and k == UNITS - 2):
                        x_high(c, k // 2 + 1)
                    at_step(pieces, c, k, 0)
                    b_sin(c, k + 1)
                    cT_out(c, k)
                    c_turn(c, k + 1, 0)
                    c_turn(c, k + 1, 1)
                    at_step(pieces, c, k, 1)
                    at_step(pieces, c, k, 2)
                    if not (first and k == 0):
                        y_square(c if k > 1 else c - 1, (k // 2 - 1) % NB)
                else:
                    at_step(pieces, c, k, 0)
                    bT_out(c, k)
                    if nxt:
                        u_out(c, k + 1)
                        b_sin(c, k + 1)
                    at_step(pieces, c, k, 1)
                    cT_out(c, k)
                    if nxt:
                        c_turn(c, k + 1, 0)
                        c_turn(c, k + 1, 1)
                    at_step(pieces, c, k, 2)

            def finish(c):
                y_square(c, NB - 1)

            x_high(0, 0)
            u_out(0, 0)
            b_sin(0, 0)
            c_turn(0, 0, 0)
            c_turn(0, 0, 1)
            run_chunks(act, step, pieces, finish)
            for g in range(2):
                act.wait_ge(rows_free[g], 16 * NC + 16)

        @block.vector
        def _(dve):
            count = 0

            def tick(ins, name=None, wait=False):
                nonlocal count
                count += 1
                ins.then_inc(pv, 1)
                if name is not None:
                    assert PV[name] == count, (name, count)
                if wait:
                    dve.wait_ge(pv, count)

            dve.memset(rows_sb[:, 0, :, 0:1], 0.0)
            dve.wait_ge(consts, 3)
            tick(dve.tensor_reduce(even[:], ident[:].rearrange("p (a k) -> p k a", k=2), AX.X, ALU.add), "even")

            for c in range(NC):
                dve.wait_ge(ld_x[c], 16)
                for b in range(NB):
                    last = dve.bn_stats(stats4[:, c, b], x_all[:, NB * c + b, :])
                tick(last, ("bn", c), wait=True)
                for b in range(NB):
                    last = dve.bn_aggr(mv4[:, c, b], stats4[:, c, b])
                tick(last, ("aggr", c))
            for c in range(NC):
                for g in range(2):
                    dve.wait_ge(pp, PP["scal", c, g])
                    tick(dve.tensor_copy(scal[:, NB * c + 4 * g:NB * c + 4 * g + 4, :],
                                         bank(3 + g).rearrange("p (j e) -> p j e", e=P)[:, :, P - 24:P]), ("scal", c, g))
            dve.wait_ge(ld_small, 64)
            dve.wait_ge(pv, PV["scal"])
            per_head = dtb[:].unsqueeze(1).broadcast_to([P, NT, H])
            tick(dve.tensor_tensor(tiles(Z), scal[:, :, 0:8], per_head, ALU.add), None, True)
            tick(dve.scalar_tensor_tensor(AZ, Z, -1.0, Z, ALU.mult, ALU.max), "az")
            tick(dve.tensor_scalar(RZ, Z, 0.0, None, ALU.max))
            W = NB * H
            tick(dve.memset(VP[:, 0:W], 0.0))
            dve.wait_ge(pa, PA["es"])
            tick(dve.tensor_scalar(TMP, ES, 1.0, None, ALU.add), None, True)
            tick(dve.reciprocal(LAM, TMP), None, True)
            tick(dve.tensor_scalar(OM, LAM, -1.0, 1.0, ALU.mult, ALU.add))
            dve.wait_ge(pa, PA["lz"])
            dve.wait_ge(pv, count)
            tick(dve.tensor_tensor(DT, RZ, LZ, ALU.add), "dt", True)
            dve.wait_ge(pa, PA["a"])
            per_head = a_pos[:].unsqueeze(1).broadcast_to([P, NT, H])
            tick(dve.scalar_tensor_tensor(tiles(NLA), tiles(DT), -1.0, per_head, ALU.mult, ALU.mult), "nla")
            tick(dve.tensor_tensor(tiles(V), tiles(DT), scal[:, :, 16:24], ALU.mult), "v", True)
            for c in range(1, NC):
                tick(dve.tensor_tensor(VP[:, W * c:W * (c + 1)], VP[:, W * (c - 1):W * c], V[:, W * (c - 1):W * c], ALU.add),
                     "vp" if c == NC - 1 else None, True)

            def low_part(g):
                dve.wait_ge(pa, PA["W", g])
                hi, lo = (w_sel_hi[:, 512 * g:512 * g + 512], w_sel_lo[:, 512 * g:512 * g + 512]) if g < 4 else (w_in_hi[:], w_in_lo[:])
                tick(dve.tensor_tensor(lo, bank(bank_of[g]), hi.bitcast(F32), ALU.subtract), ("lo", g))

            low_part(0)
            tick(dve.tensor_tensor(GAM, LAM, DT, ALU.mult))
            tick(dve.tensor_tensor(DEL, OM, DT, ALU.mult), None, True)
            dve.wait_ge(pa, PA["alpha"])
            tick(dve.tensor_tensor(BETA, DEL, ALPHA, ALU.mult), "beta")
            dve.wait_ge(pp, PP["phi"])
            c1, c2, c3 = pi_parts()
            tick(dve.tensor_scalar(R1, bank(0)[:, 0:NT * H], 1.0 / TWO_PI, ROUND, ALU.mult, ALU.add), None, True)
            tick(dve.tensor_scalar(R1, R1, -ROUND, None, ALU.add), None, True)
            tick(dve.scalar_tensor_tensor(PHI, R1, -c1, bank(0)[:, 0:NT * H], ALU.mult, ALU.add), None, True)
            tick(dve.scalar_tensor_tensor(R2, R1, -c2, PHI, ALU.mult, ALU.add), None, True)
            tick(dve.scalar_tensor_tensor(PHI, R1, -c3, R2, ALU.mult, ALU.add), None, True)
            pi32 = float(np.nextafter(np.float32(np.pi), np.float32(0)))
            tick(dve.tensor_scalar(R1, PHI, pi32, -pi32, ALU.min, ALU.max), None, True)
            tick(dve.scalar_tensor_tensor(R2, R1, -1.0, R1, ALU.mult, ALU.max), None, True)
            tick(dve.tensor_scalar(R2, R2, -1.0, float(np.pi / 2), ALU.mult, ALU.add), "red")
            low_part(1)
            low_part(2)
            dve.wait_ge(pp, PP["shifts"])
            tick(dve.tensor_tensor(G1, GAM, bank(5)[:, 0:NT * H], ALU.add))
            tick(dve.tensor_copy(TMP, bank(5)[:, NT * H:2 * NT * H]), None, True)
            dve.wait_ge(pa, PA["suf"])
            tick(dve.tensor_tensor(packed[:, :, SW:SW + H], tiles(G1), tiles(SUF), ALU.mult))
            tick(dve.tensor_tensor(DIF, GAM, TMP, ALU.subtract), None, True)
            pairs = packed[:, :, BAND:BAND + 2 * H].rearrange("p j (h k) -> p j h k", k=2)
            for k in range(2):
                tick(dve.scalar_tensor_tensor(pairs[:, :, :, k], tiles(DIF), even[:, k:k + 1], tiles(TMP), ALU.mult, ALU.add),
                     "packed" if k == 1 else None)
            dve.wait_ge(pa, PA["cd"])
            tick(dve.tensor_scalar(fsm[:, 1:2], bank(3)[:, NT * H:NT * H + 1], 1.0 / (D * D), TERNARY, ALU.mult, ALU.mult), None, True)
            tick(dve.tensor_scalar(fsm[:, 2:3], fsm[:, 1:2], -1.0, None, ALU.mult))
            low_part(3)
            low_part(4)
            dve.wait_ge(pv, PV["lo", 3] - 1)
            tick(dve.tensor_scalar(f_abs, f_raw, fsm[:, 1:2], alpha_c[:, 0:1], ALU.is_gt, ALU.mult))
            tick(dve.tensor_scalar(f_lo, f_raw, fsm[:, 2:3], alpha_c[:, 0:1], ALU.is_lt, ALU.mult), None, True)
            tick(dve.tensor_tensor(f_tern, f_abs, f_lo, ALU.subtract), "tern")
            dve.wait_ge(pp, PP["W", 5])
            for j in range(4):
                last = dve.tensor_scalar(w_out[:, j], bank(bank_of[5])[:, P * j:P * j + P], rms_c[:, j:j + 1], None, ALU.mult)
            tick(last, "w_out")
            for g in range(2):
                dve.wait_ge(rows_free[g], 16)

            def b_cos(c, k):
                h, i2, n = k % 2, (k // 2) % 2, UNITS * c + k
                dve.wait_ge(b_pe, n + 1)
                dve.wait_ge(sct_in[i2], 16 * (NB // 2 * c + k // 4 + 1))
                after(dve, bn_pool, n - 1)
                cosv = sct[i2][:, COS + HH * h:COS + HH * h + HH].unsqueeze(2).broadcast_to([P, HH, N])
                dve.tensor_tensor(bc[h].rearrange("p (h n) -> p h n", n=N), bank(BK_B).rearrange("p (h n) -> p h n", n=N),
                                  cosv, ALU.mult).then_inc(bc_dve, 1)

            def x_low(c, b):
                dve.wait_ge(xh_act, NB * c + b + 1)
                dve.tensor_tensor(xt_lo[b % 2], xt[b % 2], xt_hi[b % 2].bitcast(F32), ALU.subtract).then_inc(xl_dve, 1)

            def scan(c, k):
                h, i2, n = k % 2, (k // 2) % 2, UNITS * c + k
                dve.wait_ge(arow_in[i2], 16 * (NB // 2 * c + k // 4 + 1))
                dve.wait_ge(band_pool, n + 1)
                dve.tensor_tensor_scan(lmat[h], arow[i2][:, HH * P * h:HH * P * (h + 1)], band[h], 0.0,
                                       ALU.mult, ALU.add).then_inc(l_dve, 1)

            def weigh_scores(c, k):
                h, n = k % 2, UNITS * c + k
                dve.wait_ge(g_pe, n + 1)
                dve.wait_ge(l_dve, n + 1)
                after(dve, y_pe, n - 1)
                dve.tensor_tensor(mmat[h], bank(BK_G), lmat[h], ALU.mult).then_inc(m_dve, 1)

            def y_of(c, k, inter):
                h, i2, n = k % 2, (k // 2) % 2, UNITS * c + k
                tile = NB * c + k // 2
                dve.wait_ge(y_pe, n + 1)
                after(dve, o_pe, tile - 1)
                dst = yT[i2][:, 2 * P * h:2 * P * (h + 1)]
                if inter:
                    dve.wait_ge(drow_in[i2], 32 * (NB // 2 * c + k // 4 + 1))
                    dve.tensor_tensor(yinter[:], bank(BK_Y)[:, 2 * P:4 * P], drow[i2][:, 2 * P * h:2 * P * (h + 1)],
                                      ALU.mult).then_inc(yi_dve, 1)
                    dve.wait_ge(yi_dve, n - UNITS + 2)
                    dve.tensor_tensor(dst, bank(BK_Y)[:, 0:2 * P], yinter[:], ALU.add).then_inc(y_dve, 1)
                else:
                    dve.tensor_copy(dst, bank(BK_Y)[:, 0:2 * P]).then_inc(y_dve, 1)

            def state_of(c, k):
                h, i2, n = k % 2, (k // 2) % 2, UNITS * c + k
                b = k // 2
                st = state[:, b, HH * PD * h:HH * PD * (h + 1)].rearrange("p (h q) -> p h q", q=PD)
                dec = sct[i2][:, CD + HH * h:CD + HH * h + HH].unsqueeze(2).broadcast_to([P, HH, PD])
                dve.tensor_tensor(sdec[:].rearrange("p (h q) -> p h q", q=PD), st, dec, ALU.mult).then_inc(sd_dve, 1)
                dve.wait_ge(s_pe, n + 1)
                dve.wait_ge(y_pe, n + 1)
                dve.wait_ge(sd_dve, n + 1)
                own = bank(BK_G).rearrange("p (h q) -> p h q", q=N)[:, :, 0:PD]
                dve.tensor_tensor(st, sdec[:].rearrange("p (h q) -> p h q", q=PD), own, ALU.add).then_inc(s_dve, 1)

            def o_out(c, b):
                dve.wait_ge(o_pe, NB * c + b + 1)
                dve.tensor_copy(oraw[:, b, 0:D + 1], bank(BK_M)[:, 0:D + 1]).then_inc(o_dve, 1)

            def f_x1(c, g):
                dve.wait_ge(f_g[g], g_step("rr", c))
                dve.wait_ge(fx_in[g], 16 * c + 16)
                dve.scalar_tensor_tensor(temp[:, half(g)], oraw[:, half(g), 0:D], float(np.sqrt(H * PD)),
                                         rr_f[:, half(g)].unsqueeze(2).broadcast_to([P, 4, D]),
                                         ALU.mult, ALU.mult).then_inc(f_v[g], 1)
                dve.wait_ge(f_v[g], v_step("scaled", c))
                dve.tensor_tensor(xres[:, half(g)], xres[:, half(g)], temp[:, half(g)], ALU.add).then_inc(f_x[g], 1)

            def f_mean(c, k, g):
                dve.wait_ge(f_x[g], x_step(XSTEPS[k], c))
                dve.tensor_reduce(mean_f[:, half(g)], xres[:, half(g)], AX.X, ALU.add).then_inc(f_v[g], 1)
                dve.wait_ge(f_v[g], v_step(f"mean{k}", c))
                dve.scalar_tensor_tensor(xn[:, half(g)], mean_f[:, half(g)].unsqueeze(2).broadcast_to([P, 4, D]), -1.0 / D,
                                         xres[:, half(g)], ALU.mult, ALU.add).then_inc(f_v[g], 1)

            def f_var(c, k, g):
                dve.wait_ge(f_sq[g], 3 * c + k + 1)
                dve.tensor_reduce(var_f[:, half(g)], temp[:, half(g)], AX.X, ALU.add).then_inc(f_v[g], 1)

            def f_norm(c, k, g):
                dve.wait_ge(f_g[g], g_step(f"rs{k}", c))
                dve.scalar_tensor_tensor(xn[:, half(g)], xn[:, half(g)], float(np.sqrt(D)),
                                         rs_f[:, half(g)].unsqueeze(2).broadcast_to([P, 4, D]),
                                         ALU.mult, ALU.mult).then_inc(f_v[g], 1)

            def f_add(c, what):
                g = what[1] % 2
                dve.wait_ge(f_pe, use_done(what, c))
                rows = xres[:, half(g), :].rearrange("p j d -> p (j d)")
                dve.tensor_tensor(rows, f_bank(what), rows, ALU.add).then_inc(f_x[g], 1)

            def f_product(c, m):
                attention_product(dve, c, m, f_prod_v)

            def f_reduce(c, m):
                if m in POOL_PRODUCTS:
                    dve.wait_ge(f_prod_g, len(POOL_PRODUCTS) * c + POOL_PRODUCTS.index(m) + 1)
                else:
                    mine = [q for q in range(2 * NB) if q not in POOL_PRODUCTS]
                    dve.wait_ge(f_prod_v, len(mine) * c + mine.index(m) + 1)
                if m < NB:
                    dve.tensor_reduce(att[:, P * m:P * (m + 1)], prod[:, m % 2].rearrange("p (e d) -> p e d", d=AD),
                                      AX.X, ALU.add).then_inc(f_red, 1)
                else:
                    dve.tensor_reduce(xn[:, m - NB, :], prod[:, m % 2].rearrange("p (r e) -> p e r", r=NB),
                                      AX.X, ALU.add).then_inc(f_red, 1)

            def f_softmax(c, g):
                rows = att_s[:, half(g)]
                dve.wait_ge(f_red, 2 * NB * c + 4 * g + 4)
                dve.tensor_reduce(amax[:, half(g)], rows.rearrange("p s r h -> p s h r"), AX.X, ALU.max).then_inc(f_v[g], 1)
                dve.wait_ge(f_v[g], v_step("max", c))
                dve.tensor_tensor(rows, rows, amax[:, half(g)].unsqueeze(2).broadcast_to([P, 4, NB, AH]), ALU.subtract).then_inc(f_v[g], 1)

            def f_norms(c, g):
                dve.wait_ge(f_exp[g], c + 1)
                dve.tensor_reduce(asum[:, half(g)], att_s[:, half(g)].rearrange("p s r h -> p s h r"), AX.X, ALU.add).then_inc(f_v[g], 1)
                dve.wait_ge(f_v[g], v_step("sum", c))
                dve.reciprocal(asum[:, half(g)], asum[:, half(g)]).then_inc(f_v[g], 1)

            def f_onorm(c, g):
                dve.wait_ge(f_red, 2 * NB * c + NB + 4 * g + 4)
                dve.wait_ge(f_v[g], v_step("rec", c))
                rows = xn[:, half(g)].rearrange("p s (h d) -> p (s h) d", d=AD)
                dve.tensor_tensor(rows, rows, asum[:, half(g)].rearrange("p s h -> p (s h)").unsqueeze(2).broadcast_to([P, 4 * AH, AD]),
                                  ALU.mult).then_inc(f_v[g], 1)

            pieces = []
            for g in range(2):
                place(pieces, f"x1:{g}", lambda c, g=g: f_x1(c, g))
                for k in range(3):
                    place(pieces, f"mean{k}:{g}", lambda c, k=k, g=g: f_mean(c, k, g))
                    place(pieces, f"var{k}:{g}", lambda c, k=k, g=g: f_var(c, k, g))
                    place(pieces, f"xn{k}:{g}", lambda c, k=k, g=g: f_norm(c, k, g))
                place(pieces, f"softmax:{g}", lambda c, g=g: f_softmax(c, g))
                place(pieces, f"norms:{g}", lambda c, g=g: f_norms(c, g))
                place(pieces, f"onorm:{g}", lambda c, g=g: f_onorm(c, g))
            for what in (("F", 0), ("F", 1), ("O", 0), ("O", 1), ("F", 2), ("F", 3)):
                place(pieces, f"add{what[0]}{what[1]}", lambda c, what=what: f_add(c, what))
            for m in range(2 * NB):
                if m not in POOL_PRODUCTS:
                    place(pieces, f"prod{m}", lambda c, m=m: f_product(c, m))
                place(pieces, f"red{m}", lambda c, m=m: f_reduce(c, m))

            def step(c, k, pieces, first=False, last=False):
                nxt = not (last and k == UNITS - 1)
                before = not (first and k == 0)
                pc, pk = (c, k - 1) if k else (c - 1, UNITS - 1)
                if k % 2 == 0:
                    b_cos(c, k + 1)
                    at_step(pieces, c, k, 0)
                    if before and has_state(pc, pk):
                        state_of(pc, pk)
                    if before:
                        y_of(pc, pk, not first)
                    if not (last and k == UNITS - 2):
                        x_low(c, k // 2 + 1)
                    at_step(pieces, c, k, 1)
                    scan(c, k + 1)
                    weigh_scores(c, k)
                    at_step(pieces, c, k, 2)
                else:
                    if nxt:
                        b_cos(c, k + 1)
                    at_step(pieces, c, k, 0)
                    y_of(pc, pk, not first)
                    if has_state(pc, pk):
                        state_of(pc, pk)
                    at_step(pieces, c, k, 1)
                    if not (first and k == 1):
                        o_out(c if k > 1 else c - 1, (k // 2 - 1) % NB)
                    if nxt:
                        scan(c, k + 1)
                    weigh_scores(c, k)
                    at_step(pieces, c, k, 2)

            def finish(c):
                y_of(c, UNITS - 1, True)
                o_out(c, NB - 1)

            x_low(0, 0)
            b_cos(0, 0)
            scan(0, 0)
            run_chunks(dve, step, pieces, finish)

        @block.tensor
        def _(pe):
            count = 0

            def tick(ins, name):
                nonlocal count
                count += 1
                ins.then_inc(pp, 1)
                assert PP[name] == count, (name, count)

            def turn(k, src, into=0):
                for q, s in enumerate(src):
                    last = pe.transpose(bank(k)[:, into + P * q:into + P * q + P], s, ident[:])
                return last

            pe.wait_ge(consts, 2)
            pe.wait_ge(ld_scal, 16)
            tick(turn(0, [scal_raw]), "scal_w")
            for c in range(NC + 1):
                if c < NC:
                    for g in range(2):
                        pe.wait_ge(pa, PA["xn", c])
                        after(pe, pa, PA["T", c - 1, g] if c else 0)
                        tick(turn(1 + g, [xn_pro[c % 2][:, 4 * g + q, :] for q in range(4)]), ("T", c, g))
                if c >= 1:
                    for g in range(2):
                        pe.wait_ge(pa, PA["T", c - 1, g])
                        after(pe, pv, PV["scal", c - 2, g] if c >= 2 else 0)
                        for q in range(4):
                            last = pe.matmul(bank(3 + g)[:, P * q:P * q + P], xnT[:, NB * (c - 1) + 4 * g + q, :], w_scal[:],
                                             start=True, stop=True)
                        tick(last, ("scal", c - 1, g))
            groups = [[sel_raw[:, 4 * g + q, :] for q in range(4)] for g in range(4)]
            groups += [[in_raw[:, q, :] for q in range(4)], [out_raw[:, P * q:P * q + P] for q in range(4)],
                       [qkv_raw[:, q, :] for q in range(3)], [ob_raw, f_tern]]
            col, total = slice(0, NT * H), NT * H
            freed = {2: ("lo", 0), 3: ("lo", 1), 4: ("lo", 2), 5: "packed", 6: ("lo", 3), 7: ("lo", 4)}

            def turn_weights(g):
                pe.wait_ge(ld_sel if g < 4 else ld_w, 32 if g < 4 else 80)
                if g >= 2:
                    pe.wait_ge(pv, PV[freed[g]])
                if g == 7:
                    pe.wait_ge(pv, PV["tern"])
                tick(turn(bank_of[g], groups[g]), ("W", g))

            for g in range(2):
                turn_weights(g)
            pe.wait_ge(consts, 3)
            pe.wait_ge(pv, PV["vp"])
            pe.matmul(bank(0)[:, col], upto[:], V, start=True, stop=False)
            tick(pe.matmul(bank(0)[:, col], ones[:], VP, start=False, stop=True), "phi")
            pe.matmul(bank(1)[:, col], upto[:], NLA, start=True, stop=True)
            pe.matmul(bank(2)[:, col], later[:], NLA, start=True, stop=True)
            pe.matmul(bank(3)[:, col], ones[:], NLA, start=True, stop=True)
            pe.wait_ge(pa, PA["abs"])
            tick(pe.matmul(bank(3)[:, total:total + 1], ones[:], fsm[:, 0:1], start=True, stop=True), "cums")
            turn_weights(2)
            pe.wait_ge(pa, PA["dec"])
            turn(4, [ALPHA[:, 0:P], ALPHA[:, P:2 * P]])
            tick(turn(4, [DEC[:, 0:P], DEC[:, P:2 * P]], 2 * P), "rows")
            pe.wait_ge(pv, PV["beta"])
            pe.matmul(bank(5)[:, col], shift[:], DEL, start=True, stop=False)
            pe.matmul(bank(5)[:, 0:total - NB * H], carry[:], DEL[:, NB * H:total], start=False, stop=True)
            tick(pe.matmul(bank(5)[:, total:2 * total], shift[:], BETA, start=True, stop=True), "shifts")
            for g in range(3, 8):
                turn_weights(g)

            pe.wait_ge(bias_in, 144)
            pe.wait_ge(pa, PA["W", 7])
            pe.wait_ge(pv, PV["w_out"])

            def three_passes(i2, out, hi, lo, signal):
                pe.matmul(out, xt_hi[i2], hi, start=True, stop=False)
                pe.matmul(out, xt_hi[i2], lo, start=False, stop=False)
                pe.matmul(out, xt_lo[i2], hi, start=False, stop=True).then_inc(signal, 1)

            def project_u(c, k):
                tile = NB * c + k // 2
                pe.wait_ge(xl_dve, tile + 1)
                after(pe, u_act, tile)
                after(pe, o_dve, tile - 2)
                three_passes((k // 2) % 2, bank(BK_M), w_in_hi[:], w_in_lo[:], u_pe)

            def project_b(c, k):
                h, i2, n = k % 2, (k // 2) % 2, UNITS * c + k
                pe.wait_ge(xl_dve, NB * c + k // 2 + 1)
                after(pe, bs_act, n)
                at = HH * N * h
                three_passes(i2, bank(BK_B), w_sel_hi[:, at:at + HH * N], w_sel_lo[:, at:at + HH * N], b_pe)

            def project_c(c, k):
                h, i2, n = k % 2, (k // 2) % 2, UNITS * c + k
                pe.wait_ge(xl_dve, NB * c + k // 2 + 1)
                after(pe, c_act, n)
                at = HH * N * (2 + h)
                three_passes(i2, bank(BK_C), w_sel_hi[:, at:at + HH * N], w_sel_lo[:, at:at + HH * N], c_pe)

            def turn_b(c, k):
                h, n = k % 2, UNITS * c + k
                pe.wait_ge(bn_pool, n + 1)
                after(pe, cT_act, n)
                turn(BK_T, [bn[h][:, N * q:N * q + N] for q in range(HH)]).then_inc(tb_pe, 1)

            def turn_c(c, k):
                h, n = k % 2, UNITS * c + k
                pe.wait_ge(cn_pool, n + 1)
                pe.wait_ge(bT_act, n + 1)
                turn(BK_T, [cn[h][:, N * q:N * q + N] for q in range(HH)]).then_inc(tc_pe, 1)

            def scores(c, k):
                h, n = k % 2, UNITS * c + k
                pe.wait_ge(bT_act, n + 1)
                pe.wait_ge(cT_act, n + 1)
                after(pe, m_dve, n)
                if has_state(c, k - 1):
                    after(pe, s_dve, n)
                for q in range(HH):
                    last = pe.matmul(bank(BK_G)[:, P * q:P * q + P], bT[h][:, P * q:P * q + P], cT[h][:, P * q:P * q + P],
                                     start=True, stop=True)
                last.then_inc(g_pe, 1)

            def outputs(c, k, inter):
                h, i2, n = k % 2, (k // 2) % 2, UNITS * c + k
                b, tile = k // 2, NB * c + k // 2
                pe.wait_ge(m_dve, n + 1)
                pe.wait_ge(u_act, tile + 1)
                after(pe, y_dve, n)
                for q in range(HH):
                    rows, at = slice(64 * (q % 2), 64 * (q % 2) + 64), P * (q // 2)
                    last = pe.matmul(bank(BK_Y)[rows, at:at + P], u_nat[i2][:, PD * (HH * h + q):PD * (HH * h + q + 1)],
                                     mmat[h][:, P * q:P * q + P], start=True, stop=True)
                if inter:
                    after(pe, s_dve, n - UNITS + 1)
                    for q in range(HH):
                        rows, at = slice(64 * (q % 2), 64 * (q % 2) + 64), 2 * P + P * (q // 2)
                        last = pe.matmul(bank(BK_Y)[rows, at:at + P], state[:, b, PD * (HH * h + q):PD * (HH * h + q + 1)],
                                         cT[h][:, P * q:P * q + P], start=True, stop=True)
                last.then_inc(y_pe, 1)

            def states(c, k):
                h, n = k % 2, UNITS * c + k
                pe.wait_ge(wu_pool, n + 1)
                after(pe, m_dve, n + 1)
                for q in range(HH):
                    at = 2 * P * (q // 2) + 64 * (q % 2)
                    last = pe.matmul(bank(BK_G)[:, at:at + P], bn[h][:, N * q:N * q + N],
                                     wu[h][:, 2 * PD * (q // 2):2 * PD * (q // 2) + 2 * PD], start=True, stop=True)
                last.then_inc(s_pe, 1)

            def project_out(c, b, more):
                tile = NB * c + b
                pe.wait_ge(ysq_act, tile + 1)
                pe.wait_ge(u_act, tile + 3 if more else NT)
                for j in range(4):
                    pe.matmul(bank(BK_M)[:, 0:D], yT[b % 2][:, P * j:P * j + P], w_out[:, j], start=(j == 0), stop=(j == 3))
                for j in range(4):
                    last = pe.matmul(bank(BK_M)[:, D:2 * D], ysq[:, P * j:P * j + P], ones[:], start=(j == 0), stop=(j == 3))
                last.then_inc(o_pe, 1)

            def f_free(c, use):
                m = USES.index(use)
                what, q = USES[m - 2]
                if m < 2:
                    return
                if what == "T":
                    pe.wait_ge(f_T[q % 2], 4 * c + q // 2 + 1)
                elif what == "Q":
                    pe.wait_ge(f_q, NB * c + q + 1)
                else:
                    pe.wait_ge(f_x[q % 2], x_step("attn" if what == "O" else f"ffn{q // 2}", c))

            def f_turn(c, t):
                f_free(c, ("T", t))
                pe.wait_ge(f_v[t % 2], v_step(["xn0", "xn1", "onorm", "xn2"][t // 2], c))
                turn(BK_F[USES.index(("T", t)) % 2], [xn[:, 4 * (t % 2) + q, :] for q in range(4)]).then_inc(f_pe, 1)

            def f_project(c, use):
                what, q4 = use
                f_free(c, use)
                w = w_of[:, 0 if what == "O" else 1]
                turned_before = 3 if what == "O" else 1 if q4 < 2 else 4
                pe.wait_ge(f_T[q4 % 2], 4 * c + turned_before)
                at = BIAS_O if what == "O" else BIAS_F
                pe.matmul(f_bank(use), ones3[:], bias3[:, at:at + 4 * D], start=True, stop=False)
                for q in range(4):
                    last = pe.matmul(f_bank(use)[:, P * q:P * q + P], xnT_f[:, 4 * (q4 % 2) + q, :], w, start=False, stop=(q == 3))
                last.then_inc(f_pe, 1)

            def f_qkv(c, s):
                f_free(c, ("Q", s))
                pe.wait_ge(f_T[s // 4], 4 * c + 2)
                dst = f_bank(("Q", s))[:, 0:3 * D]
                pe.matmul(dst, ones3[:], bias3[:, 0:3 * D], start=True, stop=False)
                pe.matmul(dst, xnT_f[:, s, :], w_qkv[:], start=False, stop=True).then_inc(f_pe, 1)

            pieces = []
            for what, q in USES:
                if what == "T":
                    place(pieces, f"T{q}", lambda c, q=q: f_turn(c, q))
                elif what == "Q":
                    place(pieces, f"qkv{q}", lambda c, q=q: f_qkv(c, q))
                else:
                    place(pieces, f"{what}{q}", lambda c, what=what, q=q: f_project(c, (what, q)))

            def step(c, k, pieces, first=False, last=False):
                nxt = not (last and k == UNITS - 1)
                before = not (first and k == 0)
                pc, pk = (c, k - 1) if k else (c - 1, UNITS - 1)
                if k % 2 == 0:
                    turn_b(c, k)
                    project_b(c, k + 1)
                    if before and has_state(pc, pk):
                        states(pc, pk)
                    if before:
                        outputs(pc, pk, not first)
                    at_step(pieces, c, k, 0)
                    turn_c(c, k)
                    project_c(c, k + 1)
                    at_step(pieces, c, k, 1)
                    scores(c, k)
                    at_step(pieces, c, k, 2)
                else:
                    if nxt:
                        project_b(c, k + 1)
                    turn_b(c, k)
                    outputs(pc, pk, not first)
                    at_step(pieces, c, k, 0)
                    if nxt:
                        project_u(c, k + 1)
                        project_c(c, k + 1)
                    if has_state(pc, pk):
                        states(pc, pk)
                    turn_c(c, k)
                    at_step(pieces, c, k, 1)
                    if not (first and k == 1):
                        project_out(c if k > 1 else c - 1, (k // 2 - 1) % NB, not (last and k >= UNITS - 1))
                    scores(c, k)
                    at_step(pieces, c, k, 2)

            def finish(c):
                outputs(c, UNITS - 1, True)
                project_out(c, NB - 1, False)

            project_u(0, 0)
            project_b(0, 0)
            project_c(0, 0)
            run_chunks(pe, step, pieces, finish)


_INS = ["L0_attn_a_x", "L0_attn_a_in_proj_w", "L0_attn_a_sel_proj_w", "L0_attn_a_out_proj_w", "L0_attn_a_A_log",
        "L0_attn_a_dt_bias", "L0_attn_a_rms_weight", "L0_attn_b_in_proj_w", "L0_attn_b_in_proj_b",
        "L0_attn_b_out_proj_w", "L0_attn_b_out_proj_b", "L0_ffn_weight", "L0_ffn_alpha", "L0_ffn_bias"]


def kernel(**inputs):
    import concourse.bacc as bacc
    from concourse.bass_utils import run_bass_kernel_spmd

    nc = bacc.Bacc("TRN2", target_bir_lowering=False, num_devices=1)
    arrays, args = {}, []
    for name in _INS:
        a = np.ascontiguousarray(inputs[name])
        arrays[f"in_{name}_dram"] = a
        args.append(nc.dram_tensor(f"in_{name}_dram", a.shape, mybir.dt.from_np(a.dtype), kind="ExternalInput").ap())
    args.append(nc.dram_tensor("out_dram", arrays["in_L0_attn_a_x_dram"].shape, F32, kind="ExternalOutput").ap())
    hybrid_block(nc, *args)
    r = run_bass_kernel_spmd(nc, [arrays], core_ids=[0])
    return r.results[0]["out_dram"]
```

```python
from contextlib import ExitStack

import numpy as np

import concourse.bass as bass
from concourse import mybir

F32 = mybir.dt.float32
ALU = mybir.AluOpType
ACT = mybir.ActivationFunctionType
AX = mybir.AxisListType
BF16 = mybir.dt.bfloat16
F32R = mybir.dt.float32r

P = 128
NB = 8
NC = 4
NT = NB * NC
H = 8
HH = 4
N = 128
PD = 64
D = 128
UNITS = 2 * NB
AH = 16
AD = D // AH
BIAS_F, BIAS_O = 3 * D, 7 * D
BIAS = 11 * D
BIAS_IN = 5 * D
SC = 48
COS, SIN, BAND, SW, CD = 0, 8, 16, 32, 40
EPS_LN, EPS_RMS = 1e-5, 1e-6
TERNARY = 0.7
TWO_PI = 2.0 * np.pi
ROUND = 1.5 * 2.0 ** 23
POS = 3
WARM_STATS, WARM_NORM, WARM_SCALARS, WARM_ANGLE, WARM_VALUES, WARM_LAST = 4, 1, 4, 2, 3, 2

USES = [[("T", g), ("F", g), ("T", 2 + g)] + [("Q", 4 * g + s) for s in range(4)] +
        [("T", 4 + g), ("O", g), ("T", 6 + g), ("F", 2 + g)] for g in range(2)]
VSTEPS = ["scaled", "stats0", "var0", "xn0", "stats1", "var1", "xn1", "max", "sub", "sum", "rec", "onorm",
          "stats2", "var2", "xn2"]
GSTEPS = ["ms", "rr", "ve0", "rs0", "ve1", "rs1", "ve2", "rs2"]
XSTEPS = ["x1", "ffn0", "attn", "ffn1"]
POOL_PRODUCTS = (1, 2, 5, 6, 7, 8, 9, 10, 12, 13, 14, 15)
LAST_POOL_PRODUCTS = (1, 2, 4, 5, 6, 7, 8, 9, 10, 11, 12, 13, 14)


PLACE = {"rr:0": 41, "load:0": 41.01, "x1:0": 43, "var0:0": 44, "rs0:0": 45, "xn0:0": 46, "T0": 47, "F0": 47.01,
         "addF0": 47.02, "load:1": 48, "var1:0": 48.01, "rs1:0": 50, "xn1:0": 50.01, "T2": 51, "qkv0": 52,
         "qadd0": 52.01, "rr:1": 52.02, "qkv1": 53, "x1:1": 53.01, "qadd1": 54, "var0:1": 54.01, "qkv2": 55,
         "rs0:1": 56, "xn0:1": 56.01, "T1": 57, "F1": 58, "addF1": 58.01, "qadd2": 59, "var1:1": 59.01, "rs1:1": 60,
         "qkv3": 61, "xn1:1": 61.01, "T3": 62, "qkv4": 63, "qadd4": 63.01, "qkv5": 64, "qadd5": 64.01, "qadd3": 65,
         "qkv6": 65.01, "qadd6": 65.02, "qkv7": 66, "qadd7": 67, "prod0": 67.01, "prod1": 67.02, "red0": 68,
         "red1": 69, "prod2": 69.01, "prod3": 70, "red2": 70.01, "red3": 70.02, "prod4": 71, "softmax:0": 71.01,
         "prod5": 72, "red4": 72.01, "exp:0": 72.02, "red5": 73, "prod6": 73.01, "prod7": 73.02, "red6": 74,
         "norms:0": 74.01, "prod8": 74.02, "red7": 74.03, "prod9": 74.04, "softmax:1": 74.05, "red8": 75,
         "exp:1": 75.01, "prod10": 75.02, "red9": 76, "norms:1": 76.01, "red10": 77, "prod11": 77.01, "red11": 78,
         "onorm:0": 78.01, "prod12": 78.02, "T4": 79, "prod13": 79.01, "red12": 79.02, "red13": 80, "prod14": 80.01,
         "prod15": 80.02, "red14": 81, "O0": 81.01, "red15": 81.02, "onorm:1": 82, "addO0": 82.01, "var2:0": 83,
         "T5": 83.01, "rs2:0": 83.02, "xn2:0": 84, "O1": 84.01, "addO1": 85, "T6": 85.01, "var2:1": 86, "F2": 86.01,
         "addF2": 87, "store:0": 88, "rs2:1": 88.01, "xn2:1": 90, "T7": 91, "F3": 92, "addF3": 94, "store:1": 95}


def place(pieces, name, emit):
    pieces.append((PLACE[name], emit))
    pieces.sort(key=lambda piece: piece[0])


def at_pos(pieces, pos, c):
    for at, emit in pieces:
        if int(at) == pos:
            emit(c)


def run_chunks(eng, step, pieces, finish=None):
    for k in range(UNITS):
        step(0, k, pieces, first=True)
    with eng.Fori(1, NC - 1) as c:
        for k in range(UNITS):
            step(c, k, pieces)
    for k in range(UNITS):
        step(NC - 1, k, pieces, last=True)
    if finish:
        finish(NC - 1)
    for pos in range(POS * UNITS, 2 * POS * UNITS):
        at_pos(pieces, pos, NC - 1)


def at_step(pieces, c, k, sub):
    if not (isinstance(c, int) and c == 0):
        at_pos(pieces, POS * (UNITS + k) + sub, c - 1)
    at_pos(pieces, POS * k + sub, c)


def v_step(name, c):
    return len(VSTEPS) * c + VSTEPS.index(name) + 1


def g_step(name, c):
    return len(GSTEPS) * c + GSTEPS.index(name) + 1


def x_step(name, c):
    return len(XSTEPS) * c + XSTEPS.index(name) + 1


def pool_products(c):
    return LAST_POOL_PRODUCTS if isinstance(c, int) and c == NC - 1 else POOL_PRODUCTS


def half_of(use):
    return use[1] // 4 if use[0] == "Q" else use[1] % 2


def use_done(use, c):
    uses = USES[half_of(use)]
    return len(uses) * c + uses.index(use) + 1


def has_state(c, k):
    return not (isinstance(c, int) and c == NC - 1 and k >= 0)


def numbered(steps):
    return {name: at + 1 for at, name in enumerate(steps) if name is not None}


PA = numbered(["scal_w"] + [n for c in range(NC + 1) for n in
                            ([("xn", c, 0)] if c < NC else []) + ([("T", c - 1, 0), ("T", c - 1, 1)] if c else [])] +
              ["abs", "a", ("W", 0), ("W", 1), "ez", "es", "lz", "alpha", "dec", "suf", "cd", ("W", 2), "rows_a", "rows",
               "sin", "packed"] + [("W", g) for g in (3, 4, 6, 7)])
PA["xnT"] = PA["T", NC - 1, 1]
PV = numbered(["even"] + [n for c in range(NC + 1) for n in
                          ([("bn", c), ("aggr", c)] if c < NC else []) + ([("xn", c - 1, 1)] if c else [])] +
              [("scal", c, g) for c in range(NC) for g in range(2)] +
              [None, "az"] + [None] * 5 + ["dt", "nla", "v", None, None, "vp", ("lo", 0), None, None, "beta"] +
              [None] * 7 + ["red", None, None, None, None, None, "packed", ("lo", 1), ("lo", 2), None, None,
                            ("lo", 3), ("lo", 4), None, None, "tern", "w_out"])
PV["scal"] = PV["scal", NC - 1, 1]
PP = numbered(["scal_w"] + [n for c in range(NC + 1) for n in
                            ([("T", c, 0), ("T", c, 1)] if c < NC else []) +
                            ([("scal", c - 1, 0), ("scal", c - 1, 1)] if c else [])] +
              [("W", 0), ("W", 1), "phi", "cums", ("W", 2), "rows", "shifts"] + [("W", g) for g in range(3, 8)])


def pi_parts():
    c1 = 6.28125
    c2 = float(np.float32(np.round((TWO_PI - c1) * 2.0 ** 21) / 2.0 ** 21))
    return c1, c2, float(np.float32(TWO_PI - c1 - c2))


def hybrid_block(nc, x, in_w, sel_w, out_w, a_log, dt_bias, rms_w, qkv_w, qkv_b, ob_w, ob_b, f_w, f_alpha, f_b, out):
    ctx = ExitStack()
    with ctx:
        def sb(name, shape):
            return ctx.enter_context(nc.sbuf_tensor(name, shape, F32))

        def sem(name):
            return ctx.enter_context(nc.semaphore(name))

        def after(eng, s, count):
            if not isinstance(count, int) or count > 0:
                eng.wait_ge(s, count)

        x_rows = x.rearrange("b (c t) d -> c t b d", c=NC)
        out_rows = out.rearrange("b (c t) d -> c t b d", c=NC)
        alpha_rows = nc.dram_tensor("alpha_rows", [NT * H, P], F32, kind="Internal").ap()
        xT_rows = nc.dram_tensor("xT_rows", [NT, D, P], F32, kind="Internal").ap()
        decay_rows = nc.dram_tensor("decay_rows", [NT * H, P], F32, kind="Internal").ap()

        alpha_of_tile = alpha_rows.rearrange("(j h) t -> j (h t)", h=H)
        decay_of_tile = decay_rows.rearrange("(j r k) t -> j k r t", k=2, r=4)

        ident = sb("ident", [P, P])
        ones = sb("ones", [P, P])
        upto = sb("upto", [P, P])
        later = sb("later", [P, P])
        shift = sb("shift", [P, P])
        carry = sb("carry", [P, P])
        bandm = sb("bandm", [P, P])
        even = sb("even", [P, 2])
        mhalf = sb("mhalf", [P, NB])
        zeros = sb("zeros", [P, P])
        w_sel_hi = ctx.enter_context(nc.sbuf_tensor("w_sel_hi", [P, 2 * H * N], F32R))
        w_sel_lo = ctx.enter_context(nc.sbuf_tensor("w_sel_lo", [P, 2 * H * N], F32R))
        w_in_hi = ctx.enter_context(nc.sbuf_tensor("w_in_hi", [P, H * PD], F32R))
        w_in_lo = ctx.enter_context(nc.sbuf_tensor("w_in_lo", [P, H * PD], F32R))
        w_scal = sb("w_scal", [P, P])
        w_out = sb("w_out", [P, 4, D])
        w_qkv = sb("w_qkv", [P, 3 * D])
        w_of = sb("w_of", [P, 2, D])
        bias3 = ctx.enter_context(nc.sbuf_tensor("bias3", [3, BIAS], BF16))
        ones3 = ctx.enter_context(nc.sbuf_tensor("ones3", [3, P], BF16))
        rms_c = sb("rms_c", [P, 4])
        dtb = sb("dtb", [P, H])
        alog = sb("alog", [P, H])
        a_pos = sb("a_pos", [P, H])
        alpha_c = sb("alpha_c", [P, 1])
        turned = sb("turned", [P, NT * P])
        xnT = turned[:].rearrange("p (j t) -> p j t", t=P)
        scal = sb("scal", [P, NT, 24])
        packed = sb("packed", [P, NT, SC])
        small = sb("small", [P, 24, NT * H])
        stats4 = sb("stats4", [P, NC, NB, 6])
        mv4 = sb("mv4", [P, NC, NB, 2])
        rstd4 = sb("rstd4", [P, NC, NB])
        shift4 = sb("shift4", [P, NC, NB])
        rows_sb = sb("rows_sb", [P, 2, 2, P])
        fsm = sb("fsm", [P, 4])

        area = sb("area", [P, 9216])
        x_all = area[:, 0:4096].rearrange("p (j d) -> p j d", d=D)
        sel_raw = area[:, 4096:6144].rearrange("p (r d) -> p r d", d=D)
        scal_raw = area[:, 6144:6272]
        in_raw = area[:, 6272:6784].rearrange("p (r d) -> p r d", d=D)
        out_raw = area[:, 6784:7296]
        qkv_raw = area[:, 7296:7680].rearrange("p (r d) -> p r d", d=D)
        ob_raw = area[:, 7680:7808]
        f_raw = area[:, 7808:7936]
        f_abs = area[:, 7936:8064]
        f_lo = area[:, 8064:8192]
        f_tern = area[:, 8192:8320]
        qkv = area[:, 0:3072].rearrange("p (s e) -> p s e", s=NB)
        xres = area[:, 3072:4096].rearrange("p (s d) -> p s d", s=NB)
        xn = area[:, 4096:5120].rearrange("p (s d) -> p s d", s=NB)
        xnT_f = area[:, 5120:6144].rearrange("p (s d) -> p s d", s=NB)
        prod = area[:, 6144:8192].rearrange("p (k e) -> p k e", k=2)
        att = area[:, 8192:9216]
        att_s = att.rearrange("p (s r h) -> p s r h", s=NB, r=NB)
        amax = sb("amax", [P, NB, AH])
        asum = sb("asum", [P, NB, AH])
        rr_f = sb("rr_f", [P, NB])
        temp = small[:, 0:4].rearrange("p a (s d) -> p (a s) d", d=D)
        stats_f = sb("stats_f", [P, NB, 6])
        mv_f = sb("mv_f", [P, NB, 2])
        carrier = sb("carrier", [P, 1])
        eps_ln = sb("eps_ln", [P, NB])
        eps_rms = sb("eps_rms", [P, NB])
        rs_f = sb("rs_f", [P, NB])

        def two(name, cols):
            t = sb(name, [P, 2, cols])
            return [t[:, 0], t[:, 1]]

        xt = two("xt", P)
        xt_hi_both = ctx.enter_context(nc.sbuf_tensor("xt_hi", [P, 2, P], F32R))
        xt_lo_both = ctx.enter_context(nc.sbuf_tensor("xt_lo", [P, 2, P], F32R))
        xt_hi, xt_lo = [xt_hi_both[:, k] for k in range(2)], [xt_lo_both[:, k] for k in range(2)]
        sct = two("sct", SC)
        arow = two("arow", H * P)
        drow = two("drow", 4 * P)
        bc, bs, cc_, cs = ([turned[:, 1024 * m + 512 * k:1024 * m + 512 * k + 512] for k in range(2)] for m in range(4))
        bn, cn = two("bn", HH * N), two("cn", HH * N)
        bT, cT = two("bT", HH * P), two("cT", HH * P)
        band, lmat, mmat = two("band", HH * P), two("lmat", HH * P), two("mmat", HH * P)
        u_nat = two("u_nat", H * PD)
        wu = two("wu", HH * PD)
        yinter = sb("yinter", [P, 2 * P])
        sdec = sb("sdec", [P, HH * PD])
        yT_both = sb("yT", [P, 8 * P])
        yT = [yT_both[:, 0:4 * P], yT_both[:, 4 * P:8 * P]]
        ysq = sb("ysq", [P, 4 * P])
        ysum = sb("ysum", [P, P])
        state = sb("state", [P, NB, H * PD])
        xn_pro = [state[:, 2 * k:2 * k + 2].rearrange("p a (b d) -> p (a b) d", d=D) for k in range(2)]
        bias_row, bias_mid = state[0:1, 4:6].rearrange("o a b -> o (a b)")[:, 0:BIAS_IN], state[0:1, 6:8].rearrange("o a b -> o (a b)")[:, 0:BIAS_IN]
        bias_parts = [yT_both[0:1, 320 * k:320 * k + BIAS_IN // 2].bitcast(BF16) for k in range(3)]
        oraw = sb("oraw", [P, NB, 132])

        ps = ctx.enter_context(nc.psum_tensor("ps", [P, 8, 512], F32))
        BK_B, BK_C, BK_T, BK_G, BK_Y, BK_F0, BK_M, BK_F1 = range(8)
        BK_F = (BK_F0, BK_F1)

        ld_x = [sem(f"ld_x{c}") for c in range(NC)]
        ld_scal, ld_sel, ld_w, ld_small = sem("ld_scal"), sem("ld_sel"), sem("ld_w"), sem("ld_small")
        ld_bias, bias_in, bias_split = sem("ld_bias"), sem("bias_in"), sem("bias_split")
        consts = sem("consts")
        pv, pg, pa, pp = sem("pro_vector"), sem("pro_gpsimd"), sem("pro_scalar"), sem("pro_tensor")
        rows_stored = sem("rows_stored")
        xT_stored, xh_act, xl_dve = sem("xT_stored"), sem("xh_act"), sem("xl_dve")
        packed_done = sem("packed_done")
        xt_in, sct_in = [sem("xt_in0"), sem("xt_in1")], [sem("sct_in0"), sem("sct_in1")]
        arow_in, drow_in = [sem("arow_in0"), sem("arow_in1")], [sem("drow_in0"), sem("drow_in1")]
        b_pe, c_pe, u_pe, tb_pe, tc_pe, g_pe = (sem(n) for n in ("b_pe", "c_pe", "u_pe", "tb_pe", "tc_pe", "g_pe"))
        y_pe, s_pe, o_pe = sem("y_pe"), sem("s_pe"), sem("o_pe")
        bc_dve, l_dve, m_dve, yi_dve, y_dve = (sem(n) for n in ("bc_dve", "l_dve", "m_dve", "yi_dve", "y_dve"))
        sd_dve, s_dve, q_dve, o_dve = (sem(n) for n in ("sd_dve", "s_dve", "q_dve", "o_dve"))
        bs_act, c_act, bT_act, cT_act, u_act, ysq_act = (sem(n) for n in ("bs_act", "c_act", "bT_act", "cT_act", "u_act", "ysq_act"))
        band_pool, bn_pool, cn_pool, wu_pool = sem("band_pool"), sem("bn_pool"), sem("cn_pool"), sem("wu_pool")
        f_red, f_prod_v, f_prod_g = (sem(n) for n in ("f_red", "f_prod_v", "f_prod_g"))
        fx_in, rows_free, f_pe, f_q, f_T, f_x, f_exp, f_v, f_g = ([sem(f"{n}{g}") for g in range(2)] for n in (
            "fx_in", "rows_free", "f_pe", "f_q", "f_T", "f_x", "f_exp", "f_v", "f_g"))

        block = ctx.enter_context(nc.Block())

        def attention_product(eng, c, m, signal):
            for g in range(2):
                eng.wait_ge(f_q[g], 4 * c + 4)
            if m >= 2:
                eng.wait_ge(f_red, 2 * NB * c + m - 1)
            if m < NB:
                eng.tensor_tensor(prod[:, m % 2].rearrange("p (r e) -> p r e", r=NB),
                                  qkv[:, m, 0:D].unsqueeze(1).broadcast_to([P, NB, D]), qkv[:, :, D:2 * D],
                                  ALU.mult).then_inc(signal, 1)
            else:
                eng.wait_ge(f_exp[(m - NB) // 4], c + 1)
                eng.tensor_tensor(prod[:, m % 2].rearrange("p (r h d) -> p r h d", r=NB, d=AD),
                                  att_s[:, m - NB].unsqueeze(3).broadcast_to([P, NB, AH, AD]),
                                  qkv[:, :, 2 * D:3 * D].rearrange("p r (h d) -> p r h d", d=AD),
                                  ALU.mult).then_inc(signal, 1)

        def bank(k):
            return ps[:, k, :]

        def half(g):
            return slice(4 * g, 4 * g + 4)

        bank_of = [7, 6, 7, 6, 7, 5, 7, 5]

        (Z, AZ, EZ, LZ, RZ, DT, ES, LAM, OM, GAM, DEL, V, NLA, ALPHA, BETA, VP, PHI, R1, R2, DEC, SUF, G1, DIF, TMP) = (
            small[:, k, :] for k in range(24))

        def tiles(a):
            return a.rearrange("p (j h) -> p j h", h=H)

        @block.sync
        def _(sp):
            sp.dma_start(scal_raw, sel_w[2 * H * N + 3 * H - P:2 * H * N + 3 * H, :]).then_inc(ld_scal, 16)
            for c in range(NC):
                sp.dma_start(x_all[:, NB * c:NB * (c + 1), :], x_rows[c]).then_inc(ld_x[c], 16)
            def spread(v, n):
                return v.unsqueeze(0).broadcast_to([P, n])
            smalls = [(dtb[:], spread(dt_bias, H)), (alog[:], spread(a_log, H)),
                      (alpha_c[:], spread(f_alpha, 1))]
            for dst, src in smalls:
                sp.dma_start(dst, src).then_inc(ld_small, 16)
            with nc.allow_non_contiguous_dma("four columns of weights"):
                sp.dma_start(rms_c[:], rms_w.rearrange("(j p) -> p j", p=P)).then_inc(ld_small, 16)
            sp.dma_start(bias_row[:, 0:3 * D], qkv_b.unsqueeze(0)).then_inc(ld_bias, 16)
            sp.dma_start(bias_row[:, 3 * D:4 * D], f_b.unsqueeze(0)).then_inc(ld_bias, 16)
            sp.dma_start(bias_row[:, 4 * D:5 * D], ob_b.unsqueeze(0)).then_inc(ld_bias, 16)
            for j in range(2):
                sp.dma_start(sel_raw[N // 2 * j:N // 2 * (j + 1)],
                             sel_w[0:2 * H * N, :].rearrange("(r p j) d -> j p r d", j=2, p=N // 2)[j]).then_inc(ld_sel, 16)
            for dst, src in [(in_raw, in_w.rearrange("(r p) d -> p r d", p=P)), (out_raw, out_w),
                             (qkv_raw, qkv_w.rearrange("(r p) d -> p r d", p=P)), (ob_raw, ob_w), (f_raw, f_w)]:
                sp.dma_start(dst, src).then_inc(ld_w, 16)

            for c in range(NC):
                sp.wait_ge(pa, PA["T", c, 1])
                sp.dma_start(xT_rows[NB * c:NB * (c + 1)].rearrange("j d t -> d j t"), xnT[:, NB * c:NB * (c + 1), :]).then_inc(xT_stored, 16)

            sp.wait_ge(bias_split, 5)
            for k, part in enumerate(bias_parts):
                sp.dma_start(bias3[k:k + 1, 0:3 * D], part[:, 0:3 * D]).then_inc(bias_in, 16)
                for at, src in ((BIAS_F, 3 * D), (BIAS_O, 4 * D)):
                    sp.dma_start(bias3[k:k + 1, at:at + 4 * D].rearrange("o (r d) -> o r d", d=D),
                                 part[:, src:src + D].unsqueeze(1).broadcast_to([1, 4, D])).then_inc(bias_in, 16)

            sp.wait_ge(pa, PA["rows"])
            for k in range(2):
                sp.dma_start(alpha_rows[P * k:P * (k + 1), :], rows_sb[:, 0, k, :]).then_inc(rows_stored, 16)
                sp.dma_start(decay_rows[P * k:P * (k + 1), :], rows_sb[:, 1, k, :]).then_inc(rows_stored, 16)

            def tile_loads(c, b):
                i2 = b % 2
                tile = NB * c + b
                after(sp, xl_dve, tile - 1)
                sp.dma_start(xt[i2], xT_rows[tile]).then_inc(xt_in[i2], 16)
                after(sp, l_dve, 2 * (tile - 2) + 2)
                sp.dma_start(arow[i2], alpha_of_tile[tile].unsqueeze(0)
                             .broadcast_to([P, H * P])).then_inc(arow_in[i2], 16)
                after(sp, y_dve, 2 * (tile - 2) + 2)
                if has_state(c, 2 * (b - 2)):
                    after(sp, s_dve, 2 * (tile - 2) + 2)
                sp.dma_start(sct[i2], packed[:, tile, :]).then_inc(sct_in[i2], 16)
                rows = decay_of_tile[tile]
                for k in range(2):
                    sp.dma_start(drow[i2][64 * k:64 * k + 64].rearrange("p (r t) -> p r t", t=P),
                                 rows[k].unsqueeze(0).broadcast_to([64, 4, P])).then_inc(drow_in[i2], 16)

            sp.wait_ge(pv, PV["packed"])
            sp.wait_ge(pa, PA["packed"])
            sp.wait_ge(xT_stored, 16 * NC)
            sp.wait_ge(rows_stored, 64)
            for b in range(NB):
                tile_loads(0, b)
            with sp.Fori(1, NC - 1) as c:
                for b in range(NB):
                    tile_loads(c, b)
            for b in range(NB):
                tile_loads(NC - 1, b)

        def f_alone(use, c):
            name = {"T": "T", "F": "F", "O": "O", "Q": "qkv"}[use[0]] + str(use[1])
            return isinstance(c, int) and c == NC - 1 and PLACE[name] >= POS * UNITS

        def f_bank(use, c):
            g = half_of(use)
            if use[0] == "T" or not f_alone(use, c):
                return bank(BK_F[g])
            return bank([(BK_B, BK_C), (BK_G, BK_Y)][g][use[1] % 2 if use[0] == "Q" else 0])

        @block.gpsimd
        def _(pool):
            def select(t, src, base, mult, step, op, fill):
                return pool.affine_select(out=t, in_=src, compare_op=op, fill=fill, base=base,
                                          pattern=[[step, P]], channel_multiplier=mult)
            pool.memset(zeros[:], 0.0)
            pool.memset(ones[:], 1.0)
            pool.memset(eps_ln[:], EPS_LN)
            pool.memset(eps_rms[:], H * PD * EPS_RMS)
            pool.memset(mhalf[:], -0.5).then_inc(consts, 1)
            pool.wait_ge(consts, 1)
            select(ident[:], zeros[:], 0, 1, -1, ALU.not_equal, 1.0).then_inc(consts, 1)
            select(upto[:], ones[:], 0, -1, 1, ALU.is_ge, 0.0)
            select(later[:], ones[:], 0, 1, -1, ALU.is_gt, 0.0)
            select(shift[:], zeros[:], -1, 1, -1, ALU.not_equal, 1.0)
            select(carry[:], zeros[:], P - 1, P, -1, ALU.not_equal, 1.0)
            pool.wait_ge(consts, 2)
            select(bandm[:], ident[:], 1, 1, -1, ALU.not_equal, 1.0).then_inc(consts, 1)
            for c in range(NC):
                pool.wait_ge(pv, PV["aggr", c])
                pool.tensor_scalar(rstd4[:, c], mv4[:, c, :, 1], 1.0, EPS_LN, ALU.mult, ALU.add).then_inc(pg, 1)
                pool.tensor_scalar(shift4[:, c], mv4[:, c, :, 0], -1.0, None, ALU.mult).then_inc(pg, 1)
                pool.wait_ge(pg, 4 * c + 1)
                pool.tensor_tensor(rstd4[:, c], rstd4[:, c], mhalf[:], ALU.pow).then_inc(pg, 1)
                pool.wait_ge(pg, 4 * c + 3)
                pool.tensor_tensor(shift4[:, c], shift4[:, c], rstd4[:, c], ALU.mult).then_inc(pg, 1)

            pool.memset(ones3[:], 1.0)
            pool.wait_ge(ld_bias, 48)
            pool.tensor_copy(bias_parts[0], bias_row).then_inc(bias_split, 1)
            pool.wait_ge(bias_split, 1)
            pool.tensor_tensor(bias_mid, bias_row, bias_parts[0], ALU.subtract).then_inc(bias_split, 1)
            pool.wait_ge(bias_split, 2)
            pool.tensor_copy(bias_parts[1], bias_mid).then_inc(bias_split, 1)
            pool.wait_ge(bias_split, 3)
            pool.tensor_tensor(bias_row, bias_mid, bias_parts[1], ALU.subtract).then_inc(bias_split, 1)
            pool.wait_ge(bias_split, 4)
            pool.tensor_copy(bias_parts[2], bias_row).then_inc(bias_split, 1)

            pool.wait_ge(pp, PP["T", NC - 1, 1])
            pool.wait_ge(bias_split, 5)
            for g in range(2):
                pool.memset(state[:, 4 * g:4 * g + 4], 0.0).then_inc(rows_free[g], 16)

            def rotate(dst, by_cos, by_sin):
                out, zc, zs = (a.rearrange("p (h j n) -> p j h n", h=HH, j=2) for a in (dst, by_cos, by_sin))
                pool.tensor_tensor(out[:, 0], zc[:, 0], zs[:, 1], ALU.subtract)
                return pool.tensor_tensor(out[:, 1], zc[:, 1], zs[:, 0], ALU.add)

            def add_b(c, k):
                h, n = k % 2, UNITS * c + k
                pool.wait_ge(bs_act, n + 1)
                after(pool, tb_pe, n - 1)
                if has_state(c, k - 2):
                    after(pool, s_pe, n - 1)
                rotate(bn[h], bc[h], bs[h]).then_inc(bn_pool, 1)

            def band_of(c, k):
                h, i2, n = k % 2, (k // 2) % 2, UNITS * c + k
                pool.wait_ge(sct_in[i2], 16 * (NB // 2 * c + k // 4 + 1))
                after(pool, l_dve, n - 1)
                mask = bandm[:].rearrange("p (a k) -> p a k", k=2).unsqueeze(1).broadcast_to([P, HH, P // 2, 2])
                vals = sct[i2][:, BAND + 2 * HH * h:BAND + 2 * HH * (h + 1)].rearrange("p (h k) -> p h k", k=2)
                pool.tensor_tensor(band[h].rearrange("p (h a k) -> p h a k", h=HH, k=2), mask,
                                  vals.unsqueeze(2).broadcast_to([P, HH, P // 2, 2]), ALU.mult).then_inc(band_pool, 1)

            def add_c(c, k):
                h, n = k % 2, UNITS * c + k
                pool.wait_ge(c_act, n + 1)
                after(pool, tc_pe, n - 1)
                rotate(cn[h], cc_[h], cs[h]).then_inc(cn_pool, 1)

            def weigh_u(c, k):
                h, i2, n = k % 2, (k // 2) % 2, UNITS * c + k
                pool.wait_ge(u_act, NB * c + k // 2 + 1)
                after(pool, s_pe, n - 1)
                w = sct[i2][:, SW + HH * h:SW + HH * h + HH].unsqueeze(2).broadcast_to([P, HH, PD])
                pool.tensor_tensor(wu[h].rearrange("p (h q) -> p h q", q=PD),
                                   u_nat[i2][:, HH * PD * h:HH * PD * (h + 1)].rearrange("p (h q) -> p h q", q=PD),
                                   w, ALU.mult).then_inc(wu_pool, 1)

            def rms_root(c, g):
                rr = rr_f[:, half(g)]
                pool.wait_ge(o_dve, NB * c + 4 * g + 4)
                pool.tensor_tensor(rr, oraw[:, half(g), D], eps_rms[:, half(g)], ALU.add).then_inc(f_g[g], 1)
                pool.wait_ge(f_g[g], g_step("ms", c))
                pool.tensor_tensor(rr, rr, mhalf[:, half(g)], ALU.pow).then_inc(f_g[g], 1)

            def ln_root(c, k, g):
                rs = rs_f[:, half(g)]
                pool.wait_ge(f_v[g], v_step(f"var{k}", c))
                pool.tensor_tensor(rs, mv_f[:, half(g), 1], eps_ln[:, half(g)], ALU.add).then_inc(f_g[g], 1)
                pool.wait_ge(f_g[g], g_step(f"ve{k}", c))
                pool.tensor_tensor(rs, rs, mhalf[:, half(g)], ALU.pow).then_inc(f_g[g], 1)

            def product(c, m):
                if m in pool_products(c):
                    attention_product(pool, c, m, f_prod_g)

            pieces = []
            for g in range(2):
                place(pieces, f"rr:{g}", lambda c, g=g: rms_root(c, g))
                for k in range(3):
                    place(pieces, f"rs{k}:{g}", lambda c, k=k, g=g: ln_root(c, k, g))
            for m in range(2 * NB):
                place(pieces, f"prod{m}", lambda c, m=m: product(c, m))

            def step(c, k, pieces, first=False, last=False):
                nxt = not (last and k == UNITS - 1)
                if k % 2 == 0:
                    at_step(pieces, c, k, 0)
                    band_of(c, k + 1)
                    add_b(c, k + 1)
                    at_step(pieces, c, k, 1)
                    if not last:
                        weigh_u(c, k)
                    at_step(pieces, c, k, 2)
                    add_c(c, k + 1)
                else:
                    if nxt:
                        band_of(c, k + 1)
                    at_step(pieces, c, k, 0)
                    if not last:
                        weigh_u(c, k)
                    if nxt:
                        add_b(c, k + 1)
                    at_step(pieces, c, k, 1)
                    if nxt:
                        add_c(c, k + 1)
                    at_step(pieces, c, k, 2)

            band_of(0, 0)
            add_b(0, 0)
            add_c(0, 0)
            run_chunks(pool, step, pieces)

        @block.scalar
        def _(act):
            def evac(dst, src):
                return act.activation(dst, src, ACT.Copy)

            count = 0

            def tick(ins, name=None):
                nonlocal count
                count += 1
                ins.then_inc(pa, 1)
                if name is not None:
                    assert PA[name] == count, (name, count)

            act.wait_ge(pp, PP["scal_w"])
            tick(evac(w_scal[:], bank(0)[:, 0:P]), "scal_w")
            for c in range(NC + 1):
                if c < NC:
                    act.wait_ge(pg, 4 * c + 4)
                    after(act, pp, PP["T", c - 2, 0] if c >= 2 else 0)
                    for b in range(NB // 2):
                        last = act.activation(xn_pro[c % 2][:, b], x_all[:, NB * c + b, :], ACT.Identity,
                                              bias=shift4[:, c, b:b + 1], scale=rstd4[:, c, b:b + 1])
                    tick(last, ("xn", c, 0))
                if c >= 1:
                    for g in range(2):
                        act.wait_ge(pp, PP["T", c - 1, g])
                        at = NB * (c - 1) + 4 * g
                        tick(evac(xnT[:, at:at + 4, :].rearrange("p j t -> p (j t)"), bank(1 + g)), ("T", c - 1, g))
            assert PA["xnT"] == count
            act.wait_ge(ld_w, 80)
            tick(act.activation(f_abs, f_raw, ACT.Abs, accum_out=fsm[:, 0:1]), "abs")
            act.wait_ge(ld_small, 64)
            tick(act.activation(a_pos[:], alog[:], ACT.Exp), "a")
            for g in range(2):
                act.wait_ge(pp, PP["W", g])
                tick(evac(w_sel_hi[:, 512 * g:512 * g + 512], bank(bank_of[g])), ("W", g))
            act.wait_ge(pv, PV["az"])
            tick(act.activation(EZ, AZ, ACT.Exp, scale=-1.0), "ez")
            act.wait_ge(pv, PV["scal"])
            tick(act.activation(tiles(ES), scal[:, :, 8:16], ACT.Exp, scale=-1.0), "es")
            act.wait_ge(pa, PA["ez"])
            tick(act.activation(LZ, EZ, ACT.Ln, bias=1.0), "lz")
            act.wait_ge(pv, PV["nla"])
            tick(act.activation(ALPHA, NLA, ACT.Exp), "alpha")
            act.wait_ge(pp, PP["cums"])
            tick(act.activation(DEC, bank(1)[:, 0:NT * H], ACT.Exp), "dec")
            tick(act.activation(SUF, bank(2)[:, 0:NT * H], ACT.Exp), "suf")
            tick(act.activation(packed[:, :, CD:CD + H], tiles(bank(3)[:, 0:NT * H]), ACT.Exp), "cd")
            act.wait_ge(pp, PP["W", 2])
            tick(evac(w_sel_hi[:, 1024:1536], bank(bank_of[2])), ("W", 2))
            act.wait_ge(pp, PP["rows"])
            tick(evac(rows_sb[:, 0, :, 1:P], bank(4)[:, 0:2 * P].rearrange("p (k t) -> p k t", k=2)[:, :, 1:P]), "rows_a")
            tick(evac(rows_sb[:, 1, :, :], bank(4)[:, 2 * P:4 * P].rearrange("p (k t) -> p k t", k=2)), "rows")
            act.wait_ge(pv, PV["red"])
            tick(act.activation(packed[:, :, SIN:SIN + H], tiles(R1), ACT.Sin), "sin")
            tick(act.activation(packed[:, :, COS:COS + H], tiles(R2), ACT.Sin), "packed")
            act.wait_ge(pp, PP["W", 3])
            tick(evac(w_sel_hi[:, 1536:2048], bank(bank_of[3])), ("W", 3))
            act.wait_ge(pp, PP["W", 4])
            tick(evac(w_in_hi[:], bank(bank_of[4])), ("W", 4))
            def x_high(c, b):
                act.wait_ge(xt_in[b % 2], 16 * (NB // 2 * c + b // 2 + 1))
                after(act, c_pe, 2 * (NB * c + b) - 2)
                evac(xt_hi[b % 2], xt[b % 2]).then_inc(xh_act, 1)

            def u_out(c, k):
                i2, tile = (k // 2) % 2, NB * c + k // 2
                act.wait_ge(u_pe, tile + 1)
                after(act, y_pe, 2 * (tile - 2) + 2)
                if has_state(c, k - 4):
                    after(act, wu_pool, 2 * (tile - 2) + 2)
                evac(u_nat[i2], bank(BK_M)).then_inc(u_act, 1)

            def b_sin(c, k):
                h, i2, n = k % 2, (k // 2) % 2, UNITS * c + k
                act.wait_ge(bc_dve, n + 1)
                act.wait_ge(sct_in[i2], 16 * (NB // 2 * c + k // 4 + 1))
                after(act, bn_pool, n - 1)
                for q in range(HH):
                    last = act.activation(bs[h][:, N * q:N * q + N], bank(BK_B)[:, N * q:N * q + N], ACT.Copy,
                                          scale=sct[i2][:, SIN + HH * h + q:SIN + HH * h + q + 1])
                last.then_inc(bs_act, 1)

            def c_turn(c, k, part):
                h, i2, n = k % 2, (k // 2) % 2, UNITS * c + k
                if part == 0:
                    act.wait_ge(c_pe, n + 1)
                    act.wait_ge(sct_in[i2], 16 * (NB // 2 * c + k // 4 + 1))
                    after(act, cn_pool, n - 1)
                for q in (2 * part, 2 * part + 1):
                    for dst, at in ((cc_, COS), (cs, SIN)):
                        last = act.activation(dst[h][:, N * q:N * q + N], bank(BK_C)[:, N * q:N * q + N], ACT.Copy,
                                              scale=sct[i2][:, at + HH * h + q:at + HH * h + q + 1])
                if part == 1:
                    last.then_inc(c_act, 1)

            def bT_out(c, k):
                h, n = k % 2, UNITS * c + k
                act.wait_ge(tb_pe, n + 1)
                after(act, g_pe, n - 1)
                evac(bT[h], bank(BK_T)).then_inc(bT_act, 1)

            def cT_out(c, k):
                h, n = k % 2, UNITS * c + k
                act.wait_ge(tc_pe, n + 1)
                after(act, y_pe, n - 1)
                evac(cT[h], bank(BK_T)).then_inc(cT_act, 1)

            def y_square(c, b):
                tile = NB * c + b
                act.wait_ge(y_dve, 2 * tile + 2)
                after(act, q_dve, tile)
                act.activation(ysq[:], yT[b % 2], ACT.Square).then_inc(ysq_act, 1)

            def f_T_out(c, t):
                act.wait_ge(f_pe[t % 2], use_done(("T", t), c))
                evac(xnT_f[:, half(t % 2), :].rearrange("p j t -> p (j t)"), f_bank(("T", t), c)).then_inc(f_T[t % 2], 1)

            def f_qkv_out(c, s):
                after(act, f_red, 2 * NB * c)
                act.wait_ge(f_pe[s // 4], use_done(("Q", s), c))
                evac(qkv[:, s, :], f_bank(("Q", s), c)[:, 0:3 * D]).then_inc(f_q[s // 4], 1)

            def f_softmax_exp(c, g):
                act.wait_ge(f_v[g], v_step("sub", c))
                rows = att[:, 4 * P * g:4 * P * (g + 1)]
                act.activation(rows, rows, ACT.Exp, scale=float(AD) ** -0.5).then_inc(f_exp[g], 1)

            pieces = []
            for t in range(8):
                place(pieces, f"T{t}", lambda c, t=t: f_T_out(c, t))
            for q in range(NB):
                place(pieces, f"qadd{q}", lambda c, q=q: f_qkv_out(c, q))

            def f_load(c, g):
                act.wait_ge(rows_free[g], 16 * c + 16)
                act.dma_start(xres[:, half(g)], x_rows[c][:, half(g)]).then_inc(fx_in[g], 16)

            def f_store(c, g):
                act.wait_ge(f_x[g], x_step("ffn1", c))
                act.dma_start(out_rows[c][:, half(g)], xres[:, half(g)]).then_inc(rows_free[g], 16)

            for g in range(2):
                place(pieces, f"exp:{g}", lambda c, g=g: f_softmax_exp(c, g))
                place(pieces, f"load:{g}", lambda c, g=g: f_load(c, g))
                place(pieces, f"store:{g}", lambda c, g=g: f_store(c, g))

            def step(c, k, pieces, first=False, last=False):
                nxt = not (last and k == UNITS - 1)
                if k % 2 == 0:
                    if not (last and k == UNITS - 2):
                        x_high(c, k // 2 + 1)
                    bT_out(c, k)
                    at_step(pieces, c, k, 0)
                    b_sin(c, k + 1)
                    cT_out(c, k)
                    at_step(pieces, c, k, 1)
                    c_turn(c, k + 1, 0)
                    c_turn(c, k + 1, 1)
                    if not (first and k == 0):
                        y_square(c if k > 1 else c - 1, (k // 2 - 1) % NB)
                    at_step(pieces, c, k, 2)
                else:
                    bT_out(c, k)
                    if nxt:
                        u_out(c, k + 1)
                    at_step(pieces, c, k, 0)
                    if nxt:
                        b_sin(c, k + 1)
                    at_step(pieces, c, k, 1)
                    cT_out(c, k)
                    if nxt:
                        c_turn(c, k + 1, 0)
                        c_turn(c, k + 1, 1)
                    at_step(pieces, c, k, 2)

            def finish(c):
                y_square(c, NB - 1)

            x_high(0, 0)
            b_sin(0, 0)
            c_turn(0, 0, 0)
            c_turn(0, 0, 1)
            u_out(0, 0)
            act.wait_ge(pp, PP["W", 6])
            tick(evac(w_qkv[:], bank(bank_of[6])[:, 0:3 * D]), ("W", 6))
            act.wait_ge(pp, PP["W", 7])
            tick(evac(w_of[:].rearrange("p k d -> p (k d)"), bank(bank_of[7])[:, 0:2 * D]), ("W", 7))
            run_chunks(act, step, pieces, finish)
            for g in range(2):
                act.wait_ge(rows_free[g], 16 * NC + 16)

        @block.vector
        def _(dve):
            count = 0

            def tick(ins, name=None, wait=False):
                nonlocal count
                count += 1
                ins.then_inc(pv, 1)
                if name is not None:
                    assert PV[name] == count, (name, count)
                if wait:
                    dve.wait_ge(pv, count)

            dve.memset(rows_sb[:, 0, :, 0:1], 0.0)
            dve.wait_ge(consts, 3)
            tick(dve.tensor_reduce(even[:], ident[:].rearrange("p (a k) -> p k a", k=2), AX.X, ALU.add), "even")

            for c in range(NC + 1):
                if c < NC:
                    dve.wait_ge(ld_x[c], 16)
                    for b in range(NB):
                        last = dve.bn_stats(stats4[:, c, b], x_all[:, NB * c + b, :])
                    tick(last, ("bn", c), wait=True)
                    for b in range(NB):
                        last = dve.bn_aggr(mv4[:, c, b], stats4[:, c, b])
                    tick(last, ("aggr", c))
                if c >= 1:
                    dve.wait_ge(pg, 4 * c)
                    after(dve, pp, PP["T", c - 3, 1] if c >= 3 else 0)
                    for b in range(NB // 2, NB):
                        last = dve.tensor_scalar(xn_pro[(c - 1) % 2][:, b], x_all[:, NB * (c - 1) + b, :],
                                                 mv4[:, c - 1, b, 0:1], rstd4[:, c - 1, b:b + 1], ALU.subtract, ALU.mult)
                    tick(last, ("xn", c - 1, 1))
            for c in range(NC):
                for g in range(2):
                    dve.wait_ge(pp, PP["scal", c, g])
                    tick(dve.tensor_copy(scal[:, NB * c + 4 * g:NB * c + 4 * g + 4, :],
                                         bank(3 + g).rearrange("p (j e) -> p j e", e=P)[:, :, P - 24:P]), ("scal", c, g))
            dve.wait_ge(ld_small, 64)
            dve.wait_ge(pv, PV["scal"])
            per_head = dtb[:].unsqueeze(1).broadcast_to([P, NT, H])
            tick(dve.tensor_tensor(tiles(Z), scal[:, :, 0:8], per_head, ALU.add), None, True)
            tick(dve.scalar_tensor_tensor(AZ, Z, -1.0, Z, ALU.mult, ALU.max), "az")
            tick(dve.tensor_scalar(RZ, Z, 0.0, None, ALU.max))
            W = NB * H
            tick(dve.memset(VP[:, 0:W], 0.0))
            dve.wait_ge(pa, PA["es"])
            tick(dve.tensor_scalar(TMP, ES, 1.0, None, ALU.add), None, True)
            tick(dve.reciprocal(LAM, TMP), None, True)
            tick(dve.tensor_scalar(OM, LAM, -1.0, 1.0, ALU.mult, ALU.add))
            dve.wait_ge(pa, PA["lz"])
            dve.wait_ge(pv, count)
            tick(dve.tensor_tensor(DT, RZ, LZ, ALU.add), "dt", True)
            dve.wait_ge(pa, PA["a"])
            per_head = a_pos[:].unsqueeze(1).broadcast_to([P, NT, H])
            tick(dve.scalar_tensor_tensor(tiles(NLA), tiles(DT), -1.0, per_head, ALU.mult, ALU.mult), "nla")
            tick(dve.tensor_tensor(tiles(V), tiles(DT), scal[:, :, 16:24], ALU.mult), "v", True)
            for c in range(1, NC):
                tick(dve.tensor_tensor(VP[:, W * c:W * (c + 1)], VP[:, W * (c - 1):W * c], V[:, W * (c - 1):W * c], ALU.add),
                     "vp" if c == NC - 1 else None, True)

            def low_part(g):
                dve.wait_ge(pa, PA["W", g])
                hi, lo = (w_sel_hi[:, 512 * g:512 * g + 512], w_sel_lo[:, 512 * g:512 * g + 512]) if g < 4 else (w_in_hi[:], w_in_lo[:])
                tick(dve.tensor_tensor(lo, bank(bank_of[g]), hi.bitcast(F32), ALU.subtract), ("lo", g))

            low_part(0)
            tick(dve.tensor_tensor(GAM, LAM, DT, ALU.mult))
            tick(dve.tensor_tensor(DEL, OM, DT, ALU.mult), None, True)
            dve.wait_ge(pa, PA["alpha"])
            tick(dve.tensor_tensor(BETA, DEL, ALPHA, ALU.mult), "beta")
            dve.wait_ge(pp, PP["phi"])
            c1, c2, c3 = pi_parts()
            tick(dve.tensor_scalar(R1, bank(0)[:, 0:NT * H], 1.0 / TWO_PI, ROUND, ALU.mult, ALU.add), None, True)
            tick(dve.tensor_scalar(R1, R1, -ROUND, None, ALU.add), None, True)
            tick(dve.scalar_tensor_tensor(PHI, R1, -c1, bank(0)[:, 0:NT * H], ALU.mult, ALU.add), None, True)
            tick(dve.scalar_tensor_tensor(R2, R1, -c2, PHI, ALU.mult, ALU.add), None, True)
            tick(dve.scalar_tensor_tensor(PHI, R1, -c3, R2, ALU.mult, ALU.add), None, True)
            pi32 = float(np.nextafter(np.float32(np.pi), np.float32(0)))
            tick(dve.tensor_scalar(R1, PHI, pi32, -pi32, ALU.min, ALU.max), None, True)
            tick(dve.scalar_tensor_tensor(R2, R1, -1.0, R1, ALU.mult, ALU.max), None, True)
            tick(dve.tensor_scalar(R2, R2, -1.0, float(np.pi / 2), ALU.mult, ALU.add), "red")
            dve.wait_ge(pp, PP["shifts"])
            tick(dve.tensor_tensor(G1, GAM, bank(5)[:, 0:NT * H], ALU.add))
            tick(dve.tensor_copy(TMP, bank(5)[:, NT * H:2 * NT * H]), None, True)
            dve.wait_ge(pa, PA["suf"])
            tick(dve.tensor_tensor(packed[:, :, SW:SW + H], tiles(G1), tiles(SUF), ALU.mult))
            tick(dve.tensor_tensor(DIF, GAM, TMP, ALU.subtract), None, True)
            pairs = packed[:, :, BAND:BAND + 2 * H].rearrange("p j (h k) -> p j h k", k=2)
            for k in range(2):
                tick(dve.scalar_tensor_tensor(pairs[:, :, :, k], tiles(DIF), even[:, k:k + 1], tiles(TMP), ALU.mult, ALU.add),
                     "packed" if k == 1 else None)
            low_part(1)
            low_part(2)
            dve.wait_ge(pa, PA["cd"])
            tick(dve.tensor_scalar(fsm[:, 1:2], bank(3)[:, NT * H:NT * H + 1], 1.0 / (D * D), TERNARY, ALU.mult, ALU.mult), None, True)
            tick(dve.tensor_scalar(fsm[:, 2:3], fsm[:, 1:2], -1.0, None, ALU.mult))
            low_part(3)
            low_part(4)
            for g in range(2):
                dve.wait_ge(rows_free[g], 16)

            def b_cos(c, k):
                h, i2, n = k % 2, (k // 2) % 2, UNITS * c + k
                dve.wait_ge(b_pe, n + 1)
                dve.wait_ge(sct_in[i2], 16 * (NB // 2 * c + k // 4 + 1))
                after(dve, bn_pool, n - 1)
                cosv = sct[i2][:, COS + HH * h:COS + HH * h + HH].unsqueeze(2).broadcast_to([P, HH, N])
                dve.tensor_tensor(bc[h].rearrange("p (h n) -> p h n", n=N), bank(BK_B).rearrange("p (h n) -> p h n", n=N),
                                  cosv, ALU.mult).then_inc(bc_dve, 1)

            def x_low(c, b):
                dve.wait_ge(xh_act, NB * c + b + 1)
                dve.tensor_tensor(xt_lo[b % 2], xt[b % 2], xt_hi[b % 2].bitcast(F32), ALU.subtract).then_inc(xl_dve, 1)

            def scan(c, k):
                h, i2, n = k % 2, (k // 2) % 2, UNITS * c + k
                dve.wait_ge(arow_in[i2], 16 * (NB // 2 * c + k // 4 + 1))
                dve.wait_ge(band_pool, n + 1)
                after(dve, m_dve, n - 1)
                dve.tensor_tensor_scan(lmat[h], arow[i2][:, HH * P * h:HH * P * (h + 1)], band[h], 0.0,
                                       ALU.mult, ALU.add).then_inc(l_dve, 1)

            def weigh_scores(c, k):
                h, n = k % 2, UNITS * c + k
                dve.wait_ge(g_pe, n + 1)
                dve.wait_ge(l_dve, n + 1)
                after(dve, y_pe, n - 1)
                dve.tensor_tensor(mmat[h], bank(BK_G), lmat[h], ALU.mult).then_inc(m_dve, 1)

            def y_of(c, k, inter):
                h, i2, n = k % 2, (k // 2) % 2, UNITS * c + k
                tile = NB * c + k // 2
                dve.wait_ge(y_pe, n + 1)
                after(dve, o_pe, tile - 1)
                dst = yT[i2][:, 2 * P * h:2 * P * (h + 1)]
                if inter:
                    dve.wait_ge(drow_in[i2], 32 * (NB // 2 * c + k // 4 + 1))
                    dve.tensor_tensor(yinter[:], bank(BK_Y)[:, 2 * P:4 * P], drow[i2][:, 2 * P * h:2 * P * (h + 1)],
                                      ALU.mult).then_inc(yi_dve, 1)
                    dve.wait_ge(yi_dve, n - UNITS + 2)
                    dve.tensor_tensor(dst, bank(BK_Y)[:, 0:2 * P], yinter[:], ALU.add).then_inc(y_dve, 1)
                else:
                    dve.tensor_copy(dst, bank(BK_Y)[:, 0:2 * P]).then_inc(y_dve, 1)

            def state_of(c, k):
                h, i2, n = k % 2, (k // 2) % 2, UNITS * c + k
                b = k // 2
                st = state[:, b, HH * PD * h:HH * PD * (h + 1)].rearrange("p (h q) -> p h q", q=PD)
                dec = sct[i2][:, CD + HH * h:CD + HH * h + HH].unsqueeze(2).broadcast_to([P, HH, PD])
                dve.tensor_tensor(sdec[:].rearrange("p (h q) -> p h q", q=PD), st, dec, ALU.mult).then_inc(sd_dve, 1)
                dve.wait_ge(s_pe, n + 1)
                dve.wait_ge(y_pe, n + 1)
                dve.wait_ge(sd_dve, n + 1)
                own = bank(BK_G).rearrange("p (h q) -> p h q", q=N)[:, :, 0:PD]
                dve.tensor_tensor(st, sdec[:].rearrange("p (h q) -> p h q", q=PD), own, ALU.add).then_inc(s_dve, 1)

            def y_sum(c, b):
                tile = NB * c + b
                dve.wait_ge(ysq_act, tile + 1)
                after(dve, o_pe, tile)
                dve.tensor_reduce(ysum[:], ysq[:].rearrange("p (j t) -> p t j", t=P), AX.X, ALU.add).then_inc(q_dve, 1)

            def o_out(c, b):
                dve.wait_ge(o_pe, NB * c + b + 1)
                dve.tensor_copy(oraw[:, b, 0:D + 1], bank(BK_M)[:, 0:D + 1]).then_inc(o_dve, 1)

            def f_x1(c, g):
                dve.wait_ge(f_g[g], g_step("rr", c))
                dve.wait_ge(fx_in[g], 16 * c + 16)
                dve.scalar_tensor_tensor(temp[:, half(g)], oraw[:, half(g), 0:D], float(np.sqrt(H * PD)),
                                         rr_f[:, half(g)].unsqueeze(2).broadcast_to([P, 4, D]),
                                         ALU.mult, ALU.mult).then_inc(f_v[g], 1)
                dve.wait_ge(f_v[g], v_step("scaled", c))
                dve.tensor_tensor(xres[:, half(g)], xres[:, half(g)], temp[:, half(g)], ALU.add).then_inc(f_x[g], 1)

            def f_var(c, k, g):
                dve.wait_ge(f_x[g], x_step(XSTEPS[k], c))
                for s in range(4 * g, 4 * g + 4):
                    last = dve.bn_stats(stats_f[:, s], xres[:, s])
                last.then_inc(f_v[g], 1)
                dve.wait_ge(f_v[g], v_step(f"stats{k}", c))
                dve.memset(carrier[:], 0.0)
                for s in range(4 * g, 4 * g + 4):
                    last = dve.bn_aggr(mv_f[:, s], stats_f[:, s])
                last.then_inc(f_v[g], 1)

            def f_norm(c, k, g):
                dve.wait_ge(f_g[g], g_step(f"rs{k}", c))
                for s in range(4 * g, 4 * g + 4):
                    last = dve.tensor_scalar(xn[:, s], xres[:, s], mv_f[:, s, 0:1], rs_f[:, s:s + 1], ALU.subtract, ALU.mult)
                last.then_inc(f_v[g], 1)

            def f_add(c, what):
                g = what[1] % 2
                dve.wait_ge(f_pe[g], use_done(what, c))
                rows = xres[:, half(g), :].rearrange("p j d -> p (j d)")
                dve.tensor_tensor(rows, f_bank(what, c), rows, ALU.add).then_inc(f_x[g], 1)

            def f_product(c, m):
                if m not in pool_products(c):
                    attention_product(dve, c, m, f_prod_v)

            def f_reduce(c, m):
                theirs = pool_products(c)
                if m in theirs:
                    dve.wait_ge(f_prod_g, len(POOL_PRODUCTS) * c + theirs.index(m) + 1)
                else:
                    mine = [q for q in range(2 * NB) if q not in theirs]
                    dve.wait_ge(f_prod_v, (2 * NB - len(POOL_PRODUCTS)) * c + mine.index(m) + 1)
                if m < NB:
                    dve.tensor_reduce(att[:, P * m:P * (m + 1)], prod[:, m % 2].rearrange("p (e d) -> p e d", d=AD),
                                      AX.X, ALU.add).then_inc(f_red, 1)
                else:
                    dve.tensor_reduce(xn[:, m - NB, :], prod[:, m % 2].rearrange("p (r e) -> p e r", r=NB),
                                      AX.X, ALU.add).then_inc(f_red, 1)

            def f_softmax(c, g):
                rows = att_s[:, half(g)]
                dve.wait_ge(f_red, 2 * NB * c + 4 * g + 4)
                dve.tensor_reduce(amax[:, half(g)], rows.rearrange("p s r h -> p s h r"), AX.X, ALU.max).then_inc(f_v[g], 1)
                dve.wait_ge(f_v[g], v_step("max", c))
                dve.tensor_tensor(rows, rows, amax[:, half(g)].unsqueeze(2).broadcast_to([P, 4, NB, AH]), ALU.subtract).then_inc(f_v[g], 1)

            def f_norms(c, g):
                dve.wait_ge(f_exp[g], c + 1)
                dve.tensor_reduce(asum[:, half(g)], att_s[:, half(g)].rearrange("p s r h -> p s h r"), AX.X, ALU.add).then_inc(f_v[g], 1)
                dve.wait_ge(f_v[g], v_step("sum", c))
                dve.reciprocal(asum[:, half(g)], asum[:, half(g)]).then_inc(f_v[g], 1)

            def f_onorm(c, g):
                dve.wait_ge(f_red, 2 * NB * c + NB + 4 * g + 4)
                dve.wait_ge(f_v[g], v_step("rec", c))
                rows = xn[:, half(g)].rearrange("p s (h d) -> p (s h) d", d=AD)
                dve.tensor_tensor(rows, rows, asum[:, half(g)].rearrange("p s h -> p (s h)").unsqueeze(2).broadcast_to([P, 4 * AH, AD]),
                                  ALU.mult).then_inc(f_v[g], 1)

            pieces = []
            for g in range(2):
                place(pieces, f"x1:{g}", lambda c, g=g: f_x1(c, g))
                for k in range(3):
                    place(pieces, f"var{k}:{g}", lambda c, k=k, g=g: f_var(c, k, g))
                    place(pieces, f"xn{k}:{g}", lambda c, k=k, g=g: f_norm(c, k, g))
                place(pieces, f"softmax:{g}", lambda c, g=g: f_softmax(c, g))
                place(pieces, f"norms:{g}", lambda c, g=g: f_norms(c, g))
                place(pieces, f"onorm:{g}", lambda c, g=g: f_onorm(c, g))
            for what in (("F", 0), ("F", 1), ("O", 0), ("O", 1), ("F", 2), ("F", 3)):
                place(pieces, f"add{what[0]}{what[1]}", lambda c, what=what: f_add(c, what))
            for m in range(2 * NB):
                place(pieces, f"prod{m}", lambda c, m=m: f_product(c, m))
                place(pieces, f"red{m}", lambda c, m=m: f_reduce(c, m))

            def step(c, k, pieces, first=False, last=False):
                nxt = not (last and k == UNITS - 1)
                before = not (first and k == 0)
                pc, pk = (c, k - 1) if k else (c - 1, UNITS - 1)
                if k % 2 == 0:
                    b_cos(c, k + 1)
                    at_step(pieces, c, k, 0)
                    if not (last and k == UNITS - 2):
                        x_low(c, k // 2 + 1)
                    if before and has_state(pc, pk):
                        state_of(pc, pk)
                    if before:
                        y_of(pc, pk, not first)
                    at_step(pieces, c, k, 1)
                    scan(c, k + 1)
                    weigh_scores(c, k)
                    at_step(pieces, c, k, 2)
                    if not (first and k == 0):
                        y_sum(c if k > 1 else c - 1, (k // 2 - 1) % NB)
                else:
                    if nxt:
                        b_cos(c, k + 1)
                    at_step(pieces, c, k, 0)
                    if has_state(pc, pk):
                        state_of(pc, pk)
                    at_step(pieces, c, k, 1)
                    if nxt:
                        scan(c, k + 1)
                    if not (first and k == 1):
                        o_out(c if k > 1 else c - 1, (k // 2 - 1) % NB)
                    y_of(pc, pk, not first)
                    weigh_scores(c, k)
                    at_step(pieces, c, k, 2)

            def finish(c):
                y_of(c, UNITS - 1, True)
                y_sum(c, NB - 1)
                o_out(c, NB - 1)

            x_low(0, 0)
            b_cos(0, 0)
            scan(0, 0)
            dve.wait_ge(pv, PV["lo", 3] - 1)
            tick(dve.tensor_scalar(f_abs, f_raw, fsm[:, 1:2], alpha_c[:, 0:1], ALU.is_gt, ALU.mult))
            tick(dve.tensor_scalar(f_lo, f_raw, fsm[:, 2:3], alpha_c[:, 0:1], ALU.is_lt, ALU.mult), None, True)
            tick(dve.tensor_tensor(f_tern, f_abs, f_lo, ALU.subtract), "tern")
            dve.wait_ge(pp, PP["W", 5])
            for j in range(4):
                last = dve.tensor_scalar(w_out[:, j], bank(bank_of[5])[:, P * j:P * j + P], rms_c[:, j:j + 1], None, ALU.mult)
            tick(last, "w_out")
            run_chunks(dve, step, pieces, finish)

        @block.tensor
        def _(pe):
            count = 0

            def tick(ins, name):
                nonlocal count
                count += 1
                ins.then_inc(pp, 1)
                assert PP[name] == count, (name, count)

            def turn(k, src, into=0):
                for q, s in enumerate(src):
                    last = pe.transpose(bank(k)[:, into + P * q:into + P * q + P], s, ident[:])
                return last

            def keep_warm(count, k):
                for _ in range(count):
                    turn(k, [ident[:]] * 4)

            pe.wait_ge(consts, 2)
            pe.wait_ge(ld_scal, 16)
            tick(turn(0, [scal_raw]), "scal_w")
            pe.wait_ge(pv, PV["bn", 0])
            keep_warm(WARM_STATS, 5)
            pe.wait_ge(pg, 4)
            keep_warm(WARM_NORM, 5)
            for c in range(NC + 1):
                if c < NC:
                    for g in range(2):
                        pe.wait_ge(pv if g else pa, (PV if g else PA)["xn", c, g])
                        after(pe, pa, PA["T", c - 1, g] if c else 0)
                        tick(turn(1 + g, [xn_pro[c % 2][:, 4 * g + q, :] for q in range(4)]), ("T", c, g))
                if c >= 1:
                    for g in range(2):
                        pe.wait_ge(pa, PA["T", c - 1, g])
                        after(pe, pv, PV["scal", c - 2, g] if c >= 2 else 0)
                        for q in range(4):
                            last = pe.matmul(bank(3 + g)[:, P * q:P * q + P], xnT[:, NB * (c - 1) + 4 * g + q, :], w_scal[:],
                                             start=True, stop=True)
                        tick(last, ("scal", c - 1, g))
            groups = [[sel_raw[:, 4 * g + q, :] for q in range(4)] for g in range(4)]
            groups += [[in_raw[:, q, :] for q in range(4)], [out_raw[:, P * q:P * q + P] for q in range(4)],
                       [qkv_raw[:, q, :] for q in range(3)], [ob_raw, f_tern]]
            col, total = slice(0, NT * H), NT * H
            freed = {2: ("lo", 0), 3: ("lo", 1), 4: ("lo", 2), 5: "packed", 6: ("lo", 4), 7: "w_out"}

            def turn_weights(g):
                pe.wait_ge(ld_sel if g < 4 else ld_w, 32 if g < 4 else 80)
                if g >= 2:
                    pe.wait_ge(pv, PV[freed[g]])
                tick(turn(bank_of[g], groups[g]), ("W", g))

            for g in range(2):
                turn_weights(g)
            pe.wait_ge(consts, 3)
            pe.wait_ge(pv, PV["az"])
            keep_warm(WARM_SCALARS, 5)
            pe.wait_ge(pv, PV["dt"])
            keep_warm(WARM_ANGLE, 5)
            pe.wait_ge(pv, PV["vp"])
            pe.matmul(bank(0)[:, col], upto[:], V, start=True, stop=False)
            tick(pe.matmul(bank(0)[:, col], ones[:], VP, start=False, stop=True), "phi")
            pe.matmul(bank(1)[:, col], upto[:], NLA, start=True, stop=True)
            pe.matmul(bank(2)[:, col], later[:], NLA, start=True, stop=True)
            pe.matmul(bank(3)[:, col], ones[:], NLA, start=True, stop=True)
            pe.wait_ge(pa, PA["abs"])
            tick(pe.matmul(bank(3)[:, total:total + 1], ones[:], fsm[:, 0:1], start=True, stop=True), "cums")
            turn_weights(2)
            pe.wait_ge(pa, PA["dec"])
            turn(4, [ALPHA[:, 0:P], ALPHA[:, P:2 * P]])
            tick(turn(4, [DEC[:, 0:P], DEC[:, P:2 * P]], 2 * P), "rows")
            pe.wait_ge(pv, PV["beta"])
            pe.matmul(bank(5)[:, col], shift[:], DEL, start=True, stop=False)
            pe.matmul(bank(5)[:, 0:total - NB * H], carry[:], DEL[:, NB * H:total], start=False, stop=True)
            tick(pe.matmul(bank(5)[:, total:2 * total], shift[:], BETA, start=True, stop=True), "shifts")
            for g in range(3, 5):
                turn_weights(g)
            pe.wait_ge(pv, PV["lo", 4])

            def three_passes(i2, out, hi, lo, signal):
                pe.matmul(out, xt_hi[i2], hi, start=True, stop=False)
                pe.matmul(out, xt_hi[i2], lo, start=False, stop=False)
                pe.matmul(out, xt_lo[i2], hi, start=False, stop=True).then_inc(signal, 1)

            def project_u(c, k):
                tile = NB * c + k // 2
                pe.wait_ge(xl_dve, tile + 1)
                after(pe, u_act, tile)
                after(pe, o_dve, tile - 2)
                three_passes((k // 2) % 2, bank(BK_M), w_in_hi[:], w_in_lo[:], u_pe)

            def project_b(c, k):
                h, i2, n = k % 2, (k // 2) % 2, UNITS * c + k
                pe.wait_ge(xl_dve, NB * c + k // 2 + 1)
                after(pe, bs_act, n)
                at = HH * N * h
                three_passes(i2, bank(BK_B), w_sel_hi[:, at:at + HH * N], w_sel_lo[:, at:at + HH * N], b_pe)

            def project_c(c, k):
                h, i2, n = k % 2, (k // 2) % 2, UNITS * c + k
                pe.wait_ge(xl_dve, NB * c + k // 2 + 1)
                after(pe, c_act, n)
                at = HH * N * (2 + h)
                three_passes(i2, bank(BK_C), w_sel_hi[:, at:at + HH * N], w_sel_lo[:, at:at + HH * N], c_pe)

            def turn_b(c, k):
                h, n = k % 2, UNITS * c + k
                pe.wait_ge(bn_pool, n + 1)
                after(pe, cT_act, n)
                turn(BK_T, [bn[h][:, N * q:N * q + N] for q in range(HH)]).then_inc(tb_pe, 1)

            def turn_c(c, k):
                h, n = k % 2, UNITS * c + k
                pe.wait_ge(cn_pool, n + 1)
                pe.wait_ge(bT_act, n + 1)
                turn(BK_T, [cn[h][:, N * q:N * q + N] for q in range(HH)]).then_inc(tc_pe, 1)

            def scores(c, k):
                h, n = k % 2, UNITS * c + k
                pe.wait_ge(bT_act, n + 1)
                pe.wait_ge(cT_act, n + 1)
                after(pe, m_dve, n)
                if has_state(c, k - 1):
                    after(pe, s_dve, n)
                for q in range(HH):
                    last = pe.matmul(bank(BK_G)[:, P * q:P * q + P], bT[h][:, P * q:P * q + P], cT[h][:, P * q:P * q + P],
                                     start=True, stop=True)
                last.then_inc(g_pe, 1)

            def outputs(c, k, inter):
                h, i2, n = k % 2, (k // 2) % 2, UNITS * c + k
                b, tile = k // 2, NB * c + k // 2
                pe.wait_ge(m_dve, n + 1)
                pe.wait_ge(u_act, tile + 1)
                after(pe, y_dve, n)
                for q in range(HH):
                    rows, at = slice(64 * (q % 2), 64 * (q % 2) + 64), P * (q // 2)
                    last = pe.matmul(bank(BK_Y)[rows, at:at + P], u_nat[i2][:, PD * (HH * h + q):PD * (HH * h + q + 1)],
                                     mmat[h][:, P * q:P * q + P], start=True, stop=True)
                if inter:
                    after(pe, s_dve, n - UNITS + 1)
                    for q in range(HH):
                        rows, at = slice(64 * (q % 2), 64 * (q % 2) + 64), 2 * P + P * (q // 2)
                        last = pe.matmul(bank(BK_Y)[rows, at:at + P], state[:, b, PD * (HH * h + q):PD * (HH * h + q + 1)],
                                         cT[h][:, P * q:P * q + P], start=True, stop=True)
                last.then_inc(y_pe, 1)

            def states(c, k):
                h, n = k % 2, UNITS * c + k
                pe.wait_ge(wu_pool, n + 1)
                after(pe, m_dve, n + 1)
                for q in range(HH):
                    at = 2 * P * (q // 2) + 64 * (q % 2)
                    last = pe.matmul(bank(BK_G)[:, at:at + P], bn[h][:, N * q:N * q + N],
                                     wu[h][:, 2 * PD * (q // 2):2 * PD * (q // 2) + 2 * PD], start=True, stop=True)
                last.then_inc(s_pe, 1)

            def project_out(c, b, more):
                tile = NB * c + b
                pe.wait_ge(q_dve, tile + 1)
                pe.wait_ge(u_act, tile + 3 if more else NT)
                for j in range(4):
                    pe.matmul(bank(BK_M)[:, 0:D], yT[b % 2][:, P * j:P * j + P], w_out[:, j], start=(j == 0), stop=(j == 3))
                pe.matmul(bank(BK_M)[:, D:2 * D], ysum[:], ones[:], start=True, stop=True).then_inc(o_pe, 1)

            def f_free(c, use):
                g = half_of(use)
                m = USES[g].index(use)
                if m == 0:
                    return
                what, q = USES[g][m - 1]
                if what == "T":
                    pe.wait_ge(f_T[g], 4 * c + q // 2 + 1)
                elif what == "Q":
                    pe.wait_ge(f_q[g], 4 * c + q % 4 + 1)
                else:
                    pe.wait_ge(f_x[g], x_step("attn" if what == "O" else f"ffn{q // 2}", c))

            def f_turn(c, t):
                g, norm = t % 2, ["xn0", "xn1", "onorm", "xn2"][t // 2]
                f_free(c, ("T", t))
                if f_alone(("T", t), c):
                    if norm == "onorm":
                        for m in (7, 9):
                            pe.wait_ge(f_red, 2 * NB * c + m + 4 * g)
                            keep_warm(WARM_VALUES, BK_T)
                    else:
                        for name in ("stats", "var"):
                            pe.wait_ge(f_v[g], v_step(name + norm[2], c))
                            keep_warm(WARM_LAST, BK_T)
                pe.wait_ge(f_v[g], v_step(norm, c))
                turn(BK_F[g], [xn[:, 4 * g + q, :] for q in range(4)]).then_inc(f_pe[g], 1)

            def f_project(c, use):
                what, g = use[0], use[1] % 2
                alone = f_alone(use, c)
                if not alone:
                    f_free(c, use)
                w = w_of[:, 0 if what == "O" else 1]
                at = BIAS_O if what == "O" else BIAS_F
                pe.matmul(f_bank(use, c), ones3[:], bias3[:, at:at + 4 * D], start=True, stop=False)
                if alone:
                    f_free(c, use)
                for q in range(4):
                    last = pe.matmul(f_bank(use, c)[:, P * q:P * q + P], xnT_f[:, 4 * g + q, :], w, start=False, stop=(q == 3))
                last.then_inc(f_pe[g], 1)

            def f_qkv(c, s):
                if not f_alone(("Q", s), c) or s % 4 == 0:
                    f_free(c, ("Q", s))
                elif s % 4 >= 2:
                    pe.wait_ge(f_q[s // 4], 4 * c + s % 4 - 1)
                dst = f_bank(("Q", s), c)[:, 0:3 * D]
                pe.matmul(dst, ones3[:], bias3[:, 0:3 * D], start=True, stop=False)
                pe.matmul(dst, xnT_f[:, s, :], w_qkv[:], start=False, stop=True).then_inc(f_pe[s // 4], 1)

            pieces = []
            for what, q in USES[0] + USES[1]:
                if what == "T":
                    place(pieces, f"T{q}", lambda c, q=q: f_turn(c, q))
                elif what == "Q":
                    place(pieces, f"qkv{q}", lambda c, q=q: f_qkv(c, q))
                else:
                    place(pieces, f"{what}{q}", lambda c, what=what, q=q: f_project(c, (what, q)))

            def step(c, k, pieces, first=False, last=False):
                nxt = not (last and k == UNITS - 1)
                before = not (first and k == 0)
                pc, pk = (c, k - 1) if k else (c - 1, UNITS - 1)
                if k % 2 == 0:
                    project_b(c, k + 1)
                    turn_b(c, k)
                    at_step(pieces, c, k, 0)
                    if before:
                        outputs(pc, pk, not first)
                    if before and has_state(pc, pk):
                        states(pc, pk)
                    turn_c(c, k)
                    project_c(c, k + 1)
                    at_step(pieces, c, k, 1)
                    scores(c, k)
                    at_step(pieces, c, k, 2)
                else:
                    if nxt:
                        project_u(c, k + 1)
                    turn_b(c, k)
                    if nxt:
                        project_b(c, k + 1)
                        project_c(c, k + 1)
                    if has_state(pc, pk):
                        states(pc, pk)
                    at_step(pieces, c, k, 0)
                    outputs(pc, pk, not first)
                    at_step(pieces, c, k, 1)
                    turn_c(c, k)
                    if not (first and k == 1):
                        project_out(c if k > 1 else c - 1, (k // 2 - 1) % NB, not (last and k >= UNITS - 1))
                    scores(c, k)
                    at_step(pieces, c, k, 2)

            def finish(c):
                outputs(c, UNITS - 1, True)
                project_out(c, NB - 1, False)

            project_b(0, 0)
            project_c(0, 0)
            project_u(0, 0)
            for g in range(5, 8):
                turn_weights(g)
            pe.wait_ge(bias_in, 144)
            pe.wait_ge(pa, PA["W", 7])
            pe.wait_ge(pv, PV["w_out"])
            run_chunks(pe, step, pieces, finish)


_INS = ["L0_attn_a_x", "L0_attn_a_in_proj_w", "L0_attn_a_sel_proj_w", "L0_attn_a_out_proj_w", "L0_attn_a_A_log",
        "L0_attn_a_dt_bias", "L0_attn_a_rms_weight", "L0_attn_b_in_proj_w", "L0_attn_b_in_proj_b",
        "L0_attn_b_out_proj_w", "L0_attn_b_out_proj_b", "L0_ffn_weight", "L0_ffn_alpha", "L0_ffn_bias"]


def kernel(**inputs):
    import concourse.bacc as bacc
    from concourse.bass_utils import run_bass_kernel_spmd

    nc = bacc.Bacc("TRN2", target_bir_lowering=False, num_devices=1)
    arrays, args = {}, []
    for name in _INS:
        a = np.ascontiguousarray(inputs[name])
        arrays[f"in_{name}_dram"] = a
        args.append(nc.dram_tensor(f"in_{name}_dram", a.shape, mybir.dt.from_np(a.dtype), kind="ExternalInput").ap())
    args.append(nc.dram_tensor("out_dram", arrays["in_L0_attn_a_x_dram"].shape, F32, kind="ExternalOutput").ap())
    hybrid_block(nc, *args)
    r = run_bass_kernel_spmd(nc, [arrays], core_ids=[0])
    return r.results[0]["out_dram"]
```
